# Optimizing a Trainium2 kernel written in Bass

```python
import numpy as np
import jax
import jax.numpy as jnp

def _softmax(x, axis=-1):
    return jax.nn.softmax(x, axis=axis)

def _gelu(x):
    return jax.nn.gelu(x, approximate=True)

def _silu(x):
    return jax.nn.silu(x)

def _sigmoid(x):
    return jax.nn.sigmoid(x)

def _layernorm(x, axis=-1, eps=1e-05):
    m = jnp.mean(x, axis=axis, keepdims=True)
    v = jnp.var(x, axis=axis, keepdims=True)
    return (x - m) / jnp.sqrt(v + eps)

def _scatter_add(tgt, idx, src, axis=0):
    return tgt.at[idx].add(src)

def _segment_sum(src, seg, n):
    return jax.ops.segment_sum(src, seg, n)
kernel_name = 'mk_flamingo_gated_d1_seqx_r4_ef687a'

def setup_inputs(seed: int=0):
    np.random.seed(seed)
    _w = jnp.asarray

    def _rec_inputs():
        import jax
        import jax.numpy as jnp
        _rk = jax.random.key(seed)
        x = -0.000125 + 0.9999 * jax.random.normal(jax.random.fold_in(_rk, 1), (4, 512, 256), jnp.float32)
        _lenS = 512 - jax.random.randint(jax.random.fold_in(_rk, 7), (4,), 0, max(1, 512 // 4) + 1, jnp.int32)
        _lenS2 = 512 - jax.random.randint(jax.random.fold_in(_rk, 8), (4,), 0, max(1, 512 // 4) + 1, jnp.int32)
        _ctx_1024P = jax.random.normal(jax.random.fold_in(_rk, 11), (4, 16, 256), jnp.float32)
        _ctx_1024c = jax.random.dirichlet(jax.random.fold_in(_rk, 511), 0.3 * jnp.ones((16,), jnp.float32), (4, 512))
        _ctx_1024t = jnp.einsum('bsk,bkd->bsd', _ctx_1024c, _ctx_1024P)
        _ctx_1024t = _ctx_1024t * jax.lax.rsqrt(jnp.mean(jnp.square(_ctx_1024t)) + 1e-12) * 0.953939
        ctx_1024 = -1.52775e-05 + 0.999936 * (_ctx_1024t + 0.3 * jax.random.normal(jax.random.fold_in(_rk, 611), (4, 512, 256), jnp.float32))
        _g = jax.random.normal(jax.random.fold_in(_rk, 9001), (2, 1), jnp.float32)
        _g = jnp.sign(_g) * jnp.maximum(jnp.abs(_g), 1.0) + (_g == 0) * 1.0
        g_xattn = _g[0]
        g_ffn = _g[1]
        return (x, ctx_1024, g_xattn, g_ffn)
    x, ctx_1024, g_xattn, g_ffn = _rec_inputs()

    def _L0_xattn_setup():
        import math
        import jax, jax.numpy as jnp
        import numpy as np
        key = jax.random.key(seed)
        ks = jax.random.split(key, 11)
        B, L, D = (16, 512, 256)
        s = 0.02
        return {'queries': jax.random.normal(ks[0], (B, L, D), jnp.float32), 'keys': jax.random.normal(ks[1], (B, L, D), jnp.float32), 'values': jax.random.normal(ks[2], (B, L, D), jnp.float32), 'Wq': jax.random.normal(ks[3], (D, D), jnp.float32) * s, 'bq': jax.random.normal(ks[4], (D,), jnp.float32) * s, 'Wk': jax.random.normal(ks[5], (D, D), jnp.float32) * s, 'bk': jax.random.normal(ks[6], (D,), jnp.float32) * s, 'Wv': jax.random.normal(ks[7], (D, D), jnp.float32) * s, 'bv': jax.random.normal(ks[8], (D,), jnp.float32) * s, 'Wo': jax.random.normal(ks[9], (D, D), jnp.float32) * s, 'bo': jax.random.normal(ks[10], (D,), jnp.float32) * s, 'n_heads': 8}
    _L0_xattn_all = _L0_xattn_setup()
    _L0_xattn_in = {k: v for k, v in _L0_xattn_all.items() if k in ('Wq', 'bq', 'Wk', 'bk', 'Wv', 'bv', 'Wo', 'bo')}
    del _L0_xattn_all

    def _L0_ffn_setup():
        import jax, jax.numpy as jnp
        import numpy as np
        D = 256
        F = 4 * D
        E = 8
        NS = 2
        TOP_K = 2
        B, S = (2, 256)
        key = jax.random.key(seed)
        ks = jax.random.split(key, 7)
        w = 1.0 / np.sqrt(D)
        wf = 1.0 / np.sqrt(F)
        return {'x': jax.random.normal(ks[0], (B, S, D), jnp.float32), 'centroids': jax.random.normal(ks[1], (E, D), jnp.float32) * w, 'routing_bias': jnp.zeros((E,), jnp.float32), 'Wfc_r': jax.random.normal(ks[2], (E, F, D), jnp.float32) * w, 'Wproj_r': jax.random.normal(ks[3], (E, D, F), jnp.float32) * wf, 'Wfc_sh': jax.random.normal(ks[4], (NS, F, D), jnp.float32) * w, 'Wproj_sh': jax.random.normal(ks[5], (NS, D, F), jnp.float32) * wf}
    _L0_ffn_all = _L0_ffn_setup()
    _L0_ffn_in = {k: v for k, v in _L0_ffn_all.items() if k in ('centroids', 'routing_bias', 'Wfc_r', 'Wproj_r', 'Wfc_sh', 'Wproj_sh')}
    del _L0_ffn_all
    return {'x': x, 'ctx_1024': ctx_1024, 'g_xattn': g_xattn, 'g_ffn': g_ffn, 'L0_xattn_Wq': _L0_xattn_in['Wq'], 'L0_xattn_bq': _L0_xattn_in['bq'], 'L0_xattn_Wk': _L0_xattn_in['Wk'], 'L0_xattn_bk': _L0_xattn_in['bk'], 'L0_xattn_Wv': _L0_xattn_in['Wv'], 'L0_xattn_bv': _L0_xattn_in['bv'], 'L0_xattn_Wo': _L0_xattn_in['Wo'], 'L0_xattn_bo': _L0_xattn_in['bo'], 'L0_ffn_centroids': _L0_ffn_in['centroids'], 'L0_ffn_routing_bias': _L0_ffn_in['routing_bias'], 'L0_ffn_Wfc_r': _L0_ffn_in['Wfc_r'], 'L0_ffn_Wproj_r': _L0_ffn_in['Wproj_r'], 'L0_ffn_Wfc_sh': _L0_ffn_in['Wfc_sh'], 'L0_ffn_Wproj_sh': _L0_ffn_in['Wproj_sh']}

def reference(x, ctx_1024, g_xattn, g_ffn, L0_xattn_Wq, L0_xattn_bq, L0_xattn_Wk, L0_xattn_bk, L0_xattn_Wv, L0_xattn_bv, L0_xattn_Wo, L0_xattn_bo, L0_ffn_centroids, L0_ffn_routing_bias, L0_ffn_Wfc_r, L0_ffn_Wproj_r, L0_ffn_Wfc_sh, L0_ffn_Wproj_sh):
    import jax
    import jax.numpy as jnp

    def _L0_xattn_ref(queries, keys, values, Wq, bq, Wk, bk, Wv, bv, Wo, bo, n_heads):
        import math
        import jax, jax.numpy as jnp
        import numpy as np
        B, L, D = queries.shape
        H = n_heads
        E = D // H
        q = (queries @ Wq.T + bq).reshape(B, L, H, E).transpose(0, 2, 3, 1)
        k = (keys @ Wk.T + bk).reshape(B, L, H, E).transpose(0, 2, 3, 1)
        v = (values @ Wv.T + bv).reshape(B, L, H, E).transpose(0, 2, 3, 1)
        q_fft = jnp.fft.rfft(q, axis=-1)
        k_fft = jnp.fft.rfft(k, axis=-1)
        corr = jnp.fft.irfft(q_fft * jnp.conj(k_fft), n=L, axis=-1)
        top_k = int(1 * math.log(L))
        mean_value = corr.mean(axis=(1, 2))
        _, index = jax.lax.top_k(mean_value.mean(axis=0), top_k)
        weights = mean_value[:, index]
        tmp_corr = jax.nn.softmax(weights, axis=-1)
        pos = jnp.arange(L)
        agg = jnp.zeros_like(v)
        for i in range(top_k):
            rolled = jnp.take(v, (pos + index[i]) % L, axis=-1)
            agg = agg + rolled * tmp_corr[:, i][:, None, None, None]
        out = agg.transpose(0, 3, 1, 2).reshape(B, L, D)
        return out @ Wo.T + bo

    def _L0_ffn_ref(x, centroids, routing_bias, Wfc_r, Wproj_r, Wfc_sh, Wproj_sh):
        import jax, jax.numpy as jnp
        import numpy as np
        D = 256
        F = 4 * D
        E = 8
        NS = 2
        TOP_K = 2
        B, S = (2, 256)
        raw = jnp.einsum('bsd,ed->bse', x, centroids)
        routing_scores = jax.nn.sigmoid(raw)
        balanced = jax.nn.sigmoid(raw + routing_bias)
        _, top_idx = jax.lax.top_k(balanced, TOP_K)
        gathered = jnp.take_along_axis(routing_scores, top_idx, axis=-1)
        top_w = jax.nn.softmax(gathered, axis=-1)
        combine = jnp.sum(jax.nn.one_hot(top_idx, E, dtype=x.dtype) * top_w[..., None], axis=-2)
        h_sh = jax.nn.gelu(jnp.einsum('bsd,nfd->bsnf', x, Wfc_sh), approximate=False)
        shared_out = jnp.einsum('bsnf,ndf->bsd', h_sh, Wproj_sh)
        h_r = jax.nn.gelu(jnp.einsum('bsd,efd->bsef', x, Wfc_r), approximate=False)
        expert_out = jnp.einsum('bsef,edf->bsed', h_r, Wproj_r)
        routed_out = jnp.einsum('bsed,bse->bsd', expert_out, combine)
        return x + shared_out + routed_out
    x = x + jnp.tanh(g_xattn[0]) * _L0_xattn_ref(_layernorm(x, axis=-1), ctx_1024, ctx_1024, L0_xattn_Wq, L0_xattn_bq, L0_xattn_Wk, L0_xattn_bk, L0_xattn_Wv, L0_xattn_bv, L0_xattn_Wo, L0_xattn_bo, 8)
    x = x + jnp.tanh(g_ffn[0]) * _L0_ffn_ref(_layernorm(x, axis=-1), L0_ffn_centroids, L0_ffn_routing_bias, L0_ffn_Wfc_r, L0_ffn_Wproj_r, L0_ffn_Wfc_sh, L0_ffn_Wproj_sh)
    return x

_drawn_inputs = setup_inputs


def setup_inputs(seed=0):
    import zlib

    import numpy as np

    out = dict(_drawn_inputs(seed))
    spreads = {'L0_ffn_routing_bias': (0.0, 0.1)}
    factors = {}
    for name, (base, spread) in spreads.items():
        noise = np.random.default_rng([zlib.crc32(name.encode()), seed]).standard_normal(out[name].shape)
        drawn = base * np.exp(spread * noise) if base else spread * noise
        out[name] = jnp.asarray(drawn.astype(out[name].dtype))
    for name, factor in factors.items():
        out[name] = (out[name] * factor).astype(out[name].dtype)
    return out
```

```python
from contextlib import ExitStack

import concourse.bass as bass
from concourse import mybir

F32 = mybir.dt.float32
F16 = mybir.dt.float16
I32 = mybir.dt.int32
U32 = mybir.dt.uint32
ALU = mybir.AluOpType
ACT = mybir.ActivationFunctionType
AX = mybir.AxisListType.X

P = 128
B, L, D = 4, 512, 256
T = B * L
NT = T // P
TB = L // P
KD = D // P
NE, NS, F = 8, 2, 1024
KF = F // P
LAGS = 6
SKEW = L + P
TILES = (2 * T - NE) // P + NE
SLOTS = TILES * P
ETAB = TILES + 1
UNIT = 512
PIECE = 1024
NPIECE = 2 * KD * F // PIECE
WID = 2 * KD * F
SC = 16.0
EPS = 1e-5
BIG = 3.0e38
RH, RF = 4, 2
RR = 3
CR = 4
NWARM = NE + NS


def build_kernel(nc, A):
    with ExitStack() as ctx:
        def sb(name, shape, dt=F32):
            return ctx.enter_context(nc.sbuf_tensor(name, shape, dt))

        def sem(name):
            return ctx.enter_context(nc.semaphore(name))

        wr = sb("wr", [P, NE, 2, WID], F16)
        ws = sb("ws", [P, 2, WID], F16)
        xres = sb("xres", [P, NT, D])
        xt = sb("xt", [P, 2, KD, T], F16)
        stage = sb("stage", [P, 2, PIECE])
        hf = sb("hf", [P, RF, UNIT])
        hs = sb("hs", [P, RH, 2, UNIT], F16)
        rt = sb("rt", [P, 9 * 512], F16)
        tri = sb("tri", [P, P])
        identh = sb("identh", [P, P], F16)
        stats = sb("stats", [P, NT, 6])
        mv = sb("mv", [P, NT, 2])
        rstd = sb("rstd", [P, NT, 4])
        gates = sb("gates", [P, 8])
        cent = sb("cent", [P, 2, KD, NE], F16)
        rbias = sb("rbias", [P, NE])
        slots = sb("slots", [P, NT, 2], U32)
        wt = sb("wt", [P, NT, 4])
        etab = sb("etab", [1, ETAB], I32)

        def region(e):
            return wr[:, e, :, :].rearrange("p a b -> p (a b)").bitcast(F32)

        ctxt = region(0).rearrange("p (k t) -> p k t", k=KD)
        xnt = region(1).rearrange("p (k t) -> p k t", k=KD)
        zt = region(2).rearrange("p (k t) -> p k t", k=KD)
        u = region(3).rearrange("p (n d) -> p n d", n=NT)
        xn = region(4).rearrange("p (n d) -> p n d", n=NT)
        r5, r6 = region(5), region(6)
        gband = r5[:, 0:B * SKEW].rearrange("p (b j) -> p b j", b=B)
        wkq = r5[:, B * SKEW:B * SKEW + KD * D].rearrange("p (k d) -> p k d", k=KD)
        wvo = r5[:, B * SKEW + KD * D:B * SKEW + 2 * KD * D].rearrange("p (k d) -> p k d", k=KD)
        small5 = B * SKEW + 2 * KD * D
        csum = r5[:, small5:small5 + KD * B].rearrange("p (k b) -> p k b", k=KD)
        bvb = r5[:, small5 + 8:small5 + 8 + KD * P].rearrange("p (k m) -> p k m", k=KD)
        craw = r6[:, 0:B * L].rearrange("p (b j) -> p b j", b=B)
        circ = r5[:, 0:B * L].rearrange("p (b j) -> p b j", b=B)
        o6 = B * L
        ubias = r6[:, o6:o6 + D]
        bob = r6[:, o6 + D:o6 + 2 * D]
        identf = r6[:, o6 + 2 * D:o6 + 2 * D + P]
        sel = r6[:, o6 + 2 * D + P:o6 + 2 * D + P + B * 36].rearrange("p (b m) -> p b m", b=B)
        o7 = o6 + 2 * D + P + B * 36
        vecs = r6[:, o7:o7 + 32]
        bkT, bqT, bvT = vecs[:, 0:2], vecs[:, 2:4], vecs[:, 4:6]
        zbias, v1 = vecs[:, 6:8], vecs[:, 8:10]
        bk4 = vecs[:, 10:18].rearrange("p (k b) -> p k b", k=KD)
        centf = r6[:, o7 + 32:o7 + 32 + KD * NE].rearrange("p (k e) -> p k e", k=KD)
        gsk = r6[:, 0:B * L].rearrange("p (b j) -> p b j", b=B)
        xh = wr[:, NE - 1, :, :].rearrange("p a b -> p (a b)").rearrange("p (n s d) -> p n s d", n=NT, s=2)
        xtf = xt[:, :, :, :].rearrange("p a k t -> p (a k t)").bitcast(F32)
        wsrc = xtf[:, 0:4 * KD * D].rearrange("p (w k d) -> p w k d", w=4, k=KD)
        wq, wk, wv, wo = (wsrc[:, i] for i in range(4))
        rows = xtf[0:B, 4 * KD * D:4 * KD * D + 2048].rearrange("p (a j) -> p a j", j=512)
        tot, rep, pen, cm = (rows[:, i] for i in range(4))
        crow = hf[0:B, :, :].rearrange("p a b -> p (a b)")[:, 0:SKEW]
        sml = gates[0:B, 4:8]
        top8 = rstd[0:B, 0:2, :].rearrange("p a b -> p (a b)")

        rtf = rt[:, :].bitcast(F32)
        dsp = rtf[:, 0:14 * P].rearrange("p (a n e) -> p a n e", a=14, e=NE)
        bal, sco, key, oh1, oh2, both, pos, trine, tmp, _, ramp = (dsp[:, i] for i in range(11))
        totb = rtf[:, 11 * P:12 * P]
        ones = rtf[:, 12 * P:13 * P]
        m13 = rtf[:, 13 * P:14 * P]
        lag_ramp = rtf[:, 14 * P:15 * P].rearrange("p (e t) -> p e t", e=NE)
        selE = m13[:, 0:8]
        cnt = m13[:, 8:16]
        ntile = m13[:, 16:24]
        first = m13[:, 24:32]
        totc = m13[:, 32:33]
        m1 = m13[:, 48:64]
        k1 = m13[:, 64:80]
        s1v = m13[:, 80:96]
        s2v = m13[:, 96:112]
        dv = m13[:, 112:128]
        zero = rt[:, 0:1024]
        upper = rtf[:, 15 * P:15 * P + 64].rearrange("p (e f) -> p e f", e=NE)
        up2 = rtf[:, 15 * P + 64:16 * P].rearrange("p (e f) -> p e f", e=NE)
        jramp = rtf[0:1, 16 * P:16 * P + ETAB * 1]
        jcmp = rtf[0:1, 0:ETAB * NE].rearrange("p (j e) -> p j e", e=NE)
        ej = rtf[0:1, 17 * P:17 * P + ETAB]
        xs = rt[:, 0:RR * 512].rearrange("p (r c) -> p r c", r=RR)
        xst = rt[:, RR * 512:2 * RR * 512].rearrange("p (r a k c) -> p r a k c", r=RR, a=2, k=KD)
        ysb = rtf[:, RR * 512:RR * 512 + RR * D].rearrange("p (r d) -> p r d", r=RR)
        gat = rtf[:, 0:8 * D].rearrange("p (r d) -> p r d", r=8)

        ps = ctx.enter_context(nc.psum_tensor("ps", [P, 8, 512], F32))

        band_d = nc.dram_tensor("band_d", [P, B, SKEW], F32).ap()
        crow_d = nc.dram_tensor("crow_d", [B, SKEW], F32).ap()
        xslot_d = nc.dram_tensor("xslot_d", [SLOTS, 2 * D], F16).ap()
        yslot_d = nc.dram_tensor("yslot_d", [SLOTS, D], F32).ap()

        names = ("x_in0 x_in1 x_in2 x_in3 w_in ctx_in small_in const_ready prod_done vec_done ubias_done prod_taken "
                 "z_done z_taken xn_ready xnt_done xnt_taken band_done band_taken u_done u_taken csum_done "
                 "band_out skew_in gsum_done sbias_done chain crow_ready crow_out circ_in circ_ready mix_done x2_ready "
                 "sq_req sq_done exp_req exp_done hi_done gate_done norm_ready high_ready split_ready xt_done xt_taken raw_done sig_req "
                 "sig_done disp_req disp_done slots_ready table_ready zero_set zero_out scatter_out "
                 "piece_in0 piece_in1 piece_high piece_low "
                 "h_done g_ready hs_ready p_done cent_split "
                 "xs_in0 xs_in1 xs_in2 t_done t_taken yr_taken ys_out0 ys_out1 ys_out2 "
                 "gather_in0 gather_in1 gather_in2 gather_in3 gather_in4 gather_in5 gather_in6 gather_in7 "
                 "out_done xb_ready acc_done")
        S = {n: sem(n) for n in names.split()}
        s = type("Sems", (), S)

        block = ctx.enter_context(nc.Block())

        def wtile(w, part, k, f0, n):
            return w[:, part, k * F + f0:k * F + f0 + n]

        def vtile(w, part, f):
            return w[:, part, KD * F + f * D:KD * F + (f + 1) * D]

        SH_UNITS = B * KF
        RT_UNITS = 2 * TILES
        base = [0, SH_UNITS, SH_UNITS + RT_UNITS]
        BODY = 2 * KF
        ACC0 = CR + 1
        ACC2 = ACC0 + 4 * (B // 2)
        STEP2 = BODY + 4

        def pos_of(n):
            return n if n < KF + 2 else n + 2

        @block.sync
        def _(sp):
            xin = [s.x_in0, s.x_in1, s.x_in2, s.x_in3]
            xr = A["x"].rearrange("(n p) d -> p n d", p=P)
            sp.dma_start(xres[:, 0:TB, :], xr[:, 0:TB, :]).then_inc(s.x_in0, 16)
            for i, nm in enumerate(("Wk", "Wq", "Wv", "WoT")):
                j = (1, 0, 2, 3)[i]
                sp.dma_start(wsrc[:, j], A[nm].rearrange("(k p) d -> p k d", p=P)).then_inc(s.w_in, 16)
            for nm, dst in (("bk", bkT), ("bq", bqT), ("bv", bvT)):
                with nc.allow_non_contiguous_dma(reason="a bias as a column"):
                    sp.dma_start(dst, A[nm].rearrange("(k p) -> p k", p=P)).then_inc(s.w_in, 16)
            sp.dma_start(ctxt, A["ctxT"].rearrange("(k p) t -> p k t", p=P)).then_inc(s.ctx_in, 16)
            for b in range(1, B):
                sp.dma_start(xres[:, b * TB:(b + 1) * TB, :], xr[:, b * TB:(b + 1) * TB, :]).then_inc(xin[b], 16)
            sp.dma_start(bob, A["bo"].rearrange("(a d) -> a d", a=1).to_broadcast([P, D])).then_inc(s.small_in, 16)
            sp.dma_start(gates[:, 0:1], A["gx"].rearrange("(a d) -> a d", a=1).to_broadcast([P, 1])).then_inc(s.small_in, 16)
            sp.dma_start(gates[:, 1:2], A["gf"].rearrange("(a d) -> a d", a=1).to_broadcast([P, 1])).then_inc(s.small_in, 16)
            sp.dma_start(rbias[:, :], A["rb"].rearrange("(a d) -> a d", a=1).to_broadcast([P, NE])).then_inc(s.small_in, 16)
            with nc.allow_non_contiguous_dma(reason="centroids in columns"):
                sp.dma_start(centf, A["centT"].rearrange("(k p) e -> p k e", p=P)).then_inc(s.small_in, 16)
            sp.wait_ge(s.zero_set, 1)
            zsrc = bass.AP(zero.tensor, zero.offset, [zero.ap[0], [0, TILES], [1, 2 * D]])
            sp.dma_start(xslot_d.rearrange("(t p) c -> p t c", p=P), zsrc).then_inc(s.zero_out, 16)
            def piece(p):
                if p >= 2:
                    sp.wait_ge(s.piece_low, p - 1)
                sp.dma_start(stage[:, p % 2, :], A["W"][p]).then_inc([s.piece_in0, s.piece_in1][p % 2], 16)

            piece(0)
            piece(1)
            for b in range(B):
                sp.wait_ge(s.band_taken, 2 * (b + 1))
                sp.dma_start(band_d[:, b, :], gband[:, b, :]).then_inc(s.band_out, 16)
            sp.wait_ge(s.band_out, 16 * B)
            skew = bass.AP(band_d.tensor, band_d.offset, [[B * SKEW + 1, P], [SKEW, B], [1, L]])
            sp.dma_start(gsk, skew).then_inc(s.skew_in, 16)
            sp.wait_ge(s.crow_ready, 2)
            sp.dma_start(crow_d[:, 0:SKEW - 1], crow[:, 0:SKEW - 1]).then_inc(s.crow_out, 16)
            sp.wait_ge(s.crow_out, 16)
            cskew = bass.AP(crow_d.tensor, crow_d.offset, [[1, P], [SKEW, B], [1, L]])
            sp.dma_start(craw, cskew).then_inc(s.circ_in, 16)
            piece(2)
            piece(3)
            with sp.Fori(0, NE * NPIECE // 2) as i:
                for q in range(2):
                    sp.wait_ge(s.piece_low, NPIECE - 1 + q + i * 2)
                    e = i * 2 + (NPIECE + q)
                    sp.dma_start(stage[:, q, :], A["W"][bass.ds(e, 1)].rearrange("a p c -> (a p) c")).then_inc(
                        [s.piece_in0, s.piece_in1][q], 16)
            piece((NE + 1) * NPIECE)
            piece((NE + 1) * NPIECE + 1)
            sp.wait_ge(s.scatter_out, 16 * 2 * NT)
            sp.wait_ge(s.table_ready, 1)
            xsin = [s.xs_in0, s.xs_in1, s.xs_in2]
            ysout = [s.ys_out0, s.ys_out1, s.ys_out2]
            for j in range(RR):
                sp.dma_start(xs[:, j], xslot_d[j * P:(j + 1) * P, :]).then_inc(xsin[j], 16)
            piece((NE + 1) * NPIECE + 2)
            piece((NE + 1) * NPIECE + 3)

            def store(j, q):
                sp.wait_ge(s.yr_taken, j + q + 1 + CR)
                sp.dma_start(yslot_d[bass.ds((j + q) * P, P), :], ysb[:, q]).then_inc(ysout[q], 16)
            with sp.Fori(0, TILES // RR - 1) as i:
                for q in range(RR):
                    sp.wait_ge(s.t_done, i * RR + q + 1)
                    sp.dma_start(xs[:, q], xslot_d[bass.ds(i * (RR * P) + (RR + q) * P, P), :]).then_inc(xsin[q], 16)
                    store(i * RR, q)
            for q in range(RR):
                store(TILES - RR, q)
            for b in range(B):
                sp.wait_ge(s.acc_done, ACC2 + (b // 2) * STEP2 + (12 if b % 2 == 0 else STEP2))
                o = A["out"].rearrange("(n p) d -> p n d", p=P)
                sp.dma_start(o[:, b * TB:(b + 1) * TB, :], xres[:, b * TB:(b + 1) * TB, :]).then_inc(s.out_done, 16)
            sp.wait_ge(s.out_done, 16 * B)

        @block.gpsimd
        def _(pool):
            pool.memset(zero, 0.0).then_inc(s.zero_set, 1)
            pool.memset(identf, 0.0)
            pool.memset(tri[:, :], 1.0)
            pool.memset(sel, 0.0).then_inc(s.const_ready, 1)
            pool.wait_ge(s.const_ready, 1)
            for b in range(B):
                pool.memset(sel[:, b, b:b + 1], 1.0)
            pool.memset(sel[:, :, 32:36], 1.0)
            pool.affine_select(out=identf, in_=identf, compare_op=ALU.not_equal, fill=1.0, base=0,
                               pattern=[[-1, P]], channel_multiplier=1).then_inc(s.const_ready, 1)
            pool.affine_select(out=tri[:, :], in_=tri[:, :], compare_op=ALU.is_gt, fill=0.0, base=0,
                               pattern=[[1, P]], channel_multiplier=-1).then_inc(s.const_ready, 1)
            pool.wait_ge(s.const_ready, 3)
            pool.tensor_copy(identh[:, :], identf).then_inc(s.const_ready, 1)
            pool.wait_ge(s.zero_out, 16)
            pool.iota(lag_ramp, [[0, NE], [P, NT]], base=0, channel_multiplier=0, allow_small_or_imprecise_dtypes=True)
            pool.iota(jramp, [[1, ETAB]], base=0, channel_multiplier=0, allow_small_or_imprecise_dtypes=True)
            pool.iota(ramp, [[0, NT], [-1, NE]], base=NE, channel_multiplier=0, allow_small_or_imprecise_dtypes=True)
            pool.iota(upper, [[1, NE], [-1, NE]], base=0, channel_multiplier=0, allow_small_or_imprecise_dtypes=True)
            pool.memset(ones, 1.0).then_inc(s.const_ready, 1)
            pool.wait_ge(s.slots_ready, 2)
            pool.wait_ge(s.split_ready, NT)
            pool.wait_ge(s.high_ready, NT)
            for n in range(NT):
                for k in range(2):
                    pool.indirect_dma_start(xslot_d, bass.IndirectOffsetOnAxis(slots[:, n, k:k + 1], 0),
                                            xh[:, n].rearrange("p s d -> p (s d)"), None).then_inc(s.scatter_out, 16)
            for q, so in enumerate((s.ys_out0, s.ys_out1, s.ys_out2)):
                pool.wait_ge(so, 16 * (TILES // RR + 1))
            gin = [s.gather_in0, s.gather_in1, s.gather_in2, s.gather_in3,
                   s.gather_in4, s.gather_in5, s.gather_in6, s.gather_in7]
            for n in range(NT):
                for k in range(2):
                    m = 2 * n + k
                    if m >= 8:
                        pool.wait_ge(s.acc_done, ACC2 + (m - 8) // BODY * STEP2 + pos_of((m - 8) % BODY) + 1)
                    pool.indirect_dma_start(gat[:, m % 8], None, yslot_d,
                                            bass.IndirectOffsetOnAxis(slots[:, n, k:k + 1], 0)).then_inc(gin[m % 8], 16)

        @block.tensor
        def _(pe):
            mm = pe.matmul
            pe.wait_ge(s.w_in, 16 * 7)
            for c in range(KD):
                for o in range(KD):
                    mm(ps[:, 0, c * D:(c + 1) * D], wk[:, o, c * P:(c + 1) * P], wq[:, o, :], start=(o == 0), stop=(o == KD - 1))
            for c in range(KD):
                for o in range(KD):
                    last = mm(ps[:, 1, c * D:(c + 1) * D], wv[:, o, c * P:(c + 1) * P], wo[:, o, :], start=(o == 0), stop=(o == KD - 1))
            last.then_inc(s.prod_done, 1)
            for c in range(KD):
                for o in range(KD):
                    mm(ps[:, 2, c:c + 1], wq[:, o, c * P:(c + 1) * P], bkT[:, o:o + 1], start=(o == 0), stop=(o == KD - 1))
            for c in range(KD):
                for o in range(KD):
                    last = mm(ps[:, 2, 2 + c:3 + c], wk[:, o, c * P:(c + 1) * P], bqT[:, o:o + 1], start=(o == 0), stop=(o == KD - 1))
            last.then_inc(s.vec_done, 1)
            pe.wait_ge(s.chain, 2)
            for o in range(KD):
                last = mm(ps[:, 3, 0:D], bvb[:, o, :], wo[:, o, :], start=(o == 0), stop=(o == KD - 1))
            last.then_inc(s.ubias_done, 1)
            pe.wait_ge(s.ctx_in, 16)
            pe.wait_ge(s.prod_taken, 2)
            def zjob(q):
                b, j = q // 2, q % 2
                if q >= 4:
                    pe.wait_ge(s.z_taken, q - 3)
                for c in range(KD):
                    last = mm(ps[:, 4 + q % 4, :], wkq[:, c, j * P:(j + 1) * P], ctxt[:, c, b * L:(b + 1) * L], start=(c == 0), stop=(c == KD - 1))
                last.then_inc(s.z_done, 1)
            pe.wait_ge(s.const_ready, 2)

            def xntjob(q):
                b, k = q // 2, q % 2
                pe.wait_ge(s.xn_ready, (b + 1) * TB)
                if q < 4:
                    pe.wait_ge(s.prod_taken, 4)
                else:
                    pe.wait_ge(s.xnt_taken, q - 3)
                for n in range(TB):
                    last = pe.transpose(ps[:, q % 4, n * P:(n + 1) * P], xn[:, b * TB + n, k * P:(k + 1) * P], identf)
                last.then_inc(s.xnt_done, 1)

            for b in range(B):
                zjob(2 * b)
                zjob(2 * b + 1)
                xntjob(2 * b)
                xntjob(2 * b + 1)
            pe.wait_ge(s.z_taken, 2 * B)
            pe.wait_ge(s.xnt_taken, 2 * B)
            for b in range(B):
                for m in range(TB):
                    for c in range(KD):
                        z = zt[:, c, b * L + m * P:b * L + (m + 1) * P]
                        o, w = m * P, L - m * P
                        last = mm(ps[:, b, 0:w], z, xnt[:, c, b * L + o:(b + 1) * L],
                                  start=(m == 0 and c == 0), stop=False, skip_group_check=True)
                        if m:
                            last = mm(ps[:, b, w:L], z, xnt[:, c, b * L:b * L + o], start=False,
                                      stop=(m == TB - 1 and c == KD - 1), skip_group_check=True)
                last.then_inc(s.band_done, 1)
            for q in range(NT // 2):
                if q < 4:
                    pe.wait_ge(s.z_taken, 5 + q)
                else:
                    pe.wait_ge(s.u_taken, q - 3)
                for h in range(2):
                    for c in range(KD):
                        n = 2 * q + h
                        last = mm(ps[:, 4 + q % 4, h * D:(h + 1) * D], ctxt[:, c, n * P:(n + 1) * P], wvo[:, c, :],
                                  start=(c == 0), stop=(c == KD - 1))
                last.then_inc(s.u_done, 1)
            pe.wait_ge(s.csum_done, 2)
            pe.wait_ge(s.band_taken, 4)
            for c in range(KD):
                mm(ps[0:B, 1, 0:1], csum[:, c, :], v1[:, c:c + 1], start=(c == 0), stop=False)
            for o in range(KD):
                last = mm(ps[0:B, 1, 0:1], bk4[:, o, :], bqT[:, o:o + 1], start=False, stop=(o == KD - 1))
            last.then_inc(s.sbias_done, 1)
            pe.wait_ge(s.skew_in, 16)
            for b in range(B):
                last = mm(ps[0:36, 0, :], sel[:, b, :], gsk[:, b, :], start=(b == 0), stop=(b == B - 1))
            last.then_inc(s.gsum_done, 1)
            def mixjob(n):
                b, t = n // TB, n % TB
                pe.wait_ge(s.circ_ready, b + 1)
                if n % 2 == 0:
                    q = n // 2
                    if q < 4:
                        pe.wait_ge(s.u_taken, NT // 2)
                    else:
                        pe.wait_ge(s.x2_ready, 2 * (q - 3))
                for m in range(TB):
                    d = (m - t) % TB
                    last = mm(ps[:, 4 + n // 2 % 4, n % 2 * D:(n % 2 + 1) * D], circ[:, b, (TB - 1 - d) * P:(TB - d) * P],
                              u[:, b * TB + m, :], start=(m == 0), stop=(m == TB - 1))
                last.then_inc(s.mix_done, 1)
            pe.wait_ge(s.const_ready, 4)

            def xtjob(n):
                pe.wait_ge(s.split_ready, n + 1)
                pe.wait_ge(s.high_ready, n + 1)
                if n < 4:
                    pe.wait_ge(s.crow_ready, 2)
                else:
                    pe.wait_ge(s.xt_taken, n - 3)
                tb = ps[:, n % 4, :].bitcast(F16)
                for a in range(2):
                    for k in range(KD):
                        last = pe.transpose(tb[:, (a * KD + k) * P:(a * KD + k + 1) * P], xh[:, n, a, k * P:(k + 1) * P], identh[:, :])
                last.then_inc(s.xt_done, 1)
            for b in range(B + 1):
                for t in range(TB):
                    if b < B:
                        mixjob(b * TB + t)
                for t in range(TB):
                    if b:
                        xtjob((b - 1) * TB + t)
            pe.wait_ge(s.xt_taken, NT)
            pe.wait_ge(s.cent_split, 2)
            pe.wait_ge(s.x2_ready, NT)
            for n in range(NT):
                i = 0
                for k in range(KD):
                    for a, c in ((0, 0), (0, 1), (1, 0)):
                        last = mm(ps[:, 4, n * NE:(n + 1) * NE], xt[:, a, k, n * P:(n + 1) * P], cent[:, c, k, :],
                                  start=(i == 0), stop=(i == 5))
                        i += 1
            last.then_inc(s.raw_done, 1)
            pe.wait_ge(s.disp_req, 1)
            mm(ps[:, 5, 0:1], both.rearrange("p n e -> p (n e)"), ones[:, 0:1], start=True, stop=True).then_inc(s.disp_done, 1)
            pe.wait_ge(s.disp_req, 2)
            mm(ps[:, 6, 0:P], tri[:, :], both.rearrange("p n e -> p (n e)"), start=True, stop=False)
            mm(ps[:, 6, 0:P], totb, trine.rearrange("p n e -> p (n e)"), start=False, stop=True).then_inc(s.disp_done, 1)
            mm(ps[:, 7, 0:NE], totb, selE, start=True, stop=True).then_inc(s.disp_done, 1)

            def shared(ph):
                def up(i, n):
                    pe.wait_ge(s.g_ready, CR + base[ph] + n + 1 - RH + i * BODY)
                    f, blk = n % KF, n // KF
                    j = 0
                    for k in range(KD):
                        for a, c in ((0, 0), (0, 1), (1, 0)):
                            rhs = xt[:, c, k, bass.ds(i * (2 * L) + blk * L, L)]
                            last = mm(ps[:, n % RH, :], wtile(ws, a, k, f * P, P), rhs, start=(j == 0), stop=(j == 5))
                            j += 1
                    last.then_inc(s.h_done, 1)

                def down(i, n):
                    pe.wait_ge(s.hs_ready, CR + base[ph] + n + 1 + i * BODY)
                    f, blk = n % KF, n // KF
                    if f == 0:
                        if ph == 0:
                            pe.wait_ge(s.acc_done, ACC0 - 4 + 2 * (blk + 1) + i * 4)
                        else:
                            pe.wait_ge(s.acc_done, ACC2 - STEP2 + (12 if blk == 0 else STEP2) + i * STEP2)
                    for t in range(TB):
                        for j, (a, c) in enumerate(((0, 0), (0, 1), (1, 0))):
                            out = ps[:, RH + 2 * blk + t // 2, (t % 2) * D:(t % 2 + 1) * D]
                            last = mm(out, hs[:, n % RH, a, t * P:(t + 1) * P], vtile(ws, c, f),
                                      start=(f == 0 and j == 0 and t % 2 == 0), stop=(f == KF - 1 and j == 2),
                                      skip_group_check=True)
                    last.then_inc(s.p_done, 1)

                with pe.Fori(0, B // 2) as i:
                    up(i, 0)
                    up(i, 1)
                    for n in range(BODY):
                        if n + 2 < BODY:
                            up(i, n + 2)
                        down(i, n)

            pe.wait_ge(s.disp_req, 3)
            pe.wait_ge(s.piece_low, NPIECE)
            pe.wait_ge(s.piece_high, NPIECE)
            shared(0)

            xsin = [s.xs_in0, s.xs_in1, s.xs_in2]
            TBANK, YBANK = 3, 4

            def turn(i, q, j):
                pe.wait_ge(xsin[q], 16 * (j // RR + 1) + i * 16)
                pe.wait_ge(s.t_taken, i * RR + j + CR)
                tb = ps[:, TBANK, :].bitcast(F16)
                for a in range(2):
                    for k in range(KD):
                        last = pe.transpose(tb[:, (a * KD + k) * P:(a * KD + k + 1) * P], xs[:, q, a * D + k * P:a * D + (k + 1) * P], identh[:, :])
                last.then_inc(s.t_done, 1)

            def expert(i, j):
                return pe.value_load(etab[0:1, bass.ds(i * RR + j, 1)], min_val=0, max_val=NE - 1)

            def rup(i, q, j, h, e):
                n = 2 * j + h
                if h == 0:
                    pe.wait_ge(s.t_taken, i * RR + j + 1 + CR)
                pe.wait_ge(s.g_ready, CR + base[1] + n + 1 - RR + i * (2 * RR))
                w = wr[:, bass.ds(e, 1), :, :].rearrange("p e a c -> p (e a) c")
                for f in range(4):
                    m = 0
                    for k in range(KD):
                        for a, c in ((0, 0), (0, 1), (1, 0)):
                            last = mm(ps[:, n % RR, f * P:(f + 1) * P], wtile(w, a, k, (4 * h + f) * P, P), xst[:, q, c, k, :],
                                      start=(m == 0), stop=(m == 5))
                            m += 1
                last.then_inc(s.h_done, 1)

            def rdown(i, q, j, h, e):
                n = 2 * j + h
                pe.wait_ge(s.hs_ready, CR + base[1] + n + 1 + i * (2 * RR))
                if h == 0:
                    pe.wait_ge(s.yr_taken, i * RR + j + 1 - RR + CR)
                w = wr[:, bass.ds(e, 1), :, :].rearrange("p e a c -> p (e a) c")
                for f in range(4):
                    for m, (a, c) in enumerate(((0, 0), (0, 1), (1, 0))):
                        last = mm(ps[:, YBANK + q, 0:D], hs[:, n % RR, a, f * P:(f + 1) * P], vtile(w, c, 4 * h + f),
                                  start=(h == 0 and f == 0 and m == 0), stop=(h == 1 and f == 3 and m == 2))
                last.then_inc(s.p_done, 1)

            def rbody(i, j0, count):
                for q in range(count):
                    j = j0 + q
                    e_now = expert(i, j)
                    if j0 == 0 or q + 2 < count:
                        turn(i, (q + 2) % RR, j + 2)
                    more = j0 == 0 or q + 1 < count
                    if more:
                        e_next = expert(i, j + 1)
                        rup(i, (q + 1) % RR, j + 1, 0, e_next)
                    rdown(i, q, j, 0, e_now)
                    if more:
                        rup(i, (q + 1) % RR, j + 1, 1, e_next)
                    rdown(i, q, j, 1, e_now)

            pe.wait_ge(s.table_ready, 1)
            pe.wait_ge(s.piece_low, (NE + 1) * NPIECE)
            pe.wait_ge(s.piece_high, (NE + 1) * NPIECE)
            pe.wait_ge(s.acc_done, ACC2)
            turn(0, 0, 0)
            turn(0, 1, 1)
            e0 = expert(0, 0)
            rup(0, 0, 0, 0, e0)
            rup(0, 0, 0, 1, e0)
            with pe.Fori(0, TILES // RR - 1) as i:
                rbody(i, 0, RR)
            rbody(0, TILES - RR, RR)

            pe.wait_ge(s.piece_low, (NE + 2) * NPIECE)
            pe.wait_ge(s.piece_high, (NE + 2) * NPIECE)
            pe.wait_ge(s.yr_taken, TILES + CR)
            shared(2)

        @block.scalar
        def _(act):
            act.sem_inc(s.g_ready, CR)
            act.sem_inc(s.t_taken, CR)
            act.sem_inc(s.yr_taken, CR)
            act.sem_inc(s.ys_out0, 16)
            act.sem_inc(s.ys_out1, 16)
            act.sem_inc(s.ys_out2, 16)

            def high(dst, n):
                q = n % 2
                act.wait_ge([s.piece_in0, s.piece_in1][q], 16 * (n // 2 + 1))
                act.activation(dst, stage[:, q, :], ACT.Copy, scale=SC).then_inc(s.piece_high, 1)

            def zevac(q):
                b, j = q // 2, q % 2
                act.wait_ge(s.z_done, q + 1)
                if q == 0:
                    act.wait_ge(s.prod_taken, 3)
                act.activation(zt[:, j, b * L:(b + 1) * L], ps[:, 4 + q % 4, :], ACT.Identity, bias=zbias[:, j:j + 1]).then_inc(s.z_taken, 1)

            def xntevac(q):
                b, k = q // 2, q % 2
                act.wait_ge(s.xnt_done, q + 1)
                act.copy(xnt[:, k, b * L:(b + 1) * L], ps[:, q % 4, :]).then_inc(s.xnt_taken, 1)

            def sqrt(m):
                act.wait_ge(s.sq_req, m + 1)
                b = m % B
                act.activation(rstd[:, b * TB:(b + 1) * TB, 1], rstd[:, b * TB:(b + 1) * TB, 0], ACT.Sqrt).then_inc(s.sq_done, 1)

            for b in range(B):
                sqrt(b)
                zevac(2 * b)
                zevac(2 * b + 1)
                if b:
                    xntevac(2 * b - 2)
                    xntevac(2 * b - 1)
            xntevac(2 * B - 2)
            xntevac(2 * B - 1)
            act.wait_ge(s.small_in, 80)
            act.activation(gates[:, 2:4], gates[:, 0:2], ACT.Tanh).then_inc(s.gate_done, 1)
            for b in range(B):
                act.wait_ge(s.band_done, b + 1)
                act.copy(gband[:, b, 0:L], ps[:, b, :]).then_inc(s.band_taken, 1)
                act.copy(gband[:, b, L:SKEW], ps[:, b, 0:P]).then_inc(s.band_taken, 1)
            for p in range(2):
                high(ws[:, 0, p * PIECE:(p + 1) * PIECE], p)
            act.wait_ge(s.gsum_done, 1)
            act.copy(tot, ps[32:36, 0, :]).then_inc(s.crow_ready, 1)
            act.wait_ge(s.exp_req, 1)
            act.activation(pen, cm, ACT.Exp, bias=sml[:, 1:2], scale=1.0 / D, accum_out=sml[:, 2:3]).then_inc(s.exp_done, 1)
            for p in range(2, NPIECE):
                high(ws[:, 0, p * PIECE:(p + 1) * PIECE], p)

            def xtevac(n):
                act.wait_ge(s.xt_done, n + 1)
                act.copy(xt[:, :, :, n * P:(n + 1) * P], ps[:, n % 4, :].bitcast(F16)[:, 0:4 * P].rearrange(
                    "p (a k t) -> p a k t", a=2, k=KD)).then_inc(s.xt_taken, 1)

            for b in range(B):
                sqrt(B + b)
                for n in range(b * TB, (b + 1) * TB):
                    act.wait_ge(s.norm_ready, n + 1)
                    act.activation(xh[:, n, 0, :], xn[:, n, :], ACT.Copy, scale=SC).then_inc(s.high_ready, 1)
                for n in range(max(0, b - 1) * TB, b * TB):
                    xtevac(n)
            for n in range(NT - TB, NT):
                xtevac(n)
            act.wait_ge(s.raw_done, 1)
            act.activation(sco.rearrange("p n e -> p (n e)"), ps[:, 4, 0:P], ACT.Sigmoid, scale=1.0 / (SC * SC)).then_inc(s.sig_done, 1)
            act.wait_ge(s.sig_req, 1)
            act.activation(bal, bal, ACT.Sigmoid).then_inc(s.sig_done, 1)
            act.wait_ge(s.sig_req, 2)
            act.activation(wt[:, :, 0], dv, ACT.Sigmoid).then_inc(s.sig_done, 1)
            act.activation(wt[:, :, 1], dv, ACT.Sigmoid, scale=-1.0).then_inc(s.sig_done, 1)

            def gelu(wait_h, wait_f, rb, rf):
                act.wait_ge(s.h_done, wait_h)
                act.wait_ge(s.hs_ready, wait_f)
                act.activation(hf[:, rf, :], ps[:, rb, :], ACT.Gelu, scale=1.0 / (SC * SC)).then_inc(s.g_ready, 1)

            def routed_high(i, n):
                q = n % 2
                act.wait_ge([s.piece_in0, s.piece_in1][q], 16 * (NPIECE // 2 + n // 2 + 1) + i * (16 * BODY // 2))
                if n == BODY - NPIECE:
                    act.wait_ge(s.scatter_out, 16 * 2 * NT)
                w = wr[:, bass.ds(i * (BODY // NPIECE) + n // NPIECE, 1), 0, (n % NPIECE) * PIECE:(n % NPIECE + 1) * PIECE]
                act.activation(w.rearrange("p a c -> p (a c)"), stage[:, q, :], ACT.Copy, scale=SC).then_inc(s.piece_high, 1)

            def shared(ph):
                with act.Fori(0, B // 2) as i:
                    for n in range(BODY):
                        gelu(base[ph] + n + 1 + i * BODY, CR + base[ph] + n + 1 - RF + i * BODY, n % RH, n % RF)
                        if ph == 0:
                            routed_high(i, n)

            shared(0)

            def routed_gelu(i, n):
                gelu(base[1] + n + 1 + i * (2 * RR), CR + base[1] + n + 1 - RF + i * (2 * RR), n % RR, n % RF)

            def columns(i, q, j):
                act.wait_ge(s.t_done, i * RR + j + 1)
                act.wait_ge(s.h_done, base[1] + 2 * (j - RR) + 2 + i * (2 * RR))
                act.copy(xst[:, q].rearrange("p a k c -> p (a k c)"), ps[:, 3, :].bitcast(F16)[:, 0:4 * P]).then_inc(s.t_taken, 1)

            ysout = [s.ys_out0, s.ys_out1, s.ys_out2]

            def yevac(i, q, j):
                act.wait_ge(s.p_done, CR + base[1] + 2 * j + 2 + i * (2 * RR))
                act.wait_ge(ysout[q], 16 * (j // RR + 1) + i * 16)
                act.activation(ysb[:, q, :], ps[:, 4 + q, 0:D], ACT.Copy, scale=1.0 / (SC * SC)).then_inc(s.yr_taken, 1)

            columns(0, 0, 0)
            columns(0, 1, 1)
            routed_gelu(0, 0)
            routed_gelu(0, 1)

            def rbody(i, j0, count, extra=None):
                for q in range(count):
                    j = j0 + q
                    if j0 == 0 or q + 2 < count:
                        columns(i, (q + 2) % RR, j + 2)
                    if j0 == 0 or q + 1 < count:
                        routed_gelu(i, 2 * j + 2)
                        routed_gelu(i, 2 * j + 3)
                    yevac(i, q, j)

            for p in range(NPIECE):
                high(ws[:, 0, p * PIECE:(p + 1) * PIECE], (NE + 1) * NPIECE + p)
            with act.Fori(0, TILES // RR - 1) as i:
                rbody(i, 0, RR)
            rbody(0, TILES - RR, RR)
            shared(2)

        @block.vector
        def _(v):
            v.sem_inc(s.hs_ready, CR)
            v.sem_inc(s.p_done, CR)
            v.sem_inc(s.acc_done, CR)
            count = [0]

            def link(ins):
                count[0] += 1
                ins.then_inc(s.chain, 1)
                v.wait_ge(s.chain, count[0])

            v.wait_ge(s.w_in, 16 * 7)
            v.memset(bk4, 1.0).then_inc(s.chain, 1)
            v.tensor_copy(bvb, bvT.rearrange("p (k a) -> p k a", a=1).to_broadcast([P, KD, P])).then_inc(s.chain, 1)
            count[0] = 2
            v.wait_ge(s.chain, 2)
            link(v.tensor_tensor(bk4, bk4, bkT.rearrange("p (k a) -> p k a", a=1).to_broadcast([P, KD, B]), ALU.mult))
            v.tensor_scalar(bk4, bk4, float(L), None, ALU.mult).then_inc(s.csum_done, 1)
            v.wait_ge(s.prod_done, 1)
            v.tensor_copy(wkq.rearrange("p k d -> p (k d)"), ps[:, 0, :]).then_inc(s.prod_taken, 1)
            v.tensor_copy(wvo.rearrange("p k d -> p (k d)"), ps[:, 1, :]).then_inc(s.prod_taken, 1)
            v.wait_ge(s.vec_done, 1)
            v.tensor_copy(vecs[:, 6:10], ps[:, 2, 0:4]).then_inc(s.prod_taken, 1)
            v.wait_ge(s.ubias_done, 1)
            v.tensor_copy(ubias, ps[:, 3, 0:D]).then_inc(s.prod_taken, 1)

            def norm_stats(n):
                v.bn_stats(stats[:, n, :], xres[:, n, :]).then_inc(s.chain, 1)

            def rstds(b, m):
                t = slice(b * TB, (b + 1) * TB)
                v.tensor_scalar(rstd[:, t, 0], mv[:, t, 1], EPS, None, ALU.add).then_inc(s.sq_req, 1)
                v.wait_ge(s.sq_done, m + 1)
                link(v.reciprocal(rstd[:, t, 2], rstd[:, t, 1]))
                link(v.tensor_tensor(rstd[:, t, 3], rstd[:, t, 0], rstd[:, t, 2], ALU.mult))
                link(v.tensor_tensor(rstd[:, t, 3], rstd[:, t, 3], rstd[:, t, 1], ALU.add))
                link(v.tensor_scalar(rstd[:, t, 3], rstd[:, t, 3], 0.5, None, ALU.mult))
                link(v.reciprocal(rstd[:, t, 2], rstd[:, t, 3]))

            xin = [s.x_in0, s.x_in1, s.x_in2, s.x_in3]
            for b in range(B):
                v.wait_ge(xin[b], 16)
                for n in range(b * TB, (b + 1) * TB):
                    norm_stats(n)
                count[0] += TB
                v.wait_ge(s.chain, count[0])
                for n in range(b * TB, (b + 1) * TB):
                    v.bn_aggr(mv[:, n, :], stats[:, n, :]).then_inc(s.chain, 1)
                count[0] += TB
                v.wait_ge(s.chain, count[0])
                rstds(b, b)
                for n in range(b * TB, (b + 1) * TB):
                    v.tensor_scalar(xn[:, n, :], xres[:, n, :], mv[:, n, 0:1], rstd[:, n, 2:3], ALU.subtract, ALU.mult).then_inc(s.xn_ready, 1)
            v.wait_ge(s.ctx_in, 16)
            v.tensor_reduce(csum, ctxt.rearrange("p k (b t) -> p k b t", b=B), AX, ALU.add).then_inc(s.csum_done, 1)
            v.wait_ge(s.small_in, 80)
            v.wait_ge(s.gate_done, 1)
            v.wait_ge(s.xn_ready, NT)
            v.scalar_tensor_tensor(out=xres[:, :, :], in0=bob.rearrange("p (a d) -> p a d", a=1).to_broadcast([P, NT, D]),
                                   scalar=gates[:, 2:3], in1=xres[:, :, :], op0=ALU.mult, op1=ALU.add).then_inc(s.xb_ready, 1)
            v.tensor_scalar(cent[:, 0], centf, SC, None, ALU.mult).then_inc(s.cent_split, 1)
            v.wait_ge(s.cent_split, 1)
            v.scalar_tensor_tensor(out=cent[:, 1], in0=centf, scalar=SC, in1=cent[:, 0], op0=ALU.mult, op1=ALU.subtract).then_inc(s.cent_split, 1)

            def uevac(q):
                v.wait_ge(s.u_done, q + 1)
                if q == 0:
                    v.wait_ge(s.prod_taken, 4)
                v.tensor_tensor(u[:, 2 * q:2 * q + 2, :], ps[:, 4 + q % 4, :].rearrange("p (n d) -> p n d", n=2),
                                ubias.rearrange("p (a d) -> p a d", a=1).to_broadcast([P, 2, D]), ALU.add).then_inc(s.u_taken, 1)

            for q in range(NT // 2):
                uevac(q)

            def low(dst, hi, n):
                q = n % 2
                v.wait_ge([s.piece_in0, s.piece_in1][q], 16 * (n // 2 + 1))
                v.wait_ge(s.piece_high, n + 1)
                v.scalar_tensor_tensor(out=dst, in0=stage[:, q, :], scalar=SC, in1=hi, op0=ALU.mult, op1=ALU.subtract).then_inc(s.piece_low, 1)

            for p in range(2):
                low(ws[:, 1, p * PIECE:(p + 1) * PIECE], ws[:, 0, p * PIECE:(p + 1) * PIECE], p)

            v.wait_ge(s.sbias_done, 1)
            link(v.tensor_copy(sml[:, 0:1], ps[0:B, 1, 0:1]))
            v.wait_ge(s.crow_ready, 1)
            link(v.max(top8, tot))
            link(v.memset(top8[:, LAGS:8], -BIG))
            link(v.match_replace(rep, top8, tot, -BIG))
            link(v.tensor_tensor(pen, tot, rep, ALU.is_gt))
            link(v.tensor_scalar(pen, pen, -1.0, 1e30, ALU.add, ALU.mult))
            link(v.scalar_tensor_tensor(out=cm, in0=ps[0:B, 0, :], scalar=sml[:, 0:1], in1=pen, op0=ALU.add, op1=ALU.add))
            link(v.reduce_max(sml[:, 3:4], cm, AX))
            v.tensor_scalar(sml[:, 1:2], sml[:, 3:4], -1.0 / D, None, ALU.mult).then_inc(s.exp_req, 1)
            v.wait_ge(s.exp_done, 1)
            link(v.reciprocal(sml[:, 3:4], sml[:, 2:3]))
            link(v.tensor_scalar(crow[:, P - 1:SKEW - 1], pen, sml[:, 3:4], None, ALU.mult))
            v.tensor_copy(crow[:, 0:P - 1], crow[:, L:SKEW - 1]).then_inc(s.crow_ready, 1)
            v.wait_ge(s.circ_in, 16)
            for b in range(B):
                a = craw[:, b, :]
                v.tensor_copy(circ[:, b, :], bass.AP(a.tensor, a.offset + L - 1, [a.ap[0], [-1, L]])).then_inc(s.circ_ready, 1)
            for p in range(2, NPIECE):
                low(ws[:, 1, p * PIECE:(p + 1) * PIECE], ws[:, 0, p * PIECE:(p + 1) * PIECE], p)

            v.wait_ge(s.xb_ready, 1)
            for b in range(B):
                for n in range(b * TB, (b + 1) * TB):
                    v.wait_ge(s.mix_done, n - n % 2 + 2)
                    v.scalar_tensor_tensor(out=xres[:, n, :], in0=ps[:, 4 + n // 2 % 4, (n % 2) * D:(n % 2 + 1) * D],
                                           scalar=gates[:, 2:3], in1=xres[:, n, :], op0=ALU.mult, op1=ALU.add).then_inc(s.x2_ready, 1)
                v.wait_ge(s.x2_ready, (b + 1) * TB)
                for n in range(b * TB, (b + 1) * TB):
                    norm_stats(n)
                count[0] += TB
                v.wait_ge(s.chain, count[0])
                for n in range(b * TB, (b + 1) * TB):
                    v.bn_aggr(mv[:, n, :], stats[:, n, :]).then_inc(s.chain, 1)
                count[0] += TB
                v.wait_ge(s.chain, count[0])
                rstds(b, B + b)
                for n in range(b * TB, (b + 1) * TB):
                    v.tensor_scalar(xn[:, n, :], xres[:, n, :], mv[:, n, 0:1], rstd[:, n, 2:3], ALU.subtract, ALU.mult).then_inc(s.norm_ready, 1)
                for n in range(b * TB, (b + 1) * TB):
                    v.wait_ge(s.high_ready, n + 1)
                    v.scalar_tensor_tensor(out=xh[:, n, 1, :], in0=xn[:, n, :], scalar=SC, in1=xh[:, n, 0, :],
                                           op0=ALU.mult, op1=ALU.subtract).then_inc(s.split_ready, 1)
            v.wait_ge(s.norm_ready, NT)
            v.scalar_tensor_tensor(out=xres[:, :, :], in0=xn, scalar=gates[:, 3:4], in1=xres[:, :, :],
                                   op0=ALU.mult, op1=ALU.add).then_inc(s.acc_done, 1)
            link(v.tensor_scalar(gates[:, 0:1], gates[:, 3:4], 1.0 / (SC * SC), None, ALU.mult))

            e16 = lambda a: a.rearrange("p (n e) -> p n e", e=1).to_broadcast([P, NT, NE])
            v.wait_ge(s.const_ready, 5)
            v.wait_ge(s.raw_done, 1)
            v.wait_ge(s.sig_done, 1)
            v.scalar_tensor_tensor(out=bal, in0=ps[:, 4, 0:P].rearrange("p (n e) -> p n e", e=NE), scalar=1.0 / (SC * SC), in1=rbias[:, :].rearrange("p (a e) -> p a e", a=1).to_broadcast([P, NT, NE]),
                                   op0=ALU.mult, op1=ALU.add).then_inc(s.sig_req, 1)
            v.wait_ge(s.const_ready, 5)
            link(v.tensor_reduce(selE, identf.rearrange("p (n e) -> p e n", e=NE), AX, ALU.add))
            link(v.tensor_tensor(trine, tri[:, :].rearrange("p (n e) -> p n e", e=NE),
                                 selE.rearrange("p (a e) -> p a e", a=1).to_broadcast([P, NT, NE]), ALU.mult))
            link(v.tensor_scalar(upper, upper, 0.0, None, ALU.is_gt))
            v.wait_ge(s.sig_done, 2)
            for oh, sc in ((oh1, s1v), (oh2, s2v)):
                link(v.tensor_reduce(m1, bal, AX, ALU.max))
                link(v.tensor_tensor(key, bal, e16(m1), ALU.is_ge))
                link(v.tensor_tensor(key, key, ramp, ALU.mult))
                link(v.tensor_reduce(k1, key, AX, ALU.max))
                link(v.tensor_tensor(oh, key, e16(k1), ALU.is_equal))
                link(v.tensor_tensor(tmp, oh, sco, ALU.mult))
                link(v.tensor_reduce(sc, tmp, AX, ALU.add))
                link(v.scalar_tensor_tensor(out=bal, in0=oh, scalar=-4.0, in1=bal, op0=ALU.mult, op1=ALU.add))
            v.tensor_tensor(dv, s1v, s2v, ALU.subtract).then_inc(s.sig_req, 1)
            v.tensor_tensor(both, oh1, oh2, ALU.add).then_inc(s.disp_req, 1)
            v.wait_ge(s.disp_done, 1)
            link(v.tensor_copy(totc, ps[:, 5, 0:1]))
            v.tensor_scalar(totb, ones, totc, None, ALU.mult).then_inc(s.disp_req, 1)
            v.wait_ge(s.disp_done, 3)
            link(v.tensor_copy(cnt, ps[:, 7, 0:NE]))
            link(v.tensor_tensor(tmp.rearrange("p n e -> p (n e)").rearrange("p (e t) -> p e t", e=NE),
                                 cnt.rearrange("p (e a) -> p e a", a=1).to_broadcast([P, NE, NT]), lag_ramp, ALU.is_gt))
            link(v.tensor_reduce(ntile, tmp.rearrange("p n e -> p (n e)").rearrange("p (e t) -> p e t", e=NE), AX, ALU.add))
            link(v.tensor_tensor(up2, upper, ntile.rearrange("p (a e) -> p a e", a=1).to_broadcast([P, NE, NE]), ALU.mult))
            link(v.tensor_reduce(first, up2, AX, ALU.add))
            link(v.scalar_tensor_tensor(out=pos, in0=first.rearrange("p (a e) -> p a e", a=1).to_broadcast([P, NT, NE]), scalar=float(P),
                                        in1=ps[:, 6, 0:P].rearrange("p (n e) -> p n e", e=NE), op0=ALU.mult, op1=ALU.add))
            for k, oh in enumerate((oh1, oh2)):
                link(v.tensor_tensor(tmp, oh, pos, ALU.mult))
                link(v.tensor_reduce(k1, tmp, AX, ALU.add))
                v.tensor_copy(slots[:, :, k], k1).then_inc(s.slots_ready, 1)
                v.wait_ge(s.slots_ready, k + 1)
            v.wait_ge(s.sig_done, 4)
            v.tensor_scalar(wt[:, :, 2:4], wt[:, :, 0:2], gates[:, 3:4], None, ALU.mult).then_inc(s.disp_req, 1)
            link(v.tensor_tensor(jcmp, jramp.rearrange("p (j a) -> p j a", a=1).to_broadcast([1, ETAB, NE]),
                                 first[0:1].rearrange("p (a e) -> p a e", a=1).to_broadcast([1, ETAB, NE]), ALU.is_ge))
            link(v.tensor_reduce(ej, jcmp, AX, ALU.add))
            v.tensor_scalar(etab[:, :], ej, -1.0, None, ALU.add).then_inc(s.table_ready, 1)

            def split(g0, i, step, n, rs, p0):
                v.wait_ge(s.g_ready, CR + g0 + n + 1 + i * step)
                v.wait_ge(s.p_done, CR + p0 + i * step)
                v.tensor_scalar(hs[:, rs, 0, :], hf[:, n % RF, :], SC, None, ALU.mult).then_inc(s.hi_done, 1)
                v.wait_ge(s.hi_done, g0 + n + 1 + i * step)
                v.scalar_tensor_tensor(out=hs[:, rs, 1, :], in0=hf[:, n % RF, :], scalar=SC, in1=hs[:, rs, 0, :],
                                       op0=ALU.mult, op1=ALU.subtract).then_inc(s.hs_ready, 1)

            def accumulate(ph, i, at, **k):
                start, step = ((ACC0, 4), None, (ACC2, STEP2))[ph]
                v.wait_ge(s.acc_done, start + at + i * step)
                v.scalar_tensor_tensor(**k, op0=ALU.mult, op1=ALU.add).then_inc(s.acc_done, 1)

            def add_block(ph, i, blk):
                v.wait_ge(s.p_done, CR + base[ph] + KF * (blk + 1) + i * BODY)
                for h in range(2):
                    o = xres[:, bass.ds(i * (2 * TB) + blk * TB + 2 * h, 2), :].rearrange("p n d -> p (n d)")
                    at = h + (2 * blk if ph == 0 else (KF + 2 if blk == 0 else BODY + 2))
                    accumulate(ph, i, at, out=o, in0=ps[:, RH + 2 * blk + h, :], scalar=gates[:, 0:1], in1=o)

            def routed_low(i, n):
                q = n % 2
                v.wait_ge(s.piece_high, NPIECE + n + 1 + i * BODY)
                w = wr[:, bass.ds(i * (BODY // NPIECE) + n // NPIECE, 1), :, (n % NPIECE) * PIECE:(n % NPIECE + 1) * PIECE]
                w = w.rearrange("p e a c -> p (e a) c")
                v.scalar_tensor_tensor(out=w[:, 1, :], in0=stage[:, q, :], scalar=SC, in1=w[:, 0, :],
                                       op0=ALU.mult, op1=ALU.subtract).then_inc(s.piece_low, 1)

            gin = [s.gather_in0, s.gather_in1, s.gather_in2, s.gather_in3,
                   s.gather_in4, s.gather_in5, s.gather_in6, s.gather_in7]

            def combine(i, n):
                m = n % 8
                v.wait_ge(gin[m], 16 * (n // 8 + 1) + i * (16 * BODY // 8))
                o = xres[:, bass.ds(i * (BODY // 2) + n // 2, 1), :].rearrange("p n d -> p (n d)")
                w = wt[:, bass.ds(i * (BODY // 2) + n // 2, 1), 2 + n % 2]
                accumulate(2, i, pos_of(n), out=o, in0=gat[:, m, :], scalar=w, in1=o)

            def shared(ph):
                with v.Fori(0, B // 2) as i:
                    for n in range(BODY):
                        split(base[ph], i, BODY, n, n % RH, base[ph] + n + 1 - RH)
                        if n == KF + 2:
                            add_block(ph, i, 0)
                        if ph == 0:
                            routed_low(i, n)
                        else:
                            combine(i, n)
                    add_block(ph, i, 1)

            v.wait_ge(s.disp_req, 3)
            shared(0)

            split(base[1], 0, 2 * RR, 0, 0, base[1])
            split(base[1], 0, 2 * RR, 1, 1, base[1])
            for p in range(NPIECE):
                low(ws[:, 1, p * PIECE:(p + 1) * PIECE], ws[:, 0, p * PIECE:(p + 1) * PIECE], (NE + 1) * NPIECE + p)

            def rbody(i, j0, cnt_):
                for q in range(cnt_):
                    j = j0 + q
                    if j0 == 0 or q + 1 < cnt_:
                        for h in range(2):
                            n = 2 * j + 2 + h
                            split(base[1], i, 2 * RR, n, n % RR, base[1] + n + 1 - RR)

            with v.Fori(0, TILES // RR - 1) as i:
                rbody(i, 0, RR)
            rbody(0, TILES - RR, RR)
            shared(2)


def kernel(x, ctx_1024, g_xattn, g_ffn, L0_xattn_Wq, L0_xattn_bq, L0_xattn_Wk, L0_xattn_bk, L0_xattn_Wv, L0_xattn_bv,
           L0_xattn_Wo, L0_xattn_bo, L0_ffn_centroids, L0_ffn_routing_bias, L0_ffn_Wfc_r, L0_ffn_Wproj_r,
           L0_ffn_Wfc_sh, L0_ffn_Wproj_sh):
    import numpy as np
    import concourse.bacc as bacc
    from concourse.bass_utils import run_bass_kernel_spmd

    c = np.ascontiguousarray
    wfc = np.concatenate([np.asarray(L0_ffn_Wfc_sh)[:1], np.asarray(L0_ffn_Wfc_r), np.asarray(L0_ffn_Wfc_sh)[1:]])
    wpr = np.concatenate([np.asarray(L0_ffn_Wproj_sh)[:1], np.asarray(L0_ffn_Wproj_r), np.asarray(L0_ffn_Wproj_sh)[1:]])
    n = NE + NS
    wfc = wfc.transpose(0, 2, 1).reshape(n, KD, P, F)
    wpr = wpr.transpose(0, 2, 1).reshape(n, 2, KF // 2, P, D).transpose(0, 1, 3, 2, 4).reshape(n, 2, P, KF // 2 * D)
    arrays = {
        "x": c(np.asarray(x).reshape(T, D)), "ctxT": c(np.asarray(ctx_1024).reshape(T, D).T),
        "Wq": c(L0_xattn_Wq), "Wk": c(L0_xattn_Wk), "Wv": c(L0_xattn_Wv), "WoT": c(np.asarray(L0_xattn_Wo).T),
        "bq": c(L0_xattn_bq), "bk": c(L0_xattn_bk), "bv": c(L0_xattn_bv), "bo": c(L0_xattn_bo),
        "gx": c(g_xattn), "gf": c(g_ffn), "centT": c(np.asarray(L0_ffn_centroids).T), "rb": c(L0_ffn_routing_bias),
        "W": c(np.concatenate([wfc, wpr], axis=1).reshape(n * NPIECE, P, PIECE)),
    }
    nc = bacc.Bacc("TRN2", target_bir_lowering=False, num_devices=1)
    A = {k: nc.dram_tensor("in_" + k, a.shape, mybir.dt.from_np(a.dtype), kind="ExternalInput").ap() for k, a in arrays.items()}
    A["out"] = nc.dram_tensor("out_y", (T, D), F32, kind="ExternalOutput").ap()
    build_kernel(nc, A)
    r = run_bass_kernel_spmd(nc, [{"in_" + k: a for k, a in arrays.items()}], core_ids=[0])
    return np.asarray(r.results[0]["out_y"]).reshape(B, L, D)
```

```python
from contextlib import ExitStack

import concourse.bass as bass
from concourse import mybir

F32 = mybir.dt.float32
F16 = mybir.dt.float16
I32 = mybir.dt.int32
U32 = mybir.dt.uint32
ALU = mybir.AluOpType
ACT = mybir.ActivationFunctionType
AX = mybir.AxisListType.X

P = 128
B, L, D = 4, 512, 256
T = B * L
NT = T // P
TB = L // P
KD = D // P
NE, NS, F = 8, 2, 1024
KF = F // P
LAGS = 6
SKEW = L + P
RT = 256
HT = RT // P
TILES = (2 * T - NE) // RT + NE
SLOTS = TILES * RT
ETAB = TILES + 1
UNIT = 512
PIECE = 1024
NPIECE = 2 * KD * F // PIECE
WID = 2 * KD * F
SC = 16.0
EPS = 1e-5
BIG = 3.0e38
RH, RF = 4, 2
RR = 2
RU = 4
CR = 4
NWARM = NE + NS


def build_kernel(nc, A):
    with ExitStack() as ctx:
        def sb(name, shape, dt=F32):
            return ctx.enter_context(nc.sbuf_tensor(name, shape, dt))

        def sem(name):
            return ctx.enter_context(nc.semaphore(name))

        wr = sb("wr", [P, NE, 2, WID], F16)
        ws = sb("ws", [P, 2, WID], F16)
        xres = sb("xres", [P, NT, D])
        xt = sb("xt", [P, 2, KD, T], F16)
        stage = sb("stage", [P, 2, PIECE])
        hf = sb("hf", [P, RF, UNIT])
        hs = sb("hs", [P, RH, 2, UNIT], F16)
        rt = sb("rt", [P, 9 * 512], F16)
        tri = sb("tri", [P, P])
        identh = sb("identh", [P, P], F16)
        stats = sb("stats", [P, NT, 6])
        mv = sb("mv", [P, NT, 2])
        rstd = sb("rstd", [P, NT, 4])
        gates = sb("gates", [P, 8])
        cent = sb("cent", [P, 2, KD, NE], F16)
        rbias = sb("rbias", [P, NE])
        slots = sb("slots", [P, NT, 2], U32)
        wt = sb("wt", [P, NT, 4])
        etab = sb("etab", [1, ETAB], I32)

        def region(e):
            return wr[:, e, :, :].rearrange("p a b -> p (a b)").bitcast(F32)

        ctxt = region(0).rearrange("p (k t) -> p k t", k=KD)
        xnt = region(1).rearrange("p (k t) -> p k t", k=KD)
        zt = region(2).rearrange("p (k t) -> p k t", k=KD)
        u = region(3).rearrange("p (n d) -> p n d", n=NT)
        xn = region(4).rearrange("p (n d) -> p n d", n=NT)
        r5, r6 = region(5), region(6)
        gband = r5[:, 0:B * SKEW].rearrange("p (b j) -> p b j", b=B)
        wkq = r5[:, B * SKEW:B * SKEW + KD * D].rearrange("p (k d) -> p k d", k=KD)
        wvo = r5[:, B * SKEW + KD * D:B * SKEW + 2 * KD * D].rearrange("p (k d) -> p k d", k=KD)
        small5 = B * SKEW + 2 * KD * D
        csum = r5[:, small5:small5 + KD * B].rearrange("p (k b) -> p k b", k=KD)
        bvb = r5[:, small5 + 8:small5 + 8 + KD * P].rearrange("p (k m) -> p k m", k=KD)
        craw = r6[:, 0:B * L].rearrange("p (b j) -> p b j", b=B)
        circ = r5[:, 0:B * L].rearrange("p (b j) -> p b j", b=B)
        o6 = B * L
        ubias = r6[:, o6:o6 + D]
        bob = r6[:, o6 + D:o6 + 2 * D]
        identf = r6[:, o6 + 2 * D:o6 + 2 * D + P]
        sel = r6[:, o6 + 2 * D + P:o6 + 2 * D + P + B * 36].rearrange("p (b m) -> p b m", b=B)
        o7 = o6 + 2 * D + P + B * 36
        vecs = r6[:, o7:o7 + 32]
        bkT, bqT, bvT = vecs[:, 0:2], vecs[:, 2:4], vecs[:, 4:6]
        zbias, v1 = vecs[:, 6:8], vecs[:, 8:10]
        bk4 = vecs[:, 10:18].rearrange("p (k b) -> p k b", k=KD)
        centf = r6[:, o7 + 32:o7 + 32 + KD * NE].rearrange("p (k e) -> p k e", k=KD)
        gsk = r6[:, 0:B * L].rearrange("p (b j) -> p b j", b=B)
        xh = wr[:, NE - 1, :, :].rearrange("p a b -> p (a b)").rearrange("p (n s d) -> p n s d", n=NT, s=2)
        xtf = xt[:, :, :, :].rearrange("p a k t -> p (a k t)").bitcast(F32)
        wsrc = xtf[:, 0:4 * KD * D].rearrange("p (w k d) -> p w k d", w=4, k=KD)
        wq, wk, wv, wo = (wsrc[:, i] for i in range(4))
        rows = xtf[0:B, 4 * KD * D:4 * KD * D + 2048].rearrange("p (a j) -> p a j", j=512)
        tot, rep, pen, cm = (rows[:, i] for i in range(4))
        crow = hf[0:B, :, :].rearrange("p a b -> p (a b)")[:, 0:SKEW]
        sml = gates[0:B, 4:8]
        top8 = rstd[0:B, 0:2, :].rearrange("p a b -> p (a b)")

        rtf = rt[:, :].bitcast(F32)
        dsp = rtf[:, 0:14 * P].rearrange("p (a n e) -> p a n e", a=14, e=NE)
        bal, sco, key, oh1, oh2, both, pos, trine, tmp, _, ramp = (dsp[:, i] for i in range(11))
        totb = rtf[:, 11 * P:12 * P]
        ones = rtf[:, 12 * P:13 * P]
        m13 = rtf[:, 13 * P:14 * P]
        lag_ramp = rtf[:, 14 * P:15 * P].rearrange("p (e t) -> p e t", e=NE)
        selE = m13[:, 0:8]
        cnt = m13[:, 8:16]
        ntile = m13[:, 16:24]
        first = m13[:, 24:32]
        totc = m13[:, 32:33]
        m1 = m13[:, 48:64]
        k1 = m13[:, 64:80]
        s1v = m13[:, 80:96]
        s2v = m13[:, 96:112]
        dv = m13[:, 112:128]
        zero = rt[:, 0:1024]
        upper = rtf[:, 15 * P:15 * P + 64].rearrange("p (e f) -> p e f", e=NE)
        up2 = rtf[:, 15 * P + 64:16 * P].rearrange("p (e f) -> p e f", e=NE)
        jramp = rtf[0:1, 16 * P:16 * P + ETAB * 1]
        jcmp = rtf[0:1, 0:ETAB * NE].rearrange("p (j e) -> p j e", e=NE)
        ej = rtf[0:1, 17 * P:17 * P + ETAB]
        xs = rt[:, 0:RR * HT * 2 * D].rearrange("p (r h c) -> p r h c", r=RR, h=HT)
        xst = rt[:, RR * HT * 2 * D:2 * RR * HT * 2 * D].rearrange("p (r a k c) -> p r a k c", r=RR, a=2, k=KD)
        ysb = stage[:, :, :].rearrange("p a c -> p (a c)")[:, 0:RR * HT * D].rearrange("p (r h d) -> p r h d", r=RR, h=HT)
        gat = rtf[:, 0:8 * D].rearrange("p (r d) -> p r d", r=8)

        ps = ctx.enter_context(nc.psum_tensor("ps", [P, 8, 512], F32))

        band_d = nc.dram_tensor("band_d", [P, B, SKEW], F32).ap()
        crow_d = nc.dram_tensor("crow_d", [B, SKEW], F32).ap()
        xslot_d = nc.dram_tensor("xslot_d", [SLOTS, 2 * D], F16).ap()
        yslot_d = nc.dram_tensor("yslot_d", [SLOTS, D], F32).ap()

        names = ("x_in0 x_in1 x_in2 x_in3 w_in ctx_in small_in const_ready prod_done vec_done ubias_done prod_taken "
                 "z_done z_taken xn_ready xnt_done xnt_taken band_done band_taken u_done u_taken csum_done "
                 "band_out skew_in gsum_done sbias_done chain crow_ready crow_out circ_in circ_ready mix_done x2_ready "
                 "sq_req sq_done exp_req exp_done hi_done gate_done norm_ready high_ready split_ready xt_done xt_taken raw_done sig_req "
                 "sig_done disp_req disp_done slots_ready table_ready zero_set zero_out scatter_out "
                 "piece_in0 piece_in1 piece_high piece_low "
                 "h_done g_ready hs_ready p_done cent_split "
                 "xs_in0 xs_in1 t_done t_taken yr_taken ys_out0 ys_out1 "
                 "gather_in0 gather_in1 gather_in2 gather_in3 gather_in4 gather_in5 gather_in6 gather_in7 "
                 "out_done xb_ready acc_done")
        S = {n: sem(n) for n in names.split()}
        s = type("Sems", (), S)

        block = ctx.enter_context(nc.Block())

        def wtile(w, part, k, f0, n):
            return w[:, part, k * F + f0:k * F + f0 + n]

        def vtile(w, part, f):
            return w[:, part, KD * F + f * D:KD * F + (f + 1) * D]

        SH_UNITS = B * KF
        RT_UNITS = RU * TILES
        base = [0, SH_UNITS, SH_UNITS + RT_UNITS]
        BODY = 2 * KF
        ACC0 = CR + 1
        ACC2 = ACC0 + 4 * (B // 2)
        STEP2 = BODY + 4

        LOOP = (TILES - RR - 1) // RR

        def pos_of(n):
            return n if n < KF + 2 else n + 2

        @block.sync
        def _(sp):
            xin = [s.x_in0, s.x_in1, s.x_in2, s.x_in3]
            xr = A["x"].rearrange("(n p) d -> p n d", p=P)
            sp.dma_start(xres[:, 0:TB, :], xr[:, 0:TB, :]).then_inc(s.x_in0, 16)
            for i, nm in enumerate(("Wk", "Wq", "Wv", "WoT")):
                j = (1, 0, 2, 3)[i]
                sp.dma_start(wsrc[:, j], A[nm].rearrange("(k p) d -> p k d", p=P)).then_inc(s.w_in, 16)
            for nm, dst in (("bk", bkT), ("bq", bqT), ("bv", bvT)):
                with nc.allow_non_contiguous_dma(reason="a bias as a column"):
                    sp.dma_start(dst, A[nm].rearrange("(k p) -> p k", p=P)).then_inc(s.w_in, 16)
            sp.dma_start(ctxt, A["ctxT"].rearrange("(k p) t -> p k t", p=P)).then_inc(s.ctx_in, 16)
            for b in range(1, B):
                sp.dma_start(xres[:, b * TB:(b + 1) * TB, :], xr[:, b * TB:(b + 1) * TB, :]).then_inc(xin[b], 16)
            sp.dma_start(bob, A["bo"].rearrange("(a d) -> a d", a=1).to_broadcast([P, D])).then_inc(s.small_in, 16)
            sp.dma_start(gates[:, 0:1], A["gx"].rearrange("(a d) -> a d", a=1).to_broadcast([P, 1])).then_inc(s.small_in, 16)
            sp.dma_start(gates[:, 1:2], A["gf"].rearrange("(a d) -> a d", a=1).to_broadcast([P, 1])).then_inc(s.small_in, 16)
            sp.dma_start(rbias[:, :], A["rb"].rearrange("(a d) -> a d", a=1).to_broadcast([P, NE])).then_inc(s.small_in, 16)
            with nc.allow_non_contiguous_dma(reason="centroids in columns"):
                sp.dma_start(centf, A["centT"].rearrange("(k p) e -> p k e", p=P)).then_inc(s.small_in, 16)
            sp.wait_ge(s.zero_set, 1)
            zsrc = bass.AP(zero.tensor, zero.offset, [zero.ap[0], [0, SLOTS // P], [1, 2 * D]])
            sp.dma_start(xslot_d.rearrange("(t p) c -> p t c", p=P), zsrc).then_inc(s.zero_out, 16)
            def piece(p):
                if p >= 2:
                    sp.wait_ge(s.piece_low, p - 1)
                sp.dma_start(stage[:, p % 2, :], A["W"][p]).then_inc([s.piece_in0, s.piece_in1][p % 2], 16)

            piece(0)
            piece(1)
            for b in range(B):
                sp.wait_ge(s.band_taken, 2 * (b + 1))
                sp.dma_start(band_d[:, b, :], gband[:, b, :]).then_inc(s.band_out, 16)
            sp.wait_ge(s.band_out, 16 * B)
            skew = bass.AP(band_d.tensor, band_d.offset, [[B * SKEW + 1, P], [SKEW, B], [1, L]])
            sp.dma_start(gsk, skew).then_inc(s.skew_in, 16)
            sp.wait_ge(s.crow_ready, 2)
            sp.dma_start(crow_d[:, 0:SKEW - 1], crow[:, 0:SKEW - 1]).then_inc(s.crow_out, 16)
            sp.wait_ge(s.crow_out, 16)
            cskew = bass.AP(crow_d.tensor, crow_d.offset, [[1, P], [SKEW, B], [1, L]])
            sp.dma_start(craw, cskew).then_inc(s.circ_in, 16)
            piece(2)
            piece(3)
            with sp.Fori(0, NE * NPIECE // 2) as i:
                for q in range(2):
                    sp.wait_ge(s.piece_low, NPIECE - 1 + q + i * 2)
                    e = i * 2 + (NPIECE + q)
                    sp.dma_start(stage[:, q, :], A["W"][bass.ds(e, 1)].rearrange("a p c -> (a p) c")).then_inc(
                        [s.piece_in0, s.piece_in1][q], 16)
            piece((NE + 1) * NPIECE)
            piece((NE + 1) * NPIECE + 1)
            sp.wait_ge(s.scatter_out, 16 * 2 * NT)
            sp.wait_ge(s.table_ready, 1)
            xsin = [s.xs_in0, s.xs_in1]
            ysout = [s.ys_out0, s.ys_out1]
            for j in range(RR):
                sp.dma_start(xs[:, j], xslot_d[j * RT:(j + 1) * RT, :].rearrange("(h p) c -> p h c", p=P)).then_inc(xsin[j], 16)
            piece((NE + 1) * NPIECE + 2)
            piece((NE + 1) * NPIECE + 3)

            def load(i, j):
                sp.wait_ge(s.t_done, i * RR + j - RR + 1)
                rows_ = xslot_d[bass.ds(i * (RR * RT) + j * RT, RT), :]
                sp.dma_start(xs[:, j % RR], rows_.rearrange("(h p) c -> p h c", p=P)).then_inc(xsin[j % RR], 16)

            def store(i, j):
                sp.wait_ge(s.yr_taken, i * RR + j + 1 + CR)
                rows_ = yslot_d[bass.ds(i * (RR * RT) + j * RT, RT), :]
                sp.dma_start(rows_.rearrange("(h p) d -> p h d", p=P), ysb[:, j % RR]).then_inc(ysout[j % RR], 16)
            load(0, RR)
            with sp.Fori(0, LOOP) as i:
                for j in range(RR):
                    load(i, j + RR + 1)
                    store(i, j)
            for j in range(LOOP * RR, TILES):
                if j + RR + 1 < TILES:
                    load(0, j + RR + 1)
                store(0, j)
            for b in range(B):
                sp.wait_ge(s.acc_done, ACC2 + (b // 2) * STEP2 + (12 if b % 2 == 0 else STEP2))
                o = A["out"].rearrange("(n p) d -> p n d", p=P)
                sp.dma_start(o[:, b * TB:(b + 1) * TB, :], xres[:, b * TB:(b + 1) * TB, :]).then_inc(s.out_done, 16)
            sp.wait_ge(s.out_done, 16 * B)

        @block.gpsimd
        def _(pool):
            pool.memset(zero, 0.0).then_inc(s.zero_set, 1)
            pool.memset(identf, 0.0)
            pool.memset(tri[:, :], 1.0)
            pool.memset(sel, 0.0).then_inc(s.const_ready, 1)
            pool.wait_ge(s.const_ready, 1)
            for b in range(B):
                pool.memset(sel[:, b, b:b + 1], 1.0)
            pool.memset(sel[:, :, 32:36], 1.0)
            pool.affine_select(out=identf, in_=identf, compare_op=ALU.not_equal, fill=1.0, base=0,
                               pattern=[[-1, P]], channel_multiplier=1).then_inc(s.const_ready, 1)
            pool.affine_select(out=tri[:, :], in_=tri[:, :], compare_op=ALU.is_gt, fill=0.0, base=0,
                               pattern=[[1, P]], channel_multiplier=-1).then_inc(s.const_ready, 1)
            pool.wait_ge(s.const_ready, 3)
            pool.tensor_copy(identh[:, :], identf).then_inc(s.const_ready, 1)
            pool.wait_ge(s.zero_out, 16)
            pool.iota(lag_ramp, [[0, NE], [RT, NT]], base=0, channel_multiplier=0, allow_small_or_imprecise_dtypes=True)
            pool.iota(jramp, [[1, ETAB]], base=0, channel_multiplier=0, allow_small_or_imprecise_dtypes=True)
            pool.iota(ramp, [[0, NT], [-1, NE]], base=NE, channel_multiplier=0, allow_small_or_imprecise_dtypes=True)
            pool.iota(upper, [[1, NE], [-1, NE]], base=0, channel_multiplier=0, allow_small_or_imprecise_dtypes=True)
            pool.memset(ones, 1.0).then_inc(s.const_ready, 1)
            pool.wait_ge(s.slots_ready, 2)
            pool.wait_ge(s.split_ready, NT)
            pool.wait_ge(s.high_ready, NT)
            for n in range(NT):
                for k in range(2):
                    pool.indirect_dma_start(xslot_d, bass.IndirectOffsetOnAxis(slots[:, n, k:k + 1], 0),
                                            xh[:, n].rearrange("p s d -> p (s d)"), None).then_inc(s.scatter_out, 16)
            for q, so in enumerate((s.ys_out0, s.ys_out1)):
                pool.wait_ge(so, 16 * (len(range(q, TILES, RR)) + 1))
            gin = [s.gather_in0, s.gather_in1, s.gather_in2, s.gather_in3,
                   s.gather_in4, s.gather_in5, s.gather_in6, s.gather_in7]
            for n in range(NT):
                for k in range(2):
                    m = 2 * n + k
                    if m >= 8:
                        pool.wait_ge(s.acc_done, ACC2 + (m - 8) // BODY * STEP2 + pos_of((m - 8) % BODY) + 1)
                    pool.indirect_dma_start(gat[:, m % 8], None, yslot_d,
                                            bass.IndirectOffsetOnAxis(slots[:, n, k:k + 1], 0)).then_inc(gin[m % 8], 16)

        @block.tensor
        def _(pe):
            mm = pe.matmul
            pe.wait_ge(s.w_in, 16 * 7)
            for c in range(KD):
                for o in range(KD):
                    mm(ps[:, 0, c * D:(c + 1) * D], wk[:, o, c * P:(c + 1) * P], wq[:, o, :], start=(o == 0), stop=(o == KD - 1))
            for c in range(KD):
                for o in range(KD):
                    last = mm(ps[:, 1, c * D:(c + 1) * D], wv[:, o, c * P:(c + 1) * P], wo[:, o, :], start=(o == 0), stop=(o == KD - 1))
            last.then_inc(s.prod_done, 1)
            for c in range(KD):
                for o in range(KD):
                    mm(ps[:, 2, c:c + 1], wq[:, o, c * P:(c + 1) * P], bkT[:, o:o + 1], start=(o == 0), stop=(o == KD - 1))
            for c in range(KD):
                for o in range(KD):
                    last = mm(ps[:, 2, 2 + c:3 + c], wk[:, o, c * P:(c + 1) * P], bqT[:, o:o + 1], start=(o == 0), stop=(o == KD - 1))
            last.then_inc(s.vec_done, 1)
            pe.wait_ge(s.chain, 2)
            for o in range(KD):
                last = mm(ps[:, 3, 0:D], bvb[:, o, :], wo[:, o, :], start=(o == 0), stop=(o == KD - 1))
            last.then_inc(s.ubias_done, 1)
            pe.wait_ge(s.ctx_in, 16)
            pe.wait_ge(s.prod_taken, 2)
            def zjob(q):
                b, j = q // 2, q % 2
                if q >= 4:
                    pe.wait_ge(s.z_taken, q - 3)
                for c in range(KD):
                    last = mm(ps[:, 4 + q % 4, :], wkq[:, c, j * P:(j + 1) * P], ctxt[:, c, b * L:(b + 1) * L], start=(c == 0), stop=(c == KD - 1))
                last.then_inc(s.z_done, 1)
            pe.wait_ge(s.const_ready, 2)

            def xntjob(q):
                b, k = q // 2, q % 2
                pe.wait_ge(s.xn_ready, (b + 1) * TB)
                if q < 4:
                    pe.wait_ge(s.prod_taken, 4)
                else:
                    pe.wait_ge(s.xnt_taken, q - 3)
                for n in range(TB):
                    last = pe.transpose(ps[:, q % 4, n * P:(n + 1) * P], xn[:, b * TB + n, k * P:(k + 1) * P], identf)
                last.then_inc(s.xnt_done, 1)

            for b in range(B):
                zjob(2 * b)
                zjob(2 * b + 1)
                xntjob(2 * b)
                xntjob(2 * b + 1)
            pe.wait_ge(s.z_taken, 2 * B)
            pe.wait_ge(s.xnt_taken, 2 * B)
            for b in range(B):
                for m in range(TB):
                    for c in range(KD):
                        z = zt[:, c, b * L + m * P:b * L + (m + 1) * P]
                        o, w = m * P, L - m * P
                        last = mm(ps[:, b, 0:w], z, xnt[:, c, b * L + o:(b + 1) * L],
                                  start=(m == 0 and c == 0), stop=False, skip_group_check=True)
                        if m:
                            last = mm(ps[:, b, w:L], z, xnt[:, c, b * L:b * L + o], start=False,
                                      stop=(m == TB - 1 and c == KD - 1), skip_group_check=True)
                last.then_inc(s.band_done, 1)
            for q in range(NT // 2):
                if q < 4:
                    pe.wait_ge(s.z_taken, 5 + q)
                else:
                    pe.wait_ge(s.u_taken, q - 3)
                for h in range(2):
                    for c in range(KD):
                        n = 2 * q + h
                        last = mm(ps[:, 4 + q % 4, h * D:(h + 1) * D], ctxt[:, c, n * P:(n + 1) * P], wvo[:, c, :],
                                  start=(c == 0), stop=(c == KD - 1))
                last.then_inc(s.u_done, 1)
            pe.wait_ge(s.csum_done, 2)
            pe.wait_ge(s.band_taken, 4)
            for c in range(KD):
                mm(ps[0:B, 1, 0:1], csum[:, c, :], v1[:, c:c + 1], start=(c == 0), stop=False)
            for o in range(KD):
                last = mm(ps[0:B, 1, 0:1], bk4[:, o, :], bqT[:, o:o + 1], start=False, stop=(o == KD - 1))
            last.then_inc(s.sbias_done, 1)
            pe.wait_ge(s.skew_in, 16)
            for b in range(B):
                last = mm(ps[0:36, 0, :], sel[:, b, :], gsk[:, b, :], start=(b == 0), stop=(b == B - 1))
            last.then_inc(s.gsum_done, 1)
            def mixjob(n):
                b, t = n // TB, n % TB
                pe.wait_ge(s.circ_ready, b + 1)
                if n % 2 == 0:
                    q = n // 2
                    if q < 4:
                        pe.wait_ge(s.u_taken, NT // 2)
                    else:
                        pe.wait_ge(s.x2_ready, 2 * (q - 3))
                for m in range(TB):
                    d = (m - t) % TB
                    last = mm(ps[:, 4 + n // 2 % 4, n % 2 * D:(n % 2 + 1) * D], circ[:, b, (TB - 1 - d) * P:(TB - d) * P],
                              u[:, b * TB + m, :], start=(m == 0), stop=(m == TB - 1))
                last.then_inc(s.mix_done, 1)
            pe.wait_ge(s.const_ready, 4)

            def xtjob(n):
                pe.wait_ge(s.split_ready, n + 1)
                pe.wait_ge(s.high_ready, n + 1)
                if n < 4:
                    pe.wait_ge(s.crow_ready, 2)
                else:
                    pe.wait_ge(s.xt_taken, n - 3)
                tb = ps[:, n % 4, :].bitcast(F16)
                for a in range(2):
                    for k in range(KD):
                        last = pe.transpose(tb[:, (a * KD + k) * P:(a * KD + k + 1) * P], xh[:, n, a, k * P:(k + 1) * P], identh[:, :])
                last.then_inc(s.xt_done, 1)
            for b in range(B + 1):
                for t in range(TB):
                    if b < B:
                        mixjob(b * TB + t)
                for t in range(TB):
                    if b:
                        xtjob((b - 1) * TB + t)
            pe.wait_ge(s.xt_taken, NT)
            pe.wait_ge(s.cent_split, 2)
            pe.wait_ge(s.x2_ready, NT)
            for n in range(NT):
                i = 0
                for k in range(KD):
                    for a, c in ((0, 0), (0, 1), (1, 0)):
                        last = mm(ps[:, 4, n * NE:(n + 1) * NE], xt[:, a, k, n * P:(n + 1) * P], cent[:, c, k, :],
                                  start=(i == 0), stop=(i == 5))
                        i += 1
            last.then_inc(s.raw_done, 1)
            pe.wait_ge(s.disp_req, 1)
            mm(ps[:, 5, 0:1], both.rearrange("p n e -> p (n e)"), ones[:, 0:1], start=True, stop=True).then_inc(s.disp_done, 1)
            pe.wait_ge(s.disp_req, 2)
            mm(ps[:, 6, 0:P], tri[:, :], both.rearrange("p n e -> p (n e)"), start=True, stop=False)
            mm(ps[:, 6, 0:P], totb, trine.rearrange("p n e -> p (n e)"), start=False, stop=True).then_inc(s.disp_done, 1)
            mm(ps[:, 7, 0:NE], totb, selE, start=True, stop=True).then_inc(s.disp_done, 1)

            def shared(ph):
                def up(i, n):
                    pe.wait_ge(s.g_ready, CR + base[ph] + n + 1 - RH + i * BODY)
                    f, blk = n % KF, n // KF
                    j = 0
                    for k in range(KD):
                        for a, c in ((0, 0), (0, 1), (1, 0)):
                            rhs = xt[:, c, k, bass.ds(i * (2 * L) + blk * L, L)]
                            last = mm(ps[:, n % RH, :], wtile(ws, a, k, f * P, P), rhs, start=(j == 0), stop=(j == 5))
                            j += 1
                    last.then_inc(s.h_done, 1)

                def down(i, n):
                    pe.wait_ge(s.hs_ready, CR + base[ph] + n + 1 + i * BODY)
                    f, blk = n % KF, n // KF
                    if f == 0:
                        if ph == 0:
                            pe.wait_ge(s.acc_done, ACC0 - 4 + 2 * (blk + 1) + i * 4)
                        else:
                            pe.wait_ge(s.acc_done, ACC2 - STEP2 + (12 if blk == 0 else STEP2) + i * STEP2)
                    for t in range(TB):
                        for j, (a, c) in enumerate(((0, 0), (0, 1), (1, 0))):
                            out = ps[:, RH + 2 * blk + t // 2, (t % 2) * D:(t % 2 + 1) * D]
                            last = mm(out, hs[:, n % RH, a, t * P:(t + 1) * P], vtile(ws, c, f),
                                      start=(f == 0 and j == 0 and t % 2 == 0), stop=(f == KF - 1 and j == 2),
                                      skip_group_check=True)
                    last.then_inc(s.p_done, 1)

                with pe.Fori(0, B // 2) as i:
                    up(i, 0)
                    up(i, 1)
                    for n in range(BODY):
                        if n + 2 < BODY:
                            up(i, n + 2)
                        down(i, n)

            pe.wait_ge(s.disp_req, 3)
            pe.wait_ge(s.piece_low, NPIECE)
            pe.wait_ge(s.piece_high, NPIECE)
            shared(0)

            xsin = [s.xs_in0, s.xs_in1]
            TBANK, YBANK = 6, 4
            FU = KF // RU

            def turn(i, j):
                pe.wait_ge(xsin[j % RR], 16 * (j // RR + 1) + i * 16)
                pe.wait_ge(s.t_taken, i * RR + j + CR)
                tb = ps[:, TBANK, :].bitcast(F16)
                for a in range(2):
                    for k in range(KD):
                        for h in range(HT):
                            o = (a * KD + k) * RT + h * P
                            last = pe.transpose(tb[:, o:o + P], xs[:, j % RR, h, a * D + k * P:a * D + (k + 1) * P], identh[:, :])
                last.then_inc(s.t_done, 1)

            def expert(i, j):
                return pe.value_load(etab[0:1, bass.ds(i * RR + j, 1)], min_val=0, max_val=NE - 1)

            def rup(i, j, g, e):
                n = RU * j + g
                if g == 0:
                    pe.wait_ge(s.t_taken, i * RR + j + 1 + CR)
                pe.wait_ge(s.g_ready, CR + base[1] + n + 1 - RH + i * (RU * RR))
                w = wr[:, bass.ds(e, 1), :, :].rearrange("p e a c -> p (e a) c")
                for f in range(FU):
                    m = 0
                    for k in range(KD):
                        for a, c in ((0, 0), (0, 1), (1, 0)):
                            last = mm(ps[:, n % RH, f * RT:(f + 1) * RT], wtile(w, a, k, (FU * g + f) * P, P), xst[:, j % RR, c, k, :],
                                      start=(m == 0), stop=(m == 5))
                            m += 1
                last.then_inc(s.h_done, 1)

            def rdown(i, j, g, e):
                n = RU * j + g
                pe.wait_ge(s.hs_ready, CR + base[1] + n + 1 + i * (RU * RR))
                if g == 0:
                    pe.wait_ge(s.yr_taken, i * RR + j + 1 - RR + CR)
                w = wr[:, bass.ds(e, 1), :, :].rearrange("p e a c -> p (e a) c")
                for f in range(FU):
                    for c, a in ((0, 0), (0, 1), (1, 0)):
                        for h in range(HT):
                            first_ = g == 0 and f == 0 and a == 0 and c == 0
                            last = mm(ps[:, YBANK + j % RR, h * D:(h + 1) * D], hs[:, n % RH, a, f * RT + h * P:f * RT + (h + 1) * P],
                                      vtile(w, c, FU * g + f), start=(first_ and h == 0),
                                      stop=(g == RU - 1 and f == FU - 1 and c == 1), skip_group_check=True)
                last.then_inc(s.p_done, 1)

            def rbody(i, j):
                e_now = expert(i, j)
                if j + 1 < TILES:
                    e_next = expert(i, j + 1)
                for g in range(RU):
                    if j + 1 < TILES:
                        rup(i, j + 1, g, e_next)
                    rdown(i, j, g, e_now)
                    if g == 1 and j + 2 < TILES:
                        turn(i, j + 2)

            pe.wait_ge(s.table_ready, 1)
            pe.wait_ge(s.piece_low, (NE + 1) * NPIECE)
            pe.wait_ge(s.piece_high, (NE + 1) * NPIECE)
            pe.wait_ge(s.acc_done, ACC2)
            turn(0, 0)
            turn(0, 1)
            e0 = expert(0, 0)
            for g in range(RU):
                rup(0, 0, g, e0)
            with pe.Fori(0, LOOP) as i:
                for j in range(RR):
                    rbody(i, j)
            for j in range(LOOP * RR, TILES):
                rbody(0, j)

            pe.wait_ge(s.piece_low, (NE + 2) * NPIECE)
            pe.wait_ge(s.piece_high, (NE + 2) * NPIECE)
            pe.wait_ge(s.yr_taken, TILES + CR)
            shared(2)

        @block.scalar
        def _(act):
            act.sem_inc(s.g_ready, CR)
            act.sem_inc(s.t_taken, CR)
            act.sem_inc(s.yr_taken, CR)
            act.sem_inc(s.ys_out0, 16)
            act.sem_inc(s.ys_out1, 16)

            def high(dst, n):
                q = n % 2
                act.wait_ge([s.piece_in0, s.piece_in1][q], 16 * (n // 2 + 1))
                act.activation(dst, stage[:, q, :], ACT.Copy, scale=SC).then_inc(s.piece_high, 1)

            def zevac(q):
                b, j = q // 2, q % 2
                act.wait_ge(s.z_done, q + 1)
                if q == 0:
                    act.wait_ge(s.prod_taken, 3)
                act.activation(zt[:, j, b * L:(b + 1) * L], ps[:, 4 + q % 4, :], ACT.Identity, bias=zbias[:, j:j + 1]).then_inc(s.z_taken, 1)

            def xntevac(q):
                b, k = q // 2, q % 2
                act.wait_ge(s.xnt_done, q + 1)
                act.copy(xnt[:, k, b * L:(b + 1) * L], ps[:, q % 4, :]).then_inc(s.xnt_taken, 1)

            def sqrt(m):
                act.wait_ge(s.sq_req, m + 1)
                b = m % B
                act.activation(rstd[:, b * TB:(b + 1) * TB, 1], rstd[:, b * TB:(b + 1) * TB, 0], ACT.Sqrt).then_inc(s.sq_done, 1)

            for b in range(B):
                sqrt(b)
                zevac(2 * b)
                zevac(2 * b + 1)
                if b:
                    xntevac(2 * b - 2)
                    xntevac(2 * b - 1)
            xntevac(2 * B - 2)
            xntevac(2 * B - 1)
            act.wait_ge(s.small_in, 80)
            act.activation(gates[:, 2:4], gates[:, 0:2], ACT.Tanh).then_inc(s.gate_done, 1)
            for b in range(B):
                act.wait_ge(s.band_done, b + 1)
                act.copy(gband[:, b, 0:L], ps[:, b, :]).then_inc(s.band_taken, 1)
                act.copy(gband[:, b, L:SKEW], ps[:, b, 0:P]).then_inc(s.band_taken, 1)
            for p in range(2):
                high(ws[:, 0, p * PIECE:(p + 1) * PIECE], p)
            act.wait_ge(s.gsum_done, 1)
            act.copy(tot, ps[32:36, 0, :]).then_inc(s.crow_ready, 1)
            act.wait_ge(s.exp_req, 1)
            act.activation(pen, cm, ACT.Exp, bias=sml[:, 1:2], scale=1.0 / D, accum_out=sml[:, 2:3]).then_inc(s.exp_done, 1)
            for p in range(2, NPIECE):
                high(ws[:, 0, p * PIECE:(p + 1) * PIECE], p)

            def xtevac(n):
                act.wait_ge(s.xt_done, n + 1)
                act.copy(xt[:, :, :, n * P:(n + 1) * P], ps[:, n % 4, :].bitcast(F16)[:, 0:4 * P].rearrange(
                    "p (a k t) -> p a k t", a=2, k=KD)).then_inc(s.xt_taken, 1)

            for b in range(B):
                sqrt(B + b)
                for n in range(b * TB, (b + 1) * TB):
                    act.wait_ge(s.norm_ready, n + 1)
                    act.activation(xh[:, n, 0, :], xn[:, n, :], ACT.Copy, scale=SC).then_inc(s.high_ready, 1)
                for n in range(max(0, b - 1) * TB, b * TB):
                    xtevac(n)
            for n in range(NT - TB, NT):
                xtevac(n)
            act.wait_ge(s.raw_done, 1)
            act.activation(sco.rearrange("p n e -> p (n e)"), ps[:, 4, 0:P], ACT.Sigmoid, scale=1.0 / (SC * SC)).then_inc(s.sig_done, 1)
            act.wait_ge(s.sig_req, 1)
            act.activation(bal, bal, ACT.Sigmoid).then_inc(s.sig_done, 1)
            act.wait_ge(s.sig_req, 2)
            act.activation(wt[:, :, 0], dv, ACT.Sigmoid).then_inc(s.sig_done, 1)
            act.activation(wt[:, :, 1], dv, ACT.Sigmoid, scale=-1.0).then_inc(s.sig_done, 1)

            def gelu(wait_h, wait_f, rb, rf):
                act.wait_ge(s.h_done, wait_h)
                act.wait_ge(s.hs_ready, wait_f)
                act.activation(hf[:, rf, :], ps[:, rb, :], ACT.Gelu, scale=1.0 / (SC * SC)).then_inc(s.g_ready, 1)

            def routed_high(i, n):
                q = n % 2
                act.wait_ge([s.piece_in0, s.piece_in1][q], 16 * (NPIECE // 2 + n // 2 + 1) + i * (16 * BODY // 2))
                if n == BODY - NPIECE:
                    act.wait_ge(s.scatter_out, 16 * 2 * NT)
                w = wr[:, bass.ds(i * (BODY // NPIECE) + n // NPIECE, 1), 0, (n % NPIECE) * PIECE:(n % NPIECE + 1) * PIECE]
                act.activation(w.rearrange("p a c -> p (a c)"), stage[:, q, :], ACT.Copy, scale=SC).then_inc(s.piece_high, 1)

            def shared(ph):
                with act.Fori(0, B // 2) as i:
                    for n in range(BODY):
                        gelu(base[ph] + n + 1 + i * BODY, CR + base[ph] + n + 1 - RF + i * BODY, n % RH, n % RF)
                        if ph == 0:
                            routed_high(i, n)

            shared(0)

            def routed_gelu(i, n):
                gelu(base[1] + n + 1 + i * (RU * RR), CR + base[1] + n + 1 - RF + i * (RU * RR), n % RH, n % RF)

            def columns(i, j):
                act.wait_ge(s.t_done, i * RR + j + 1)
                if j >= RR:
                    act.wait_ge(s.h_done, base[1] + RU * (j - RR + 1) + i * (RU * RR))
                act.copy(xst[:, j % RR].rearrange("p a k c -> p (a k c)"), ps[:, 6, :].bitcast(F16)).then_inc(s.t_taken, 1)

            ysout = [s.ys_out0, s.ys_out1]

            def yevac(i, j):
                act.wait_ge(s.p_done, CR + base[1] + RU * (j + 1) + i * (RU * RR))
                act.wait_ge(ysout[j % RR], 16 * (j // RR + 1) + i * 16)
                act.activation(ysb[:, j % RR].rearrange("p h d -> p (h d)"), ps[:, 4 + j % RR, :], ACT.Copy,
                               scale=1.0 / (SC * SC)).then_inc(s.yr_taken, 1)

            def rbody(i, j):
                for g in range(RU):
                    if j + 1 < TILES:
                        routed_gelu(i, RU * (j + 1) + g)
                    if g == 2 and j + 2 < TILES:
                        columns(i, j + 2)
                yevac(i, j)

            columns(0, 0)
            columns(0, 1)
            for g in range(RU):
                routed_gelu(0, g)
                high(ws[:, 0, g * PIECE:(g + 1) * PIECE], (NE + 1) * NPIECE + g)
            act.wait_ge(s.piece_low, (NE + 2) * NPIECE)
            with act.Fori(0, LOOP) as i:
                for j in range(RR):
                    rbody(i, j)
            for j in range(LOOP * RR, TILES):
                rbody(0, j)
            shared(2)

        @block.vector
        def _(v):
            v.sem_inc(s.hs_ready, CR)
            v.sem_inc(s.p_done, CR)
            v.sem_inc(s.acc_done, CR)
            count = [0]

            def link(ins):
                count[0] += 1
                ins.then_inc(s.chain, 1)
                v.wait_ge(s.chain, count[0])

            v.wait_ge(s.w_in, 16 * 7)
            v.memset(bk4, 1.0).then_inc(s.chain, 1)
            v.tensor_copy(bvb, bvT.rearrange("p (k a) -> p k a", a=1).to_broadcast([P, KD, P])).then_inc(s.chain, 1)
            count[0] = 2
            v.wait_ge(s.chain, 2)
            link(v.tensor_tensor(bk4, bk4, bkT.rearrange("p (k a) -> p k a", a=1).to_broadcast([P, KD, B]), ALU.mult))
            v.tensor_scalar(bk4, bk4, float(L), None, ALU.mult).then_inc(s.csum_done, 1)
            v.wait_ge(s.prod_done, 1)
            v.tensor_copy(wkq.rearrange("p k d -> p (k d)"), ps[:, 0, :]).then_inc(s.prod_taken, 1)
            v.tensor_copy(wvo.rearrange("p k d -> p (k d)"), ps[:, 1, :]).then_inc(s.prod_taken, 1)
            v.wait_ge(s.vec_done, 1)
            v.tensor_copy(vecs[:, 6:10], ps[:, 2, 0:4]).then_inc(s.prod_taken, 1)
            v.wait_ge(s.ubias_done, 1)
            v.tensor_copy(ubias, ps[:, 3, 0:D]).then_inc(s.prod_taken, 1)

            def norm_stats(n):
                v.bn_stats(stats[:, n, :], xres[:, n, :]).then_inc(s.chain, 1)

            def rstds(b, m):
                t = slice(b * TB, (b + 1) * TB)
                v.tensor_scalar(rstd[:, t, 0], mv[:, t, 1], EPS, None, ALU.add).then_inc(s.sq_req, 1)
                v.wait_ge(s.sq_done, m + 1)
                link(v.reciprocal(rstd[:, t, 2], rstd[:, t, 1]))
                link(v.tensor_tensor(rstd[:, t, 3], rstd[:, t, 0], rstd[:, t, 2], ALU.mult))
                link(v.tensor_tensor(rstd[:, t, 3], rstd[:, t, 3], rstd[:, t, 1], ALU.add))
                link(v.tensor_scalar(rstd[:, t, 3], rstd[:, t, 3], 0.5, None, ALU.mult))
                link(v.reciprocal(rstd[:, t, 2], rstd[:, t, 3]))

            xin = [s.x_in0, s.x_in1, s.x_in2, s.x_in3]
            for b in range(B):
                v.wait_ge(xin[b], 16)
                for n in range(b * TB, (b + 1) * TB):
                    norm_stats(n)
                count[0] += TB
                v.wait_ge(s.chain, count[0])
                for n in range(b * TB, (b + 1) * TB):
                    v.bn_aggr(mv[:, n, :], stats[:, n, :]).then_inc(s.chain, 1)
                count[0] += TB
                v.wait_ge(s.chain, count[0])
                rstds(b, b)
                for n in range(b * TB, (b + 1) * TB):
                    v.tensor_scalar(xn[:, n, :], xres[:, n, :], mv[:, n, 0:1], rstd[:, n, 2:3], ALU.subtract, ALU.mult).then_inc(s.xn_ready, 1)
            v.wait_ge(s.ctx_in, 16)
            v.tensor_reduce(csum, ctxt.rearrange("p k (b t) -> p k b t", b=B), AX, ALU.add).then_inc(s.csum_done, 1)
            v.wait_ge(s.small_in, 80)
            v.wait_ge(s.gate_done, 1)
            v.wait_ge(s.xn_ready, NT)
            v.scalar_tensor_tensor(out=xres[:, :, :], in0=bob.rearrange("p (a d) -> p a d", a=1).to_broadcast([P, NT, D]),
                                   scalar=gates[:, 2:3], in1=xres[:, :, :], op0=ALU.mult, op1=ALU.add).then_inc(s.xb_ready, 1)
            v.tensor_scalar(cent[:, 0], centf, SC, None, ALU.mult).then_inc(s.cent_split, 1)
            v.wait_ge(s.cent_split, 1)
            v.scalar_tensor_tensor(out=cent[:, 1], in0=centf, scalar=SC, in1=cent[:, 0], op0=ALU.mult, op1=ALU.subtract).then_inc(s.cent_split, 1)

            def uevac(q):
                v.wait_ge(s.u_done, q + 1)
                if q == 0:
                    v.wait_ge(s.prod_taken, 4)
                v.tensor_tensor(u[:, 2 * q:2 * q + 2, :], ps[:, 4 + q % 4, :].rearrange("p (n d) -> p n d", n=2),
                                ubias.rearrange("p (a d) -> p a d", a=1).to_broadcast([P, 2, D]), ALU.add).then_inc(s.u_taken, 1)

            for q in range(NT // 2):
                uevac(q)

            def low(dst, hi, n):
                q = n % 2
                v.wait_ge([s.piece_in0, s.piece_in1][q], 16 * (n // 2 + 1))
                v.wait_ge(s.piece_high, n + 1)
                v.scalar_tensor_tensor(out=dst, in0=stage[:, q, :], scalar=SC, in1=hi, op0=ALU.mult, op1=ALU.subtract).then_inc(s.piece_low, 1)

            for p in range(2):
                low(ws[:, 1, p * PIECE:(p + 1) * PIECE], ws[:, 0, p * PIECE:(p + 1) * PIECE], p)

            v.wait_ge(s.sbias_done, 1)
            link(v.tensor_copy(sml[:, 0:1], ps[0:B, 1, 0:1]))
            v.wait_ge(s.crow_ready, 1)
            link(v.max(top8, tot))
            link(v.memset(top8[:, LAGS:8], -BIG))
            link(v.match_replace(rep, top8, tot, -BIG))
            link(v.tensor_tensor(pen, tot, rep, ALU.is_gt))
            link(v.tensor_scalar(pen, pen, -1.0, 1e30, ALU.add, ALU.mult))
            link(v.scalar_tensor_tensor(out=cm, in0=ps[0:B, 0, :], scalar=sml[:, 0:1], in1=pen, op0=ALU.add, op1=ALU.add))
            link(v.reduce_max(sml[:, 3:4], cm, AX))
            v.tensor_scalar(sml[:, 1:2], sml[:, 3:4], -1.0 / D, None, ALU.mult).then_inc(s.exp_req, 1)
            v.wait_ge(s.exp_done, 1)
            link(v.reciprocal(sml[:, 3:4], sml[:, 2:3]))
            link(v.tensor_scalar(crow[:, P - 1:SKEW - 1], pen, sml[:, 3:4], None, ALU.mult))
            v.tensor_copy(crow[:, 0:P - 1], crow[:, L:SKEW - 1]).then_inc(s.crow_ready, 1)
            v.wait_ge(s.circ_in, 16)
            for b in range(B):
                a = craw[:, b, :]
                v.tensor_copy(circ[:, b, :], bass.AP(a.tensor, a.offset + L - 1, [a.ap[0], [-1, L]])).then_inc(s.circ_ready, 1)
            for p in range(2, NPIECE):
                low(ws[:, 1, p * PIECE:(p + 1) * PIECE], ws[:, 0, p * PIECE:(p + 1) * PIECE], p)

            v.wait_ge(s.xb_ready, 1)
            for b in range(B):
                for n in range(b * TB, (b + 1) * TB):
                    v.wait_ge(s.mix_done, n - n % 2 + 2)
                    v.scalar_tensor_tensor(out=xres[:, n, :], in0=ps[:, 4 + n // 2 % 4, (n % 2) * D:(n % 2 + 1) * D],
                                           scalar=gates[:, 2:3], in1=xres[:, n, :], op0=ALU.mult, op1=ALU.add).then_inc(s.x2_ready, 1)
                v.wait_ge(s.x2_ready, (b + 1) * TB)
                for n in range(b * TB, (b + 1) * TB):
                    norm_stats(n)
                count[0] += TB
                v.wait_ge(s.chain, count[0])
                for n in range(b * TB, (b + 1) * TB):
                    v.bn_aggr(mv[:, n, :], stats[:, n, :]).then_inc(s.chain, 1)
                count[0] += TB
                v.wait_ge(s.chain, count[0])
                rstds(b, B + b)
                for n in range(b * TB, (b + 1) * TB):
                    v.tensor_scalar(xn[:, n, :], xres[:, n, :], mv[:, n, 0:1], rstd[:, n, 2:3], ALU.subtract, ALU.mult).then_inc(s.norm_ready, 1)
                for n in range(b * TB, (b + 1) * TB):
                    v.wait_ge(s.high_ready, n + 1)
                    v.scalar_tensor_tensor(out=xh[:, n, 1, :], in0=xn[:, n, :], scalar=SC, in1=xh[:, n, 0, :],
                                           op0=ALU.mult, op1=ALU.subtract).then_inc(s.split_ready, 1)
            v.wait_ge(s.norm_ready, NT)
            v.scalar_tensor_tensor(out=xres[:, :, :], in0=xn, scalar=gates[:, 3:4], in1=xres[:, :, :],
                                   op0=ALU.mult, op1=ALU.add).then_inc(s.acc_done, 1)
            link(v.tensor_scalar(gates[:, 0:1], gates[:, 3:4], 1.0 / (SC * SC), None, ALU.mult))

            e16 = lambda a: a.rearrange("p (n e) -> p n e", e=1).to_broadcast([P, NT, NE])
            v.wait_ge(s.const_ready, 5)
            v.wait_ge(s.raw_done, 1)
            v.wait_ge(s.sig_done, 1)
            v.scalar_tensor_tensor(out=bal, in0=ps[:, 4, 0:P].rearrange("p (n e) -> p n e", e=NE), scalar=1.0 / (SC * SC), in1=rbias[:, :].rearrange("p (a e) -> p a e", a=1).to_broadcast([P, NT, NE]),
                                   op0=ALU.mult, op1=ALU.add).then_inc(s.sig_req, 1)
            v.wait_ge(s.const_ready, 5)
            link(v.tensor_reduce(selE, identf.rearrange("p (n e) -> p e n", e=NE), AX, ALU.add))
            link(v.tensor_tensor(trine, tri[:, :].rearrange("p (n e) -> p n e", e=NE),
                                 selE.rearrange("p (a e) -> p a e", a=1).to_broadcast([P, NT, NE]), ALU.mult))
            link(v.tensor_scalar(upper, upper, 0.0, None, ALU.is_gt))
            v.wait_ge(s.sig_done, 2)
            for oh, sc in ((oh1, s1v), (oh2, s2v)):
                link(v.tensor_reduce(m1, bal, AX, ALU.max))
                link(v.tensor_tensor(key, bal, e16(m1), ALU.is_ge))
                link(v.tensor_tensor(key, key, ramp, ALU.mult))
                link(v.tensor_reduce(k1, key, AX, ALU.max))
                link(v.tensor_tensor(oh, key, e16(k1), ALU.is_equal))
                link(v.tensor_tensor(tmp, oh, sco, ALU.mult))
                link(v.tensor_reduce(sc, tmp, AX, ALU.add))
                link(v.scalar_tensor_tensor(out=bal, in0=oh, scalar=-4.0, in1=bal, op0=ALU.mult, op1=ALU.add))
            v.tensor_tensor(dv, s1v, s2v, ALU.subtract).then_inc(s.sig_req, 1)
            v.tensor_tensor(both, oh1, oh2, ALU.add).then_inc(s.disp_req, 1)
            v.wait_ge(s.disp_done, 1)
            link(v.tensor_copy(totc, ps[:, 5, 0:1]))
            v.tensor_scalar(totb, ones, totc, None, ALU.mult).then_inc(s.disp_req, 1)
            v.wait_ge(s.disp_done, 3)
            link(v.tensor_copy(cnt, ps[:, 7, 0:NE]))
            link(v.tensor_tensor(tmp.rearrange("p n e -> p (n e)").rearrange("p (e t) -> p e t", e=NE),
                                 cnt.rearrange("p (e a) -> p e a", a=1).to_broadcast([P, NE, NT]), lag_ramp, ALU.is_gt))
            link(v.tensor_reduce(ntile, tmp.rearrange("p n e -> p (n e)").rearrange("p (e t) -> p e t", e=NE), AX, ALU.add))
            link(v.tensor_tensor(up2, upper, ntile.rearrange("p (a e) -> p a e", a=1).to_broadcast([P, NE, NE]), ALU.mult))
            link(v.tensor_reduce(first, up2, AX, ALU.add))
            link(v.scalar_tensor_tensor(out=pos, in0=first.rearrange("p (a e) -> p a e", a=1).to_broadcast([P, NT, NE]), scalar=float(RT),
                                        in1=ps[:, 6, 0:P].rearrange("p (n e) -> p n e", e=NE), op0=ALU.mult, op1=ALU.add))
            for k, oh in enumerate((oh1, oh2)):
                link(v.tensor_tensor(tmp, oh, pos, ALU.mult))
                link(v.tensor_reduce(k1, tmp, AX, ALU.add))
                v.tensor_copy(slots[:, :, k], k1).then_inc(s.slots_ready, 1)
                v.wait_ge(s.slots_ready, k + 1)
            v.wait_ge(s.sig_done, 4)
            v.tensor_scalar(wt[:, :, 2:4], wt[:, :, 0:2], gates[:, 3:4], None, ALU.mult).then_inc(s.disp_req, 1)
            link(v.tensor_tensor(jcmp, jramp.rearrange("p (j a) -> p j a", a=1).to_broadcast([1, ETAB, NE]),
                                 first[0:1].rearrange("p (a e) -> p a e", a=1).to_broadcast([1, ETAB, NE]), ALU.is_ge))
            link(v.tensor_reduce(ej, jcmp, AX, ALU.add))
            v.tensor_scalar(etab[:, :], ej, -1.0, None, ALU.add).then_inc(s.table_ready, 1)

            def split(g0, i, step, n, rs, p0):
                v.wait_ge(s.g_ready, CR + g0 + n + 1 + i * step)
                v.wait_ge(s.p_done, CR + p0 + i * step)
                v.tensor_scalar(hs[:, rs, 0, :], hf[:, n % RF, :], SC, None, ALU.mult).then_inc(s.hi_done, 1)
                v.wait_ge(s.hi_done, g0 + n + 1 + i * step)
                v.scalar_tensor_tensor(out=hs[:, rs, 1, :], in0=hf[:, n % RF, :], scalar=SC, in1=hs[:, rs, 0, :],
                                       op0=ALU.mult, op1=ALU.subtract).then_inc(s.hs_ready, 1)

            def accumulate(ph, i, at, **k):
                start, step = ((ACC0, 4), None, (ACC2, STEP2))[ph]
                v.wait_ge(s.acc_done, start + at + i * step)
                v.scalar_tensor_tensor(**k, op0=ALU.mult, op1=ALU.add).then_inc(s.acc_done, 1)

            def add_block(ph, i, blk):
                v.wait_ge(s.p_done, CR + base[ph] + KF * (blk + 1) + i * BODY)
                for h in range(2):
                    o = xres[:, bass.ds(i * (2 * TB) + blk * TB + 2 * h, 2), :].rearrange("p n d -> p (n d)")
                    at = h + (2 * blk if ph == 0 else (KF + 2 if blk == 0 else BODY + 2))
                    accumulate(ph, i, at, out=o, in0=ps[:, RH + 2 * blk + h, :], scalar=gates[:, 0:1], in1=o)

            def routed_low(i, n):
                q = n % 2
                v.wait_ge(s.piece_high, NPIECE + n + 1 + i * BODY)
                w = wr[:, bass.ds(i * (BODY // NPIECE) + n // NPIECE, 1), :, (n % NPIECE) * PIECE:(n % NPIECE + 1) * PIECE]
                w = w.rearrange("p e a c -> p (e a) c")
                v.scalar_tensor_tensor(out=w[:, 1, :], in0=stage[:, q, :], scalar=SC, in1=w[:, 0, :],
                                       op0=ALU.mult, op1=ALU.subtract).then_inc(s.piece_low, 1)

            gin = [s.gather_in0, s.gather_in1, s.gather_in2, s.gather_in3,
                   s.gather_in4, s.gather_in5, s.gather_in6, s.gather_in7]

            def combine(i, n):
                m = n % 8
                v.wait_ge(gin[m], 16 * (n // 8 + 1) + i * (16 * BODY // 8))
                o = xres[:, bass.ds(i * (BODY // 2) + n // 2, 1), :].rearrange("p n d -> p (n d)")
                w = wt[:, bass.ds(i * (BODY // 2) + n // 2, 1), 2 + n % 2]
                accumulate(2, i, pos_of(n), out=o, in0=gat[:, m, :], scalar=w, in1=o)

            def shared(ph):
                with v.Fori(0, B // 2) as i:
                    for n in range(BODY):
                        split(base[ph], i, BODY, n, n % RH, base[ph] + n + 1 - RH)
                        if n == KF + 2:
                            add_block(ph, i, 0)
                        if ph == 0:
                            routed_low(i, n)
                        else:
                            combine(i, n)
                    add_block(ph, i, 1)

            v.wait_ge(s.disp_req, 3)
            shared(0)

            def routed_split(i, n):
                split(base[1], i, RU * RR, n, n % RH, base[1] + n + 1 - RH)

            for g in range(RU):
                routed_split(0, g)
                low(ws[:, 1, g * PIECE:(g + 1) * PIECE], ws[:, 0, g * PIECE:(g + 1) * PIECE], (NE + 1) * NPIECE + g)
            with v.Fori(0, LOOP) as i:
                for n in range(RU * RR):
                    routed_split(i, n + RU)
            for n in range((LOOP * RR + 1) * RU, TILES * RU):
                routed_split(0, n)
            shared(2)


def kernel(x, ctx_1024, g_xattn, g_ffn, L0_xattn_Wq, L0_xattn_bq, L0_xattn_Wk, L0_xattn_bk, L0_xattn_Wv, L0_xattn_bv,
           L0_xattn_Wo, L0_xattn_bo, L0_ffn_centroids, L0_ffn_routing_bias, L0_ffn_Wfc_r, L0_ffn_Wproj_r,
           L0_ffn_Wfc_sh, L0_ffn_Wproj_sh):
    import numpy as np
    import concourse.bacc as bacc
    from concourse.bass_utils import run_bass_kernel_spmd

    c = np.ascontiguousarray
    wfc = np.concatenate([np.asarray(L0_ffn_Wfc_sh)[:1], np.asarray(L0_ffn_Wfc_r), np.asarray(L0_ffn_Wfc_sh)[1:]])
    wpr = np.concatenate([np.asarray(L0_ffn_Wproj_sh)[:1], np.asarray(L0_ffn_Wproj_r), np.asarray(L0_ffn_Wproj_sh)[1:]])
    n = NE + NS
    wfc = wfc.transpose(0, 2, 1).reshape(n, KD, P, F)
    wpr = wpr.transpose(0, 2, 1).reshape(n, 2, KF // 2, P, D).transpose(0, 1, 3, 2, 4).reshape(n, 2, P, KF // 2 * D)
    arrays = {
        "x": c(np.asarray(x).reshape(T, D)), "ctxT": c(np.asarray(ctx_1024).reshape(T, D).T),
        "Wq": c(L0_xattn_Wq), "Wk": c(L0_xattn_Wk), "Wv": c(L0_xattn_Wv), "WoT": c(np.asarray(L0_xattn_Wo).T),
        "bq": c(L0_xattn_bq), "bk": c(L0_xattn_bk), "bv": c(L0_xattn_bv), "bo": c(L0_xattn_bo),
        "gx": c(g_xattn), "gf": c(g_ffn), "centT": c(np.asarray(L0_ffn_centroids).T), "rb": c(L0_ffn_routing_bias),
        "W": c(np.concatenate([wfc, wpr], axis=1).reshape(n * NPIECE, P, PIECE)),
    }
    nc = bacc.Bacc("TRN2", target_bir_lowering=False, num_devices=1)
    A = {k: nc.dram_tensor("in_" + k, a.shape, mybir.dt.from_np(a.dtype), kind="ExternalInput").ap() for k, a in arrays.items()}
    A["out"] = nc.dram_tensor("out_y", (T, D), F32, kind="ExternalOutput").ap()
    build_kernel(nc, A)
    r = run_bass_kernel_spmd(nc, [{"in_" + k: a for k, a in arrays.items()}], core_ids=[0])
    return np.asarray(r.results[0]["out_y"]).reshape(B, L, D)
```

```python
from contextlib import ExitStack

import concourse.bass as bass
from concourse import mybir

F32 = mybir.dt.float32
F16 = mybir.dt.float16
I32 = mybir.dt.int32
U32 = mybir.dt.uint32
ALU = mybir.AluOpType
ACT = mybir.ActivationFunctionType
AX = mybir.AxisListType.X

P = 128
B, L, D = 4, 512, 256
T = B * L
NT = T // P
TB = L // P
KD = D // P
NE, NS, F = 8, 2, 1024
KF = F // P
LAGS = 6
SKEW = L + P
CHUNKS = (2 * T - NE) // P + NE
NARROW = NE - 1
WIDE = (CHUNKS - NARROW) // 2
TILES = WIDE + NARROW
RT = 2 * P
HT = RT // P
SLOTS = CHUNKS * P
assert SLOTS == WIDE * RT + NARROW * P
UNIT = 512
PIECE = 512
NPIECE = 2 * KD * F // PIECE
WID = 2 * KD * F
SC = 16.0
EPS = 1e-5
RP = 4
PRE = 8
PIECES = [1, 1, 1, 1, 1, 0, 0, 0] + [2] * (B - 2) * KF + [1, 3, 3, 3, 2, 2, 2, 0]
BIG = 3.0e38
RH, RF = 4, 2
RR = 2
RU = 4
CR = 4
AHEAD = 3


def build_kernel(nc, A):
    with ExitStack() as ctx:
        def sb(name, shape, dt=F32):
            return ctx.enter_context(nc.sbuf_tensor(name, shape, dt))

        def sem(name):
            return ctx.enter_context(nc.semaphore(name))

        wr = sb("wr", [P, NE, 2, WID], F16)
        ws = sb("ws", [P, 2, WID], F16)
        xres = sb("xres", [P, NT, D])
        xt = sb("xt", [P, 2, KD, T], F16)
        stage = sb("stage", [P, RP, PIECE])
        hf = sb("hf", [P, RF, UNIT])
        hs = sb("hs", [P, RH, 2, UNIT], F16)
        rt = sb("rt", [P, 9 * 512], F16)
        tri = sb("tri", [P, P])
        identh = sb("identh", [P, P], F16)
        stats = sb("stats", [P, NT, 6])
        mv = sb("mv", [P, NT, 2])
        rstd = sb("rstd", [P, NT, 4])
        gates = sb("gates", [P, 10])
        cent = sb("cent", [P, 2, KD, NE], F16)
        rbias = sb("rbias", [P, NE])
        slots = sb("slots", [P, NT, 2], U32)
        wt = sb("wt", [P, NT, 4])
        etab = sb("etab", [1, TILES], I32)

        def region(e):
            return wr[:, e, :, :].rearrange("p a b -> p (a b)").bitcast(F32)

        ctxt = region(2).rearrange("p (k t) -> p k t", k=KD)
        xnt = region(1)[:, 0:2 * KD * 6 * P].rearrange("p (r k j) -> p r k j", r=2, k=KD)
        zt = region(0).rearrange("p (k t) -> p k t", k=KD)
        u = region(3).rearrange("p (n d) -> p n d", n=NT)
        xn = region(4).rearrange("p (n d) -> p n d", n=NT)
        r5, r6 = region(5), region(6)
        gband = r5[:, 0:B * SKEW].rearrange("p (b j) -> p b j", b=B)
        wkq = r5[:, B * SKEW:B * SKEW + KD * D].rearrange("p (k d) -> p k d", k=KD)
        wvo = r5[:, B * SKEW + KD * D:B * SKEW + 2 * KD * D].rearrange("p (k d) -> p k d", k=KD)
        small5 = B * SKEW + 2 * KD * D
        csum = r5[:, small5:small5 + KD * B].rearrange("p (k b) -> p k b", k=KD)
        bvb = r5[:, small5 + 8:small5 + 8 + KD * P].rearrange("p (k m) -> p k m", k=KD)
        craw = r6[:, 0:B * L].rearrange("p (b j) -> p b j", b=B)
        circ = r5[:, 0:B * SKEW].rearrange("p (b j) -> p b j", b=B)
        o6 = B * L
        ubias = r6[:, o6:o6 + D]
        bob = r6[:, o6 + D:o6 + 2 * D]
        identf = r6[:, o6 + 2 * D:o6 + 2 * D + P]
        sel = r6[:, o6 + 2 * D + P:o6 + 2 * D + P + B * 36].rearrange("p (b m) -> p b m", b=B)
        o7 = o6 + 2 * D + P + B * 36
        vecs = r6[:, o7:o7 + 32]
        bkT, bqT, bvT = vecs[:, 0:2], vecs[:, 2:4], vecs[:, 4:6]
        zbias, v1 = vecs[:, 6:8], vecs[:, 8:10]
        bk4 = vecs[:, 10:18].rearrange("p (k b) -> p k b", k=KD)
        sbp = vecs[:, 18:26].rearrange("p (k b) -> p k b", k=KD)
        centf = r6[:, o7 + 32:o7 + 32 + KD * NE].rearrange("p (k e) -> p k e", k=KD)
        gsk = r6[:, 0:B * L].rearrange("p (b j) -> p b j", b=B)
        xh = wr[:, NE - 1, :, :].rearrange("p a b -> p (a b)").rearrange("p (n s d) -> p n s d", n=NT, s=2)
        xtf = xt[:, :, :, :].rearrange("p a k t -> p (a k t)").bitcast(F32)
        wsrc = xtf[:, 0:4 * KD * D].rearrange("p (w k d) -> p w k d", w=4, k=KD)
        wq, wk, wv, wo = (wsrc[:, i] for i in range(4))
        rows = xtf[0:B, 4 * KD * D:4 * KD * D + 2048].rearrange("p (a j) -> p a j", j=512)
        tot, rep, pen, cm = (rows[:, i] for i in range(4))
        crow = hf[0:B, :, :].rearrange("p a b -> p (a b)")[:, 0:SKEW]
        sml = gates[0:B, 4:8]
        top8 = rstd[0:B, 0:2, :].rearrange("p a b -> p (a b)")

        rtf = rt[:, :].bitcast(F32)
        dsp = rtf[:, 0:14 * P].rearrange("p (a n e) -> p a n e", a=14, e=NE)
        bal, sco, key, oh1, oh2, both, pos, trine, tmp, npos, ramp = (dsp[:, i] for i in range(11))
        totb = rtf[:, 11 * P:12 * P]
        ones = rtf[:, 12 * P:13 * P]
        m13 = rtf[:, 13 * P:14 * P]
        lag_ramp = rtf[:, 14 * P:15 * P].rearrange("p (e t) -> p e t", e=NE)
        selE = m13[:, 0:8]
        cnt = m13[:, 8:16]
        ntile = m13[:, 16:24]
        first = m13[:, 24:32]
        totc = m13[:, 32:33]
        schunks = m13[:, 33:34]
        wend = m13[:, 40:48]
        chunks, odd = m13[:, 112:120], m13[:, 120:128]
        tiny = rtf[:, 17 * P + 80:17 * P + 112]
        nfirst, narrow_shift, sslots = tiny[:, 0:8], tiny[:, 8:16], tiny[:, 16:17]
        m1 = m13[:, 48:64]
        k1 = m13[:, 64:80]
        s1v = m13[:, 80:96]
        s2v = m13[:, 96:112]
        dv = rtf[:, 17 * P + 64:17 * P + 80]
        zero = rt[:, 0:1024]
        upper = rtf[:, 15 * P:15 * P + 64].rearrange("p (e f) -> p e f", e=NE)
        up2 = rtf[:, 15 * P + 64:16 * P].rearrange("p (e f) -> p e f", e=NE)
        jramp = rtf[0:1, 16 * P:16 * P + TILES]
        jcmp = rtf[0:1, 0:TILES * NE].rearrange("p (j e) -> p j e", e=NE)
        ej = rtf[0:1, 17 * P:17 * P + TILES]
        xs = rt[:, 0:RR * HT * 2 * D].rearrange("p (r h c) -> p r h c", r=RR, h=HT)
        xst = rt[:, RR * HT * 2 * D:2 * RR * HT * 2 * D].rearrange("p (r a k c) -> p r a k c", r=RR, a=2, k=KD)
        ysb = stage[:, :, :].rearrange("p a c -> p (a c)")[:, 0:RR * HT * D].rearrange("p (r h d) -> p r h d", r=RR, h=HT)
        gat = rtf[:, 0:8 * D].rearrange("p (r d) -> p r d", r=8)

        ps = ctx.enter_context(nc.psum_tensor("ps", [P, 8, 512], F32))

        band_d = nc.dram_tensor("band_d", [P, B, SKEW], F32).ap()
        crow_d = nc.dram_tensor("crow_d", [B, SKEW], F32).ap()
        xslot_d = nc.dram_tensor("xslot_d", [SLOTS, 2 * D], F16).ap()
        yslot_d = nc.dram_tensor("yslot_d", [SLOTS, D], F32).ap()

        names = ("x_in0 x_in1 x_in2 x_in3 w_in w2_in b_in ctx_in0 ctx_in1 ctx_in2 ctx_in3 bvb_ready split_last norm_last small_in const_ready prod_done vec_done ubias_done prod_taken "
                 "z_done z_taken xn_ready xnt_done xnt_taken band_done band_taken u_done u_taken csum_done "
                 "band_out0 band_out1 band_out2 band_out3 skew_in0 skew_in1 skew_in2 skew_in3 gsum_done chain crow_ready crow_out circ_ready mix_done x2_ready "
                 "sb_ready circ_in0 circ_in1 circ_in2 circ_in3 gb_ready sq_req norm_req z_half xnt_half band_half u_half xnt_more sq_done exp_req exp_done hi_done gate_done norm_ready high_ready split_ready xt_done xt_taken raw_done sig_req "
                 "sig_done disp_req disp_done slots_ready table_ready zero_set zero_out scatter_out "
                 "piece_in0 piece_in1 piece_in2 piece_in3 piece_high piece_low "
                 "h_done g_ready hs_ready p_done cent_split "
                 "xs_first0 xs_first1 xs_in0 xs_in1 t_done t_taken yr_taken ys_out0 ys_out1 "
                 "gather_in0 gather_in1 gather_in2 gather_in3 gather_in4 gather_in5 gather_in6 gather_in7 "
                 "out_done xb_ready wt_ready scaled base_done acc_done")
        S = {n: sem(n) for n in names.split()}
        s = type("Sems", (), S)

        piece_in = [s.piece_in0, s.piece_in1, s.piece_in2, s.piece_in3]
        band_out = [s.band_out0, s.band_out1, s.band_out2, s.band_out3]
        ctx_in = [s.ctx_in0, s.ctx_in1, s.ctx_in2, s.ctx_in3]
        circ_in = [s.circ_in0, s.circ_in1, s.circ_in2, s.circ_in3]
        skew_in = [s.skew_in0, s.skew_in1, s.skew_in2, s.skew_in3]

        block = ctx.enter_context(nc.Block())

        def pieces_of(n):
            return range(PRE + AHEAD + sum(PIECES[:n]), PRE + AHEAD + sum(PIECES[:n + 1]))

        def wtile(w, part, k, f0, n):
            return w[:, part, k * F + f0:k * F + f0 + n]

        def vtile(w, part, f):
            return w[:, part, KD * F + f * D:KD * F + (f + 1) * D]

        SH_UNITS = B * KF
        RT_UNITS = RU * TILES
        base = [0, SH_UNITS, SH_UNITS + RT_UNITS]
        MORE = B - 2
        STEP0, STEP2 = 2, 2 * TB + 2
        ACC0 = CR
        ACC2 = ACC0 + STEP0 * B

        FIRST = [B * KF - 4, B * KF - 3]
        LOOPW, LOOPN = (WIDE - RR - 1) // RR, (NARROW - RR - 1) // RR

        def routed_tiles(eng, body):
            with eng.Fori(0, LOOPW) as i:
                for j in range(RR):
                    body(i, j, j % RR > 0)
            for j in range(LOOPW * RR, WIDE):
                body(0, j, j > LOOPW * RR)
            with eng.Fori(0, LOOPN) as i:
                for j in range(WIDE, WIDE + RR):
                    body(i, j, j % RR > 0)
            for j in range(WIDE + LOOPN * RR, TILES):
                body(0, j, j > WIDE + LOOPN * RR)

        def width(j):
            return RT if j < WIDE else P

        def row_of(j):
            return j * RT if j < WIDE else WIDE * RT + (j - WIDE) * P

        @block.sync
        def _(sp):
            xin = [s.x_in0, s.x_in1, s.x_in2, s.x_in3]
            xr = A["x"].rearrange("(n p) d -> p n d", p=P)
            def weight(j, name, done):
                sp.dma_start(wsrc[:, j], A[name].rearrange("(k p) d -> p k d", p=P)).then_inc(done, 16)

            weight(1, "Wk", s.w_in)
            weight(0, "Wq", s.w_in)
            for b in range(B):
                cr = A["ctxT"].rearrange("(k p) t -> p k t", p=P)
                sp.dma_start(ctxt[:, :, b * L:(b + 1) * L], cr[:, :, b * L:(b + 1) * L]).then_inc(ctx_in[b], 16)
                sp.dma_start(xres[:, b * TB:(b + 1) * TB, :], xr[:, b * TB:(b + 1) * TB, :]).then_inc(xin[b], 16)
                if b == 0:
                    weight(2, "Wv", s.w2_in)
                    weight(3, "WoT", s.w2_in)

            def piece(p):
                if p >= RP:
                    sp.wait_ge(s.piece_low, p - RP + 1)
                sp.dma_start(stage[:, p % RP, :], A["W"][p]).then_inc(piece_in[p % RP], 16)

            for p in range(RP):
                piece(p)
            for b in range(B):
                sp.wait_ge(s.band_taken, 3 * (b + 1))
                sp.dma_start(band_d[:, b, :], gband[:, b, :]).then_inc(band_out[b], 16)
                sp.wait_ge(band_out[b], 16)
                skew = bass.AP(band_d.tensor, band_d.offset + b * SKEW, [[B * SKEW + 1, P], [1, L]])
                sp.dma_start(gsk[:, b, :], skew).then_inc(skew_in[b], 16)
            for p in range(RP, NPIECE):
                piece(p)
            sp.wait_ge(s.crow_ready, 2)
            sp.dma_start(crow_d[:, 0:SKEW - 1], crow[:, 0:SKEW - 1]).then_inc(s.crow_out, 16)
            sp.wait_ge(s.crow_out, 16)
            for b in range(B):
                cskew = bass.AP(crow_d.tensor, crow_d.offset + b * SKEW, [[1, P], [1, L]])
                sp.dma_start(craw[:, b, :], cskew).then_inc(circ_in[b], 16)
            sp.wait_ge(s.zero_set, 1)
            zsrc = bass.AP(zero.tensor, zero.offset, [zero.ap[0], [0, SLOTS // P], [1, 2 * D]])
            sp.dma_start(xslot_d.rearrange("(t p) c -> p t c", p=P), zsrc).then_inc(s.zero_out, 16)
            with sp.Fori(0, NE * NPIECE // RP) as i:
                for q in range(RP):
                    sp.wait_ge(s.piece_low, NPIECE - RP + 1 + q + i * RP)
                    e = i * RP + (NPIECE + q)
                    sp.dma_start(stage[:, q, :], A["W"][bass.ds(e, 1)].rearrange("a p c -> (a p) c")).then_inc(
                        piece_in[q], 16)
            xsin = [s.xs_in0, s.xs_in1]
            ysout = [s.ys_out0, s.ys_out1]
            for p in range((NE + 1) * NPIECE, (NE + 2) * NPIECE):
                piece(p)

            def load(i, j):
                sp.wait_ge(s.t_done, i * RR + j - RR + 1)
                w = width(j)
                rows_ = xslot_d[bass.ds(i * (RR * w) + row_of(j), w), :]
                sp.dma_start(xs[:, j % RR, 0:w // P], rows_.rearrange("(h p) c -> p h c", p=P)).then_inc(xsin[j % RR], 16)

            def store(i, j):
                sp.wait_ge(s.yr_taken, i * RR + j + 1 + CR)
                w = width(j)
                rows_ = yslot_d[bass.ds(i * (RR * w) + row_of(j), w), :]
                sp.dma_start(rows_.rearrange("(h p) d -> p h d", p=P), ysb[:, j % RR, 0:w // P]).then_inc(ysout[j % RR], 16)
            load(0, RR)

            def sbody(i, j, follows):
                if j + RR + 1 < TILES:
                    load(i, j + RR + 1)
                store(i, j)
            routed_tiles(sp, sbody)
            for b in range(B):
                sp.wait_ge(s.acc_done, ACC2 + (b + 1) * STEP2)
                o = A["out"].rearrange("(n p) d -> p n d", p=P)
                sp.dma_start(o[:, b * TB:(b + 1) * TB, :], xres[:, b * TB:(b + 1) * TB, :]).then_inc(s.out_done, 16)
            sp.wait_ge(s.out_done, 16 * B)

        @block.gpsimd
        def _(pool):
            pool.memset(zero, 0.0).then_inc(s.zero_set, 1)
            pool.memset(identf, 0.0)
            pool.memset(tri[:, :], 1.0)
            pool.memset(sel, 0.0).then_inc(s.const_ready, 1)
            pool.wait_ge(s.const_ready, 1)
            for b in range(B):
                pool.memset(sel[:, b, b:b + 1], 1.0)
            pool.memset(sel[:, :, 32:36], 1.0)
            pool.affine_select(out=identf, in_=identf, compare_op=ALU.not_equal, fill=1.0, base=0,
                               pattern=[[-1, P]], channel_multiplier=1).then_inc(s.const_ready, 1)
            pool.affine_select(out=tri[:, :], in_=tri[:, :], compare_op=ALU.is_gt, fill=0.0, base=0,
                               pattern=[[1, P]], channel_multiplier=-1).then_inc(s.const_ready, 1)
            pool.wait_ge(s.const_ready, 3)
            pool.tensor_copy(identh[:, :], identf).then_inc(s.const_ready, 1)
            pool.iota(lag_ramp, [[0, NE], [P, NT]], base=0, channel_multiplier=0, allow_small_or_imprecise_dtypes=True)
            pool.iota(jramp, [[1, TILES]], base=0, channel_multiplier=0, allow_small_or_imprecise_dtypes=True)
            pool.iota(ramp, [[0, NT], [-1, NE]], base=NE, channel_multiplier=0, allow_small_or_imprecise_dtypes=True)
            pool.iota(upper, [[1, NE], [-1, NE]], base=0, channel_multiplier=0, allow_small_or_imprecise_dtypes=True)
            pool.memset(ones, 1.0).then_inc(s.const_ready, 1)
            pool.wait_ge(s.gb_ready, 1)
            for b in range(B):
                pool.wait_ge(s.xn_ready, (b + 1) * TB)
                tb = slice(b * TB, (b + 1) * TB)
                pool.tensor_tensor(xres[:, tb, :], xres[:, tb, :], bob.rearrange("p (a d) -> p a d", a=1).to_broadcast([P, TB, D]),
                                   ALU.add).then_inc(s.xb_ready, 1)
            def lows(b):
                for n in range(b * TB, (b + 1) * TB, 2):
                    pool.wait_ge(s.high_ready, n + 2)
                    pool.tensor_tensor(xh[:, n:n + 2, 1, :], xn[:, n:n + 2, :], xh[:, n:n + 2, 0, :], ALU.subtract).then_inc(s.split_ready, 2)

            def residual(b):
                if b < B - 1:
                    pool.wait_ge(s.split_ready, (b + 1) * TB)
                else:
                    pool.wait_ge(s.split_last, TB)
                tb = slice(b * TB, (b + 1) * TB)
                pool.tensor_scalar(xn[:, tb, :], xn[:, tb, :], gates[:, 3:4], 1.0 / SC, ALU.mult, ALU.mult).then_inc(s.scaled, 1)
                pool.wait_ge(s.scaled, b + 1)
                pool.tensor_tensor(xres[:, tb, :], xres[:, tb, :], xn[:, tb, :], ALU.add).then_inc(s.base_done, 1)

            lows(0)
            for b in range(B):
                if 1 <= b + 1 < B - 1:
                    lows(b + 1)
                residual(b)
            pool.wait_ge(s.slots_ready, 2)
            pool.wait_ge(s.zero_out, 16)
            pool.wait_ge(s.split_last, TB)
            pool.wait_ge(s.split_ready, NT - TB)
            for n in range(NT):
                for k in range(2):
                    pool.indirect_dma_start(xslot_d, bass.IndirectOffsetOnAxis(slots[:, n, k:k + 1], 0),
                                            xh[:, n].rearrange("p s d -> p (s d)"), None).then_inc(s.scatter_out, 16)
            pool.wait_ge(s.scatter_out, 16 * 2 * NT)
            pool.wait_ge(s.table_ready, 1)
            for j, x_in in enumerate((s.xs_first0, s.xs_first1)):
                pool.dma_start(xs[:, j], xslot_d[j * RT:(j + 1) * RT, :].rearrange("(h p) c -> p h c", p=P)).then_inc(x_in, 16)
            for q, so in enumerate((s.ys_out0, s.ys_out1)):
                pool.wait_ge(so, 16 * (len(range(q, TILES, RR)) + 1))
            gin = [s.gather_in0, s.gather_in1, s.gather_in2, s.gather_in3,
                   s.gather_in4, s.gather_in5, s.gather_in6, s.gather_in7]
            for n in range(NT):
                for k in range(2):
                    m = 2 * n + k
                    if m >= 8:
                        pool.wait_ge(s.acc_done, ACC2 + (m - 8) // KF * STEP2 + (m - 8) % KF + 1)
                    pool.indirect_dma_start(gat[:, m % 8], None, yslot_d,
                                            bass.IndirectOffsetOnAxis(slots[:, n, k:k + 1], 0)).then_inc(gin[m % 8], 16)

        @block.tensor
        def _(pe):
            mm = pe.matmul
            pe.wait_ge(s.w_in, 16 * 2)
            for c in range(KD):
                for o in range(KD):
                    last = mm(ps[:, 0, c * D:(c + 1) * D], wk[:, o, c * P:(c + 1) * P], wq[:, o, :], start=(o == 0), stop=(o == KD - 1))
            last.then_inc(s.prod_done, 1)
            pe.wait_ge(s.b_in, 16 * 3)
            for c in range(KD):
                for o in range(KD):
                    mm(ps[:, 2, c:c + 1], wq[:, o, c * P:(c + 1) * P], bkT[:, o:o + 1], start=(o == 0), stop=(o == KD - 1))
            for c in range(KD):
                for o in range(KD):
                    last = mm(ps[:, 2, 2 + c:3 + c], wk[:, o, c * P:(c + 1) * P], bqT[:, o:o + 1], start=(o == 0), stop=(o == KD - 1))
            last.then_inc(s.vec_done, 1)

            def outproducts():
                pe.wait_ge(s.w2_in, 16 * 2)
                for c in range(KD):
                    for o in range(KD):
                        last = mm(ps[:, 6, c * D:(c + 1) * D], wv[:, o, c * P:(c + 1) * P], wo[:, o, :], start=(o == 0), stop=(o == KD - 1))
                last.then_inc(s.prod_done, 1)
                pe.wait_ge(s.bvb_ready, 1)
                for o in range(KD):
                    last = mm(ps[:, 7, 0:D], bvb[:, o, :], wo[:, o, :], start=(o == 0), stop=(o == KD - 1))
                last.then_inc(s.ubias_done, 1)

            pe.wait_ge(s.prod_taken, 1)
            def zjob(q):
                b, j = q // 2, q % 2
                if j == 0:
                    pe.wait_ge(ctx_in[b], 16)
                if q >= 2:
                    pe.wait_ge(s.z_taken, 2 * (q - 1))
                for c in range(KD):
                    last = mm(ps[:, 4 + q % 2, :], wkq[:, c, j * P:(j + 1) * P], ctxt[:, c, b * L:(b + 1) * L], start=(c == 0), stop=(c == KD - 1))
                last.then_inc(s.z_done, 1)
            pe.wait_ge(s.const_ready, 2)

            def xntjob(q):
                b, k = q // 2, q % 2
                pe.wait_ge(s.xn_ready, (b + 1) * TB)
                if q >= 2:
                    pe.wait_ge(s.xnt_taken, 2 * (q - 1))
                for n in range(TB):
                    last = pe.transpose(ps[:, q % 2, n * P:(n + 1) * P], xn[:, b * TB + n, k * P:(k + 1) * P], identf)
                last.then_inc(s.xnt_done, 1)

            def bandjob(b):
                pe.wait_ge(s.z_taken, 4 * (b + 1))
                pe.wait_ge(s.xnt_taken, 4 * (b + 1))
                pe.wait_ge(s.xnt_more, 4 * (b + 1))
                if b < 2:
                    pe.wait_ge(s.prod_taken, 4)
                else:
                    pe.wait_ge(s.band_taken, 3 * (b - 1))
                for h in range(2):
                    for m in range(2):
                        for c in range(KD):
                            last = mm(ps[:, 2 + b % 2, h * 2 * P:(h + 1) * 2 * P], zt[:, c, b * L + (2 * h + m) * P:b * L + (2 * h + m + 1) * P],
                                      xnt[:, b % 2, c, (3 * h + m) * P:(3 * h + m + 2) * P],
                                      start=(m == 0 and c == 0), stop=(m == 1 and c == KD - 1))
                last.then_inc(s.band_done, 1)

            def ujob(q):
                if q < 4:
                    pe.wait_ge(s.z_taken, 4 * B)
                else:
                    pe.wait_ge(s.u_taken, 2 * (q // 2 - 1))
                for h in range(2):
                    for c in range(KD):
                        n = 2 * q + h
                        last = mm(ps[:, 4 + q % 4, h * D:(h + 1) * D], ctxt[:, c, n * P:(n + 1) * P], wvo[:, c, :],
                                  start=(c == 0), stop=(c == KD - 1))
                last.then_inc(s.u_done, 1)

            for b in range(B):
                zjob(2 * b)
                zjob(2 * b + 1)
                if b == 0:
                    outproducts()
                xntjob(2 * b)
                xntjob(2 * b + 1)
                if b:
                    bandjob(b - 1)
            bandjob(B - 1)
            ujob(0)
            ujob(1)
            pe.wait_ge(s.xnt_taken, 4 * B)
            for b in range(B):
                pe.wait_ge(skew_in[b], 16)
                last = mm(ps[0:36, 0, :], sel[:, b, :], gsk[:, b, :], start=(b == 0), stop=(b == B - 1), skip_group_check=True)
                if b == 0:
                    pe.wait_ge(s.sb_ready, 1)
                    mm(ps[0:B, 0, :], sbp[:, 0, :], sel[:, 0, 32:33].to_broadcast([P, L]), start=False, stop=False, skip_group_check=True)
            last.then_inc(s.gsum_done, 1)
            for q in range(2, NT // 2):
                ujob(q)
            def mixjob(b):
                pe.wait_ge(s.circ_ready, 3 * (b + 1))
                if b < 2:
                    pe.wait_ge(s.u_taken, 2 * B)
                else:
                    pe.wait_ge(s.x2_ready, TB * (b - 1))
                for h in range(2):
                    u01, u0, u1 = (u[:, b * TB + 2 * h + m:b * TB + 2 * h + e, :] for m, e in ((0, 2), (0, 1), (1, 2)))
                    bank = 4 + 2 * (b % 2) + h
                    c1, c0 = (circ[:, b, (2 * h + j) * P:(2 * h + j + 1) * P] for j in range(2))
                    c1n = circ[:, b, 4 * P:5 * P] if h else c1
                    mm(ps[:, bank, :], c0, u01.rearrange("p n d -> p (n d)"), start=True, stop=False, skip_group_check=True)
                    mm(ps[:, bank, 0:D], c1, u1.rearrange("p n d -> p (n d)"), start=False, stop=False, skip_group_check=True)
                    mm(ps[:, bank, D:2 * D], c1n, u0.rearrange("p n d -> p (n d)"), start=False, stop=True,
                       skip_group_check=True).then_inc(s.mix_done, 1)
            pe.wait_ge(s.const_ready, 4)

            def xtjob(n):
                if n < NT - TB:
                    pe.wait_ge(s.split_ready, n // 2 * 2 + 2)
                else:
                    pe.wait_ge(s.split_last, n // 2 * 2 + 2 - (NT - TB))
                pe.wait_ge(s.high_ready, n // 2 * 2 + 2)
                if n < 4:
                    pe.wait_ge(s.crow_ready, 2)
                else:
                    pe.wait_ge(s.xt_taken, n - 3)
                tb = ps[:, n % 4, :].bitcast(F16)
                for a in range(2):
                    for k in range(KD):
                        last = pe.transpose(tb[:, (a * KD + k) * P:(a * KD + k + 1) * P], xh[:, n, a, k * P:(k + 1) * P], identh[:, :])
                last.then_inc(s.xt_done, 1)
            mixjob(0)
            mixjob(1)
            for b in range(B):
                if b + 2 < B:
                    mixjob(b + 2)
                for t in range(TB):
                    xtjob(b * TB + t)
            pe.wait_ge(s.xt_taken, NT)
            pe.wait_ge(s.cent_split, 2)
            pe.wait_ge(s.x2_ready, NT)
            for n in range(NT):
                i = 0
                for k in range(KD):
                    for a, c in ((0, 0), (0, 1), (1, 0)):
                        last = mm(ps[:, 7, n * NE:(n + 1) * NE], xt[:, a, k, n * P:(n + 1) * P], cent[:, c, k, :],
                                  start=(i == 0), stop=(i == 5))
                        i += 1
            last.then_inc(s.raw_done, 1)
            def totals():
                pe.wait_ge(s.disp_req, 1)
                mm(ps[:, 7, P:P + 1], both.rearrange("p n e -> p (n e)"), ones[:, 0:1], start=True, stop=True).then_inc(s.disp_done, 1)

            def places():
                pe.wait_ge(s.disp_req, 2)
                mm(ps[:, 7, 2 * P:3 * P], tri[:, :], both.rearrange("p n e -> p (n e)"), start=True, stop=False)
                mm(ps[:, 7, 2 * P:3 * P], totb, trine.rearrange("p n e -> p (n e)"), start=False, stop=True)
                mm(ps[:, 7, 3 * P:3 * P + NE], totb, selE, start=True, stop=True).then_inc(s.disp_done, 1)

            def up(ph, i, n):
                pe.wait_ge(s.g_ready, CR + base[ph] + n + 1 - RH + i * KF)
                f, blk = n % KF, n // KF
                j = 0
                for k in range(KD):
                    for a, c in ((0, 0), (0, 1), (1, 0)):
                        rhs = xt[:, c, k, bass.ds(i * L + blk * L, L)]
                        last = mm(ps[:, n % RH, :], wtile(ws, a, k, f * P, P), rhs, start=(j == 0), stop=(j == 5))
                        j += 1
                last.then_inc(s.h_done, 1)

            def down(ph, i, n):
                pe.wait_ge(s.hs_ready, CR + base[ph] + n + 1 + i * KF)
                f, blk = n % KF, n // KF
                start, step = ((ACC0, STEP0), None, (ACC2, STEP2))[ph]
                for t in range(TB):
                    if f == 0 and t % 2 == 0:
                        pe.wait_ge(s.acc_done, start + step * blk - 1 + t // 2 + i * step)
                    for j, (a, c) in enumerate(((0, 0), (0, 1), (1, 0))):
                        out = ps[:, RH + t // 2, (t % 2) * D:(t % 2 + 1) * D]
                        last = mm(out, hs[:, n % RH, a, t * P:(t + 1) * P], vtile(ws, c, f),
                                  start=(f == 0 and j == 0 and t % 2 == 0), stop=(f == KF - 1 and j == 2),
                                  skip_group_check=True)
                last.then_inc(s.p_done, 1)

            xsin = [s.xs_in0, s.xs_in1]
            TBANK = 6

            def turn(i, j):
                if j < RR:
                    pe.wait_ge([s.xs_first0, s.xs_first1][j], 16)
                else:
                    pe.wait_ge(xsin[j % RR], 16 * (j // RR) + i * 16)
                pe.wait_ge(s.t_taken, i * RR + j + CR)
                tb = ps[:, TBANK, :].bitcast(F16)
                for a in range(2):
                    for k in range(KD):
                        for h in range(width(j) // P):
                            o = (a * KD + k) * RT + h * P
                            last = pe.transpose(tb[:, o:o + P], xs[:, j % RR, h, a * D + k * P:a * D + (k + 1) * P], identh[:, :])
                last.then_inc(s.t_done, 1)

            def shared_block(ph, i, blk):
                for n in range(blk * KF, (blk + 1) * KF):
                    if n + AHEAD < B * KF:
                        up(ph, i, n + AHEAD)
                    down(ph, i, n)
                    if ph == 0 and n == 2:
                        totals()
                    if ph == 0 and n == 4:
                        places()
                    if ph == 0 and n in FIRST:
                        turn(0, FIRST.index(n))

            def shared(ph):
                for n in range(AHEAD):
                    up(ph, 0, n)
                shared_block(ph, 0, 0)
                with pe.Fori(0, MORE) as i:
                    shared_block(ph, i, 1)
                shared_block(ph, 0, B - 1)

            pe.wait_ge(s.piece_low, NPIECE)
            pe.wait_ge(s.piece_high, NPIECE)
            shared(0)

            YBANK = 4
            FU = KF // RU

            def expert(i, j):
                return pe.value_load(etab[0:1, bass.ds(i * RR + j, 1)], min_val=0, max_val=NE - 1)

            def rup(i, j, g, e):
                n = RU * j + g
                if g == 0:
                    pe.wait_ge(s.t_taken, i * RR + j + 1 + CR)
                pe.wait_ge(s.g_ready, CR + base[1] + n + 1 - RH + i * (RU * RR))
                w = wr[:, bass.ds(e, 1), :, :].rearrange("p e a c -> p (e a) c")
                cols = width(j)
                for f in range(FU):
                    m = 0
                    for k in range(KD):
                        for a, c in ((0, 0), (0, 1), (1, 0)):
                            last = mm(ps[:, n % RH, f * cols:(f + 1) * cols], wtile(w, a, k, (FU * g + f) * P, P), xst[:, j % RR, c, k, 0:cols],
                                      start=(m == 0), stop=(m == 5))
                            m += 1
                last.then_inc(s.h_done, 1)

            def rdown(i, j, g, e):
                n = RU * j + g
                pe.wait_ge(s.hs_ready, CR + base[1] + n + 1 + i * (RU * RR))
                if g == 0:
                    pe.wait_ge(s.yr_taken, i * RR + j + 1 - RR + CR)
                w = wr[:, bass.ds(e, 1), :, :].rearrange("p e a c -> p (e a) c")
                cols = width(j)
                for f in range(FU):
                    for c, a in ((0, 0), (0, 1), (1, 0)):
                        for h in range(cols // P):
                            first_ = g == 0 and f == 0 and a == 0 and c == 0
                            last = mm(ps[:, YBANK + j % RR, h * D:(h + 1) * D], hs[:, n % RH, a, f * cols + h * P:f * cols + (h + 1) * P],
                                      vtile(w, c, FU * g + f), start=(first_ and h == 0),
                                      stop=(g == RU - 1 and f == FU - 1 and c == 1), skip_group_check=True)
                last.then_inc(s.p_done, 1)

            e_next = None

            def rbody(i, j, follows):
                nonlocal e_next
                e_now = e_next if follows else expert(i, j)
                if j + 1 < TILES:
                    e_next = expert(i, j + 1)
                for g in range(RU):
                    if j + 1 < TILES:
                        rup(i, j + 1, g, e_next)
                    rdown(i, j, g, e_now)
                    if g == 1 and j + 2 < TILES:
                        turn(i, j + 2)

            pe.wait_ge(s.table_ready, 1)
            e0 = expert(0, 0)
            pe.wait_ge(s.piece_low, (NE + 1) * NPIECE)
            pe.wait_ge(s.piece_high, (NE + 1) * NPIECE)
            for g in range(RU):
                rup(0, 0, g, e0)
            pe.wait_ge(s.acc_done, ACC2)
            routed_tiles(pe, rbody)

            pe.wait_ge(s.piece_low, (NE + 2) * NPIECE)
            pe.wait_ge(s.piece_high, (NE + 2) * NPIECE)
            pe.wait_ge(s.yr_taken, TILES + CR)
            shared(2)

        @block.scalar
        def _(act):
            for nm, dst in (("bk", bkT), ("bq", bqT), ("bv", bvT)):
                with nc.allow_non_contiguous_dma(reason="a bias as a column"):
                    act.dma_start(dst, A[nm].rearrange("(k p) -> p k", p=P)).then_inc(s.b_in, 16)
            act.dma_start(bob, A["bo"].rearrange("(a d) -> a d", a=1).to_broadcast([P, D])).then_inc(s.small_in, 16)
            act.dma_start(gates[:, 0:1], A["gx"].rearrange("(a d) -> a d", a=1).to_broadcast([P, 1])).then_inc(s.small_in, 16)
            act.dma_start(gates[:, 1:2], A["gf"].rearrange("(a d) -> a d", a=1).to_broadcast([P, 1])).then_inc(s.small_in, 16)
            act.dma_start(rbias[:, :], A["rb"].rearrange("(a d) -> a d", a=1).to_broadcast([P, NE])).then_inc(s.small_in, 16)
            with nc.allow_non_contiguous_dma(reason="centroids in columns"):
                act.dma_start(centf, A["centT"].rearrange("(k p) e -> p k e", p=P)).then_inc(s.small_in, 16)
            act.sem_inc(s.g_ready, CR)
            act.sem_inc(s.t_taken, CR)
            act.sem_inc(s.yr_taken, CR)
            act.sem_inc(s.ys_out0, 16)
            act.sem_inc(s.ys_out1, 16)

            def high(n):
                act.wait_ge(piece_in[n % RP], 16 * (n // RP + 1))
                p = n % NPIECE
                act.activation(ws[:, 0, p * PIECE:(p + 1) * PIECE], stage[:, n % RP, :], ACT.Copy, scale=SC).then_inc(s.piece_high, 1)

            def zhalf(q):
                b, j = q // 2, q % 2
                act.wait_ge(s.z_done, q + 1)
                if q == 0:
                    act.wait_ge(s.prod_taken, 2)
                act.activation(zt[:, j, b * L + 2 * P:(b + 1) * L], ps[:, 4 + q % 2, 2 * P:4 * P], ACT.Identity,
                               bias=zbias[:, j:j + 1]).then_inc(s.z_half, 1)

            def xnthalf(q):
                b, k = q // 2, q % 2
                act.wait_ge(s.xnt_done, q + 1)
                if b >= 2:
                    act.wait_ge(s.band_done, b - 1)
                act.copy(xnt[:, b % 2, k, 3 * P:5 * P], ps[:, q % 2, 2 * P:4 * P]).then_inc(s.xnt_half, 1)

            def bandhalf(b):
                act.wait_ge(s.band_done, b + 1)
                act.copy(gband[:, b, 2 * P:4 * P], ps[:, 2 + b % 2, 2 * P:4 * P]).then_inc(s.band_half, 1)

            def uhalf(b):
                act.wait_ge(s.u_done, 2 * (b + 1))
                act.copy(u[:, b * TB + 2:b * TB + 4, :].rearrange("p n d -> p (n d)"), ps[:, 5 + 2 * (b % 2), :]).then_inc(s.u_half, 1)

            def xntmore(q):
                b, k = q // 2, q % 2
                act.wait_ge(s.xnt_taken, 2 * (q + 1))
                x = xnt[:, b % 2, k, :]
                act.copy(x[:, 2 * P:3 * P], x[:, 0:P]).then_inc(s.xnt_more, 1)
                act.activation(x[:, 5 * P:6 * P], x[:, 3 * P:4 * P], ACT.Copy, scale=-1.0).then_inc(s.xnt_more, 1)

            def sqrt(m):
                act.wait_ge(s.sq_req, m + 1)
                b = m % B
                act.activation(rstd[:, b * TB:(b + 1) * TB, 1], rstd[:, b * TB:(b + 1) * TB, 0], ACT.Sqrt).then_inc(s.sq_done, 1)

            def contextsums(b):
                act.wait_ge(ctx_in[b], 16)
                for k in range(KD):
                    if b or k:
                        act.wait_ge(s.csum_done, b * KD + k)
                    act.activation(hf[:, 0, :], ctxt[:, k, b * L:(b + 1) * L], ACT.Copy, accum_out=csum[:, k, b:b + 1]).then_inc(s.csum_done, 1)

            sqrt(0)
            for b in range(B):
                zhalf(2 * b)
                zhalf(2 * b + 1)
                contextsums(b)
                if b + 1 < B:
                    sqrt(b + 1)
                xnthalf(2 * b)
                xnthalf(2 * b + 1)
                xntmore(2 * b)
                xntmore(2 * b + 1)
                if b:
                    bandhalf(b - 1)
            bandhalf(B - 1)
            act.wait_ge(s.small_in, 80)
            act.activation(gates[:, 2:4], gates[:, 0:2], ACT.Tanh).then_inc(s.gate_done, 1)
            uhalf(0)
            for p in range(RP):
                high(p)
            act.wait_ge(s.gsum_done, 1)
            act.copy(tot, ps[32:36, 0, :]).then_inc(s.crow_ready, 1)
            uhalf(1)
            act.wait_ge(s.exp_req, 1)
            act.activation(pen, cm, ACT.Exp, bias=sml[:, 1:2], scale=1.0 / D, accum_out=sml[:, 2:3]).then_inc(s.exp_done, 1)
            uhalf(2)
            uhalf(3)
            for p in range(RP, NPIECE):
                high(p)

            def xtevac(n):
                act.wait_ge(s.xt_done, n + 1)
                act.copy(xt[:, :, :, n * P:(n + 1) * P], ps[:, n % 4, :].bitcast(F16)[:, 0:4 * P].rearrange(
                    "p (a k t) -> p a k t", a=2, k=KD)).then_inc(s.xt_taken, 1)

            def routed_high(i, n):
                q = n % RP
                act.wait_ge(piece_in[q], 16 * (NPIECE // RP + n // RP + 1) + i * (16 * 2 * KF // RP))
                w = wr[:, bass.ds(i * (2 * KF // NPIECE) + n // NPIECE, 1), 0, (n % NPIECE) * PIECE:(n % NPIECE + 1) * PIECE]
                act.activation(w.rearrange("p a c -> p (a c)"), stage[:, q, :], ACT.Copy, scale=SC).then_inc(s.piece_high, 1)

            for b in range(B):
                sqrt(B + b)
                act.wait_ge(s.norm_req, b + 1)
                for n in range(b * TB, (b + 1) * TB if b < B - 1 else NT - 2):
                    act.activation(xn[:, n, :], xres[:, n, :], ACT.Identity, bias=rstd[:, n, 3:4], scale=rstd[:, n, 2:3]).then_inc(s.norm_ready, 1)
                for n in range(b * TB, (b + 1) * TB, 2):
                    if n < NT - 2:
                        act.wait_ge(s.norm_ready, n + 2)
                    else:
                        act.wait_ge(s.norm_last, 2)
                    act.copy(xh[:, n:n + 2, 0, :], xn[:, n:n + 2, :]).then_inc(s.high_ready, 2)
                for n in range(max(0, b - 1) * TB, b * TB):
                    xtevac(n)
                if b in (1, 2):
                    routed_high(0, 2 * b - 2)
                    routed_high(0, 2 * b - 1)
            routed_high(0, 4)
            routed_high(0, 5)
            for n in range(NT - TB, NT):
                xtevac(n)
            routed_high(0, 6)
            routed_high(0, 7)
            act.wait_ge(s.raw_done, 1)
            act.activation(sco.rearrange("p n e -> p (n e)"), ps[:, 7, 0:P], ACT.Sigmoid, scale=1.0 / (SC * SC)).then_inc(s.sig_done, 1)
            act.wait_ge(s.sig_req, 1)
            act.activation(bal, bal, ACT.Sigmoid).then_inc(s.sig_done, 1)

            def gelu(ih, n0, n, rb, cols=UNIT):
                act.wait_ge(s.h_done, n0 + n + 1 + ih)
                act.wait_ge(s.hs_ready, CR + n0 + n + 1 - RF + ih)
                act.activation(hf[:, n % RF, 0:cols], ps[:, rb, 0:cols], ACT.Gelu, scale=1.0 / (SC * SC)).then_inc(s.g_ready, 1)
                act.wait_ge(s.g_ready, CR + n0 + n + 1 + ih)
                act.wait_ge(s.p_done, CR + n0 + n + 1 - RH + ih)
                act.activation(hs[:, rb, 0, 0:cols], hf[:, n % RF, 0:cols], ACT.Copy, scale=SC).then_inc(s.hi_done, 1)

            def columns(i, j):
                act.wait_ge(s.t_done, i * RR + j + 1)
                if j >= RR:
                    act.wait_ge(s.h_done, base[1] + RU * (j - RR + 1) + i * (RU * RR))
                w = width(j)
                act.copy(xst[:, j % RR].rearrange("p a k c -> p (a k) c")[:, :, 0:w],
                         ps[:, 6, :].bitcast(F16).rearrange("p (a c) -> p a c", c=RT)[:, :, 0:w]).then_inc(s.t_taken, 1)

            def shared_block(ph, i, blk):
                for n in range(blk * KF, (blk + 1) * KF):
                    if n + AHEAD < B * KF:
                        gelu(i * KF, base[ph], n + AHEAD, (n + AHEAD) % RH)
                    if ph == 0 and n - 1 in FIRST:
                        columns(0, FIRST.index(n - 1))
                    if ph == 0:
                        for m in pieces_of(n):
                            if m == (NE - 1) * NPIECE:
                                act.wait_ge(s.scatter_out, 16 * 2 * NT)
                            routed_high(i, m)

            def shared(ph):
                for n in range(AHEAD):
                    gelu(0, base[ph], n, n % RH)
                    if ph == 0:
                        routed_high(0, PRE + n)
                shared_block(ph, 0, 0)
                if ph == 0:
                    act.wait_ge(s.base_done, B)
                with act.Fori(0, MORE) as i:
                    shared_block(ph, i, 1)
                shared_block(ph, 0, B - 1)

            shared(0)

            def routed_gelu(i, j, g):
                gelu(i * (RU * RR), base[1], RU * j + g, g % RH, cols=(KF // RU) * width(j))

            ysout = [s.ys_out0, s.ys_out1]

            def yevac(i, j):
                act.wait_ge(s.p_done, CR + base[1] + RU * (j + 1) + i * (RU * RR))
                act.wait_ge(ysout[j % RR], 16 * (j // RR + 1) + i * 16)
                w = width(j) // P * D
                act.activation(ysb[:, j % RR].rearrange("p h d -> p (h d)")[:, 0:w], ps[:, 4 + j % RR, 0:w], ACT.Copy,
                               scale=1.0 / (SC * SC)).then_inc(s.yr_taken, 1)

            def rbody(i, j, follows):
                for g in range(RU):
                    if j + 1 < TILES:
                        routed_gelu(i, j + 1, g)
                    if g == 2 and j + 2 < TILES:
                        columns(i, j + 2)
                yevac(i, j)

            act.wait_ge(s.sig_req, 2)
            act.activation(wt[:, :, 0], dv, ACT.Sigmoid).then_inc(s.sig_done, 1)
            act.activation(wt[:, :, 1], dv, ACT.Sigmoid, scale=-1.0).then_inc(s.sig_done, 1)
            for g in range(RU):
                routed_gelu(0, 0, g)
                for m in range(NPIECE // RU):
                    high((NE + 1) * NPIECE + g * (NPIECE // RU) + m)
            act.wait_ge(s.piece_low, (NE + 2) * NPIECE)
            routed_tiles(act, rbody)
            shared(2)

        @block.vector
        def _(v):
            v.sem_inc(s.hs_ready, CR)
            v.sem_inc(s.p_done, CR)
            v.sem_inc(s.acc_done, CR)
            count = [0]

            def link(ins):
                count[0] += 1
                ins.then_inc(s.chain, 1)
                v.wait_ge(s.chain, count[0])

            v.wait_ge(s.b_in, 16 * 3)
            v.tensor_copy(bvb, bvT.rearrange("p (k a) -> p k a", a=1).to_broadcast([P, KD, P])).then_inc(s.bvb_ready, 1)
            link(v.memset(bk4, float(L)))
            for bias in (bkT, bqT):
                link(v.tensor_tensor(bk4, bk4, bias.rearrange("p (k a) -> p k a", a=1).to_broadcast([P, KD, B]), ALU.mult))
            v.wait_ge(s.prod_done, 1)
            v.tensor_scalar(wkq.rearrange("p k d -> p (k d)"), ps[:, 0, :], 0.5, None, ALU.mult).then_inc(s.prod_taken, 1)
            v.wait_ge(s.vec_done, 1)
            v.tensor_copy(vecs[:, 6:10], ps[:, 2, 0:4]).then_inc(s.prod_taken, 1)

            def norm_stats(n):
                v.bn_stats(stats[:, n, :], xres[:, n, :]).then_inc(s.chain, 1)

            def rstds(b, m, scale=1.0, meanwhile=None):
                t = slice(b * TB, (b + 1) * TB)
                v.tensor_scalar(rstd[:, t, 0], mv[:, t, 1], EPS, None, ALU.add).then_inc(s.sq_req, 1)
                if meanwhile in (0, 1):
                    circulant(2 + meanwhile)
                    low(RP + 2 + meanwhile)
                elif meanwhile is not None:
                    routed_low(0, meanwhile - 2)
                v.wait_ge(s.sq_done, m + 1)
                link(v.reciprocal(rstd[:, t, 2], rstd[:, t, 1]))
                link(v.tensor_tensor(rstd[:, t, 3], rstd[:, t, 0], rstd[:, t, 2], ALU.mult))
                link(v.tensor_tensor(rstd[:, t, 3], rstd[:, t, 3], rstd[:, t, 1], ALU.add))
                link(v.tensor_scalar(rstd[:, t, 3], rstd[:, t, 3], 0.5 / scale, None, ALU.mult))
                link(v.reciprocal(rstd[:, t, 2], rstd[:, t, 3]))

            def zevac(q):
                b, j = q // 2, q % 2
                v.wait_ge(s.z_half, q + 1)
                lo, su, di = ps[:, 4 + q % 2, 0:2 * P], zt[:, j, b * L:b * L + 2 * P], zt[:, j, b * L + 2 * P:(b + 1) * L]
                v.tensor_tensor(su, lo, di, ALU.add).then_inc(s.z_taken, 1)
                v.scalar_tensor_tensor(out=di, in0=lo, scalar=zbias[:, j:j + 1], in1=di, op0=ALU.add, op1=ALU.subtract).then_inc(s.z_taken, 1)

            def xntevac(q):
                b, k = q // 2, q % 2
                v.wait_ge(s.xnt_half, q + 1)
                lo, su, di = ps[:, q % 2, 0:2 * P], xnt[:, b % 2, k, 0:2 * P], xnt[:, b % 2, k, 3 * P:5 * P]
                v.tensor_tensor(su, lo, di, ALU.add).then_inc(s.xnt_taken, 1)
                v.tensor_tensor(di, lo, di, ALU.subtract).then_inc(s.xnt_taken, 1)

            def bandevac(b):
                v.wait_ge(s.band_half, b + 1)
                su, di = ps[:, 2 + b % 2, 0:2 * P], gband[:, b, 2 * P:4 * P]
                v.tensor_tensor(gband[:, b, 0:2 * P], su, di, ALU.add).then_inc(s.band_taken, 1)
                v.tensor_tensor(gband[:, b, 4 * P:5 * P], su[:, 0:P], di[:, 0:P], ALU.add).then_inc(s.band_taken, 1)
                v.wait_ge(s.band_taken, 3 * b + 2)
                v.tensor_tensor(di, su, di, ALU.subtract).then_inc(s.band_taken, 1)

            def norm(b):
                v.wait_ge(xin[b], 16)
                for n in range(b * TB, (b + 1) * TB):
                    norm_stats(n)
                count[0] += TB
                v.wait_ge(s.chain, count[0])
                for n in range(b * TB, (b + 1) * TB):
                    v.bn_aggr(mv[:, n, :], stats[:, n, :]).then_inc(s.chain, 1)
                count[0] += TB
                v.wait_ge(s.chain, count[0])
                rstds(b, b)
                for n in range(b * TB, (b + 1) * TB):
                    v.tensor_scalar(xn[:, n, :], xres[:, n, :], mv[:, n, 0:1], rstd[:, n, 2:3], ALU.subtract, ALU.mult).then_inc(s.xn_ready, 1)

            xin = [s.x_in0, s.x_in1, s.x_in2, s.x_in3]
            norm(0)
            for b in range(B):
                zevac(2 * b)
                zevac(2 * b + 1)
                if b == 0:
                    v.wait_ge(s.prod_done, 2)
                    v.tensor_copy(wvo.rearrange("p k d -> p (k d)"), ps[:, 6, :]).then_inc(s.prod_taken, 1)
                    v.wait_ge(s.ubias_done, 1)
                    v.tensor_copy(ubias, ps[:, 7, 0:D]).then_inc(s.prod_taken, 1)
                if b + 1 < B:
                    norm(b + 1)
                xntevac(2 * b)
                xntevac(2 * b + 1)
                if b:
                    bandevac(b - 1)
            v.wait_ge(s.csum_done, KD * B)
            link(v.tensor_tensor(sbp, csum, v1.rearrange("p (k a) -> p k a", a=1).to_broadcast([P, KD, B]), ALU.mult))
            link(v.tensor_tensor(sbp, sbp, bk4, ALU.add))
            v.tensor_tensor(sbp[:, 0, :], sbp[:, 0, :], sbp[:, 1, :], ALU.add).then_inc(s.sb_ready, 1)
            v.wait_ge(s.small_in, 80)
            v.tensor_scalar(cent[:, 0], centf, SC, None, ALU.mult).then_inc(s.cent_split, 1)
            v.wait_ge(s.cent_split, 1)
            v.scalar_tensor_tensor(out=cent[:, 1], in0=centf, scalar=SC, in1=cent[:, 0], op0=ALU.mult, op1=ALU.subtract).then_inc(s.cent_split, 1)

            def uevac(b):
                v.wait_ge(s.u_half, b + 1)
                su, di = (u[:, b * TB + 2 * h:b * TB + 2 * h + 2, :].rearrange("p n d -> p (n d)") for h in range(2))
                v.tensor_tensor(su, ps[:, 4 + 2 * (b % 2), :], di, ALU.add).then_inc(s.u_taken, 1)
                v.tensor_tensor(di, ps[:, 4 + 2 * (b % 2), :], di, ALU.subtract).then_inc(s.u_taken, 1)

            bandevac(B - 1)
            v.wait_ge(s.gate_done, 1)
            link(v.tensor_tensor(bob, bob, ubias, ALU.add))
            v.tensor_scalar(gates[:, 8:9], gates[:, 2:3], 0.5, None, ALU.mult)
            v.tensor_scalar(gates[:, 9:10], gates[:, 2:3], -0.5, None, ALU.mult)
            v.tensor_scalar(bob, bob, gates[:, 2:3], None, ALU.mult).then_inc(s.gb_ready, 1)
            uevac(0)

            def low(n):
                v.wait_ge(s.piece_high, n + 1)
                p = n % NPIECE
                v.scalar_tensor_tensor(out=ws[:, 1, p * PIECE:(p + 1) * PIECE], in0=stage[:, n % RP, :], scalar=SC,
                                       in1=ws[:, 0, p * PIECE:(p + 1) * PIECE], op0=ALU.mult, op1=ALU.subtract).then_inc(s.piece_low, 1)

            for p in range(RP):
                low(p)

            v.wait_ge(s.const_ready, 5)
            link(v.tensor_reduce(selE, identf.rearrange("p (n e) -> p e n", e=NE), AX, ALU.add))
            link(v.tensor_tensor(trine, tri[:, :].rearrange("p (n e) -> p n e", e=NE),
                                 selE.rearrange("p (a e) -> p a e", a=1).to_broadcast([P, NT, NE]), ALU.mult))
            link(v.tensor_scalar(upper, upper, 0.0, None, ALU.is_gt))
            link(v.tensor_scalar(gates[:, 0:1], gates[:, 3:4], 1.0 / (SC * SC), None, ALU.mult))

            v.wait_ge(s.crow_ready, 1)
            link(v.max(top8, tot))
            link(v.memset(top8[:, LAGS:8], -BIG))
            link(v.match_replace(rep, top8, tot, -BIG))
            link(v.tensor_tensor(pen, tot, rep, ALU.is_equal))
            link(v.scalar_tensor_tensor(out=cm, in0=pen, scalar=-1e30, in1=ps[0:B, 0, :], op0=ALU.mult, op1=ALU.add))
            link(v.reduce_max(sml[:, 3:4], cm, AX))
            v.tensor_scalar(sml[:, 1:2], sml[:, 3:4], -1.0 / D, None, ALU.mult).then_inc(s.exp_req, 1)
            uevac(1)
            v.wait_ge(s.exp_done, 1)
            link(v.reciprocal(sml[:, 3:4], sml[:, 2:3]))
            link(v.tensor_scalar(crow[:, P - 1:SKEW - 1], pen, sml[:, 3:4], None, ALU.mult))
            v.tensor_copy(crow[:, 0:P - 1], crow[:, L:SKEW - 1]).then_inc(s.crow_ready, 1)
            uevac(2)
            uevac(3)
            def circulant(b):
                v.wait_ge(circ_in[b], 16)
                def reversed_(j, w):
                    a = craw[:, b, :]
                    return bass.AP(a.tensor, a.offset + L - 1 - j, [a.ap[0], [-1, w]])
                v.tensor_tensor(circ[:, b, 0:2 * P], reversed_(0, 2 * P), reversed_(2 * P, 2 * P), ALU.add).then_inc(s.circ_ready, 1)
                v.tensor_tensor(circ[:, b, 2 * P:4 * P], reversed_(2 * P, 2 * P), reversed_(0, 2 * P), ALU.subtract).then_inc(s.circ_ready, 1)
                v.tensor_tensor(circ[:, b, 4 * P:5 * P], reversed_(0, P), reversed_(2 * P, P), ALU.subtract).then_inc(s.circ_ready, 1)

            circulant(0)
            circulant(1)
            low(RP)
            low(RP + 1)

            def routed_low(i, n):
                q = n % RP
                v.wait_ge(s.piece_high, NPIECE + n + 1 + i * (2 * KF))
                w = wr[:, bass.ds(i * (2 * KF // NPIECE) + n // NPIECE, 1), :, (n % NPIECE) * PIECE:(n % NPIECE + 1) * PIECE]
                w = w.rearrange("p e a c -> p (e a) c")
                v.scalar_tensor_tensor(out=w[:, 1, :], in0=stage[:, q, :], scalar=SC, in1=w[:, 0, :],
                                       op0=ALU.mult, op1=ALU.subtract).then_inc(s.piece_low, 1)

            for b in range(B):
                v.wait_ge(s.xb_ready, b + 1)
                tiles = range(b * TB, (b + 1) * TB)
                halves = [xres[:, b * TB + 2 * t:b * TB + 2 * t + 2, :].rearrange("p n d -> p (n d)") for t in range(2)]
                for h in range(2):
                    v.wait_ge(s.mix_done, 2 * b + h + 1)
                    if h:
                        v.wait_ge(s.x2_ready, b * TB + 2)
                    for t, x2 in enumerate(halves):
                        g = gates[:, 9:10] if h and t else gates[:, 8:9]
                        v.scalar_tensor_tensor(out=x2, in0=ps[:, 4 + 2 * (b % 2) + h, :], scalar=g, in1=x2,
                                               op0=ALU.mult, op1=ALU.add).then_inc(s.x2_ready, 1)
                v.wait_ge(s.x2_ready, (b + 1) * TB)
                for n in tiles:
                    norm_stats(n)
                count[0] += TB
                v.wait_ge(s.chain, count[0])
                for n in tiles:
                    v.bn_aggr(mv[:, n, :], stats[:, n, :]).then_inc(s.chain, 1)
                count[0] += TB
                v.wait_ge(s.chain, count[0])
                rstds(b, B + b, SC, meanwhile=b)
                t = slice(b * TB, (b + 1) * TB)
                v.scalar_tensor_tensor(out=rstd[:, t, 3], in0=mv[:, t, 0], scalar=-1.0, in1=rstd[:, t, 2],
                                       op0=ALU.mult, op1=ALU.mult).then_inc(s.norm_req, 1)
            for n in (NT - 2, NT - 1):
                v.tensor_scalar(xn[:, n, :], xres[:, n, :], mv[:, n, 0:1], rstd[:, n, 2:3], ALU.subtract, ALU.mult).then_inc(s.norm_last, 1)
            routed_low(0, 2)
            routed_low(0, 3)
            for n in range(NT - TB, NT, 2):
                v.wait_ge(s.high_ready, n + 2)
                v.tensor_tensor(xh[:, n:n + 2, 1, :], xn[:, n:n + 2, :], xh[:, n:n + 2, 0, :], ALU.subtract).then_inc(s.split_last, 2)
            for m in range(4, PRE):
                routed_low(0, m)
            e16 = lambda a: a.rearrange("p (n e) -> p n e", e=1).to_broadcast([P, NT, NE])
            nefirst = lambda a: a.rearrange("p n e -> p (n e)").rearrange("p (e t) -> p e t", e=NE)
            v.wait_ge(s.raw_done, 1)
            v.wait_ge(s.sig_done, 1)
            v.scalar_tensor_tensor(out=bal, in0=ps[:, 7, 0:P].rearrange("p (n e) -> p n e", e=NE), scalar=1.0 / (SC * SC), in1=rbias[:, :].rearrange("p (a e) -> p a e", a=1).to_broadcast([P, NT, NE]),
                                   op0=ALU.mult, op1=ALU.add).then_inc(s.sig_req, 1)

            def choose(oh, sc):
                link(v.tensor_reduce(m1, bal, AX, ALU.max))
                link(v.tensor_tensor(key, bal, e16(m1), ALU.is_ge))
                link(v.tensor_tensor(key, key, ramp, ALU.mult))
                link(v.tensor_reduce(k1, key, AX, ALU.max))
                link(v.tensor_tensor(oh, key, e16(k1), ALU.is_equal))
                link(v.tensor_tensor(tmp, oh, sco, ALU.mult))
                link(v.tensor_reduce(sc, tmp, AX, ALU.add))
                link(v.scalar_tensor_tensor(out=bal, in0=oh, scalar=-4.0, in1=bal, op0=ALU.mult, op1=ALU.add))

            def both_choices():
                v.tensor_tensor(dv, s1v, s2v, ALU.subtract).then_inc(s.sig_req, 1)
                v.tensor_tensor(both, oh1, oh2, ALU.add).then_inc(s.disp_req, 1)

            def spread_totals():
                v.wait_ge(s.disp_done, 1)
                link(v.tensor_copy(totc, ps[:, 7, P:P + 1]))
                v.tensor_scalar(totb, ones, totc, None, ALU.mult).then_inc(s.disp_req, 1)

            def place_tokens():
                v.wait_ge(s.disp_done, 2)
                link(v.tensor_copy(cnt, ps[:, 7, 3 * P:3 * P + NE]))
                link(v.tensor_tensor(nefirst(tmp), cnt.rearrange("p (e a) -> p e a", a=1).to_broadcast([P, NE, NT]), lag_ramp, ALU.is_gt))
                v.tensor_reduce(chunks, nefirst(tmp), AX, ALU.add)
                link(v.tensor_reduce(ntile, nefirst(tmp)[:, :, 1:NT:2], AX, ALU.add))
                link(v.scalar_tensor_tensor(out=odd, in0=ntile, scalar=-2.0, in1=chunks, op0=ALU.mult, op1=ALU.add))
                link(v.tensor_tensor(up2, upper, ntile.rearrange("p (a e) -> p a e", a=1).to_broadcast([P, NE, NE]), ALU.mult))
                link(v.tensor_reduce(first, up2, AX, ALU.add))
                link(v.tensor_tensor(up2, upper, odd.rearrange("p (a e) -> p a e", a=1).to_broadcast([P, NE, NE]), ALU.mult))
                link(v.tensor_reduce(nfirst, up2, AX, ALU.add))
                link(v.tensor_reduce(schunks, odd, AX, ALU.add))
                v.tensor_scalar(sslots, schunks, float(P), None, ALU.mult)
                link(v.tensor_tensor(wend, first, ntile, ALU.add))
                link(v.tensor_scalar(wend, wend, float(RT), None, ALU.mult))
                link(v.scalar_tensor_tensor(out=narrow_shift, in0=nfirst, scalar=float(P), in1=wend, op0=ALU.mult, op1=ALU.subtract))

            def choose_slots():
                per_expert = lambda a: a.rearrange("p (a e) -> p a e", a=1).to_broadcast([P, NT, NE])
                link(v.scalar_tensor_tensor(out=pos, in0=per_expert(first), scalar=float(RT),
                                            in1=ps[:, 7, 2 * P:3 * P].rearrange("p (n e) -> p n e", e=NE), op0=ALU.mult, op1=ALU.add))
                link(v.scalar_tensor_tensor(out=npos, in0=pos, scalar=float(WIDE * RT), in1=per_expert(narrow_shift), op0=ALU.add, op1=ALU.add))
                link(v.tensor_scalar(tmp, npos, float(SLOTS), float((WIDE - 1) * RT - SLOTS), ALU.is_ge, ALU.mult))
                link(v.tensor_tensor(npos, npos, tmp, ALU.add))
                link(v.tensor_tensor(key, pos, per_expert(wend), ALU.is_ge))
                link(v.tensor_scalar(tmp, pos, float(WIDE * RT), sslots, ALU.is_ge, ALU.mult))
                link(v.tensor_tensor(pos, pos, tmp, ALU.add))
                link(v.tensor_tensor(npos, npos, pos, ALU.subtract))
                link(v.tensor_tensor(npos, npos, key, ALU.mult))
                link(v.tensor_tensor(pos, pos, npos, ALU.add))
                for k, oh in enumerate((oh1, oh2)):
                    link(v.tensor_tensor(tmp, oh, pos, ALU.mult))
                    link(v.tensor_reduce(k1, tmp, AX, ALU.add))
                    v.tensor_copy(slots[:, :, k], k1).then_inc(s.slots_ready, 1)
                    v.wait_ge(s.slots_ready, k + 1)

            def expert_table():
                row = lambda a, c: a[0:1].rearrange("p (a e) -> p a e", a=1).to_broadcast([1, c, NE])
                col = lambda c: jramp[:, 0:c].rearrange("p (j a) -> p j a", a=1).to_broadcast([1, c, NE])
                link(v.tensor_tensor(jcmp[:, 0:WIDE], col(WIDE), row(first, WIDE), ALU.is_ge))
                link(v.tensor_reduce(ej[:, 0:WIDE], jcmp[:, 0:WIDE], AX, ALU.add))
                link(v.tensor_tensor(jcmp[:, 0:NARROW], col(NARROW), row(nfirst, NARROW), ALU.is_ge))
                link(v.tensor_reduce(ej[:, WIDE:TILES], jcmp[:, 0:NARROW], AX, ALU.add))
                half = wend[0:1]
                link(v.tensor_scalar(half, first[0:1], 2.0, float(-2 * WIDE), ALU.mult, ALU.add))
                link(v.tensor_scalar(half, half, schunks[0:1], None, ALU.add))
                link(v.tensor_tensor(jcmp[:, 0:NARROW], col(NARROW), row(half, NARROW), ALU.is_ge))
                over = jcmp[:, 8:9].rearrange("p a e -> p (a e)")[:, 0:NARROW]
                behind = jcmp[:, 9:10].rearrange("p a e -> p (a e)")[:, 0:NARROW]
                link(v.tensor_reduce(over, jcmp[:, 0:NARROW], AX, ALU.add))
                link(v.tensor_tensor(over, over, ej[:, WIDE:TILES], ALU.subtract))
                link(v.tensor_scalar(behind, jramp[:, 0:NARROW], schunks[0:1], None, ALU.is_ge))
                link(v.tensor_tensor(over, over, behind, ALU.mult))
                link(v.tensor_tensor(ej[:, WIDE:TILES], ej[:, WIDE:TILES], over, ALU.add))
                v.tensor_scalar(etab[:, :], ej, -1.0, None, ALU.add).then_inc(s.table_ready, 1)

            def split(ih, n0, n, cols=UNIT):
                v.wait_ge(s.hi_done, n0 + n + 1 + ih)
                v.scalar_tensor_tensor(out=hs[:, n % RH, 1, 0:cols], in0=hf[:, n % RF, 0:cols], scalar=SC, in1=hs[:, n % RH, 0, 0:cols],
                                       op0=ALU.mult, op1=ALU.subtract).then_inc(s.hs_ready, 1)

            def accumulate(ph, i, at, **k):
                start, step = ((ACC0, STEP0), None, (ACC2, STEP2))[ph]
                v.wait_ge(s.acc_done, start + at + i * step)
                v.scalar_tensor_tensor(**k, op0=ALU.mult, op1=ALU.add).then_inc(s.acc_done, 1)

            def add_block(ph, i, blk):
                v.wait_ge(s.p_done, CR + base[ph] + KF * (blk + 1) + i * KF)
                step = (STEP0, None, STEP2)[ph]
                for h in range(2):
                    o = xres[:, bass.ds(i * TB + blk * TB + 2 * h, 2), :].rearrange("p n d -> p (n d)")
                    accumulate(ph, i, blk * step + step - 2 + h, out=o, in0=ps[:, RH + h, :], scalar=gates[:, 0:1], in1=o)

            gin = [s.gather_in0, s.gather_in1, s.gather_in2, s.gather_in3,
                   s.gather_in4, s.gather_in5, s.gather_in6, s.gather_in7]

            def combine(i, n):
                m = n % 8
                v.wait_ge(gin[m], 16 * (n // 8 + 1) + i * 16)
                o = xres[:, bass.ds(i * TB + n // 2, 1), :].rearrange("p n d -> p (n d)")
                w = wt[:, bass.ds(i * TB + n // 2, 1), 2 + n % 2]
                accumulate(2, i, n // KF * STEP2 + n % KF, out=o, in0=gat[:, m, :], scalar=w, in1=o)

            def shared_block(ph, i, blk):
                for n in range(blk * KF, (blk + 1) * KF):
                    last = n == (blk + 1) * KF - 1
                    if ph == 2 and last:
                        combine(i, n)
                    if n + AHEAD < B * KF:
                        split(i * KF, base[ph], n + AHEAD)
                    if ph == 2 and not last:
                        combine(i, n)
                    if last:
                        if ph == 0:
                            v.wait_ge(s.base_done, blk + 1 + i)
                        add_block(ph, i, blk)
                    if ph == 0:
                        if n == 0:
                            choose(oh2, s2v)
                            both_choices()
                        if n == 2:
                            spread_totals()
                        if n == 4:
                            place_tokens()
                        if n == 5:
                            choose_slots()
                        for m in pieces_of(n):
                            routed_low(i, m)
                        if n == (B - 1) * KF:
                            expert_table()

            def shared(ph):
                for n in range(AHEAD):
                    split(0, base[ph], n)
                    if ph == 0:
                        routed_low(0, PRE + n)
                if ph == 0:
                    v.wait_ge(s.sig_done, 2)
                    choose(oh1, s1v)
                shared_block(ph, 0, 0)
                with v.Fori(0, MORE) as i:
                    shared_block(ph, i, 1)
                shared_block(ph, 0, B - 1)

            shared(0)

            for g in range(RU):
                split(0, base[1], g)
                for m in range(NPIECE // RU):
                    low((NE + 1) * NPIECE + g * (NPIECE // RU) + m)
            v.wait_ge(s.sig_done, 4)
            v.tensor_scalar(wt[:, :, 2:4], wt[:, :, 0:2], gates[:, 3:4], None, ALU.mult).then_inc(s.wt_ready, 1)
            v.wait_ge(s.wt_ready, 1)

            def rbody(i, j, follows):
                if j + 1 < TILES:
                    for g in range(RU):
                        split(i * (RU * RR), base[1], RU * (j + 1) + g, cols=(KF // RU) * width(j + 1))
            routed_tiles(v, rbody)
            shared(2)


def kernel(x, ctx_1024, g_xattn, g_ffn, L0_xattn_Wq, L0_xattn_bq, L0_xattn_Wk, L0_xattn_bk, L0_xattn_Wv, L0_xattn_bv,
           L0_xattn_Wo, L0_xattn_bo, L0_ffn_centroids, L0_ffn_routing_bias, L0_ffn_Wfc_r, L0_ffn_Wproj_r,
           L0_ffn_Wfc_sh, L0_ffn_Wproj_sh):
    import numpy as np
    import concourse.bacc as bacc
    from concourse.bass_utils import run_bass_kernel_spmd

    c = np.ascontiguousarray
    wfc = np.concatenate([np.asarray(L0_ffn_Wfc_sh)[:1], np.asarray(L0_ffn_Wfc_r), np.asarray(L0_ffn_Wfc_sh)[1:]])
    wpr = np.concatenate([np.asarray(L0_ffn_Wproj_sh)[:1], np.asarray(L0_ffn_Wproj_r), np.asarray(L0_ffn_Wproj_sh)[1:]])
    n = NE + NS
    wfc = wfc.transpose(0, 2, 1).reshape(n, KD, P, F)
    wpr = wpr.transpose(0, 2, 1).reshape(n, 2, KF // 2, P, D).transpose(0, 1, 3, 2, 4).reshape(n, 2, P, KF // 2 * D)
    arrays = {
        "x": c(np.asarray(x).reshape(T, D)), "ctxT": c(np.asarray(ctx_1024).reshape(T, D).T),
        "Wq": c(L0_xattn_Wq), "Wk": c(L0_xattn_Wk), "Wv": c(L0_xattn_Wv), "WoT": c(np.asarray(L0_xattn_Wo).T),
        "bq": c(L0_xattn_bq), "bk": c(L0_xattn_bk), "bv": c(L0_xattn_bv), "bo": c(L0_xattn_bo),
        "gx": c(g_xattn), "gf": c(g_ffn), "centT": c(np.asarray(L0_ffn_centroids).T), "rb": c(L0_ffn_routing_bias),
        "W": c(np.concatenate([wfc, wpr], axis=1).reshape(n, -1, P, F // PIECE, PIECE).transpose(0, 1, 3, 2, 4).reshape(n * NPIECE, P, PIECE)),
    }
    nc = bacc.Bacc("TRN2", target_bir_lowering=False, num_devices=1)
    A = {k: nc.dram_tensor("in_" + k, a.shape, mybir.dt.from_np(a.dtype), kind="ExternalInput").ap() for k, a in arrays.items()}
    A["out"] = nc.dram_tensor("out_y", (T, D), F32, kind="ExternalOutput").ap()
    build_kernel(nc, A)
    r = run_bass_kernel_spmd(nc, [{"in_" + k: a for k, a in arrays.items()}], core_ids=[0])
    return np.asarray(r.results[0]["out_y"]).reshape(B, L, D)
```
